# Optimizing a Trainium2 kernel written in Bass

```python
import numpy as np
import jax
import jax.numpy as jnp

def _softmax(x, axis=-1):
    return jax.nn.softmax(x, axis=axis)

def _gelu(x):
    return jax.nn.gelu(x, approximate=True)

def _silu(x):
    return jax.nn.silu(x)

def _sigmoid(x):
    return jax.nn.sigmoid(x)

def _layernorm(x, axis=-1, eps=1e-05):
    m = jnp.mean(x, axis=axis, keepdims=True)
    v = jnp.var(x, axis=axis, keepdims=True)
    return (x - m) / jnp.sqrt(v + eps)

def _scatter_add(tgt, idx, src, axis=0):
    return tgt.at[idx].add(src)

def _segment_sum(src, seg, n):
    return jax.ops.segment_sum(src, seg, n)
kernel_name = 'mk_adaln_ffn_d2_seqx_r4_e2e80c'

def setup_inputs(seed: int=0):
    np.random.seed(seed)
    _w = jnp.asarray

    def _rec_inputs():
        import jax
        import jax.numpy as jnp
        _rk = jax.random.key(seed)
        x = -0.0003929 + 0.9999 * jax.random.normal(jax.random.fold_in(_rk, 1), (32, 64, 1024), jnp.float32)
        _lenS = 64 - jax.random.randint(jax.random.fold_in(_rk, 7), (32,), 0, max(1, 64 // 4) + 1, jnp.int32)
        _lenS2 = 64 - jax.random.randint(jax.random.fold_in(_rk, 8), (32,), 0, max(1, 64 // 4) + 1, jnp.int32)
        cond_512 = 0.00782532 + 1.00527 * jax.random.normal(jax.random.fold_in(_rk, 11), (32, 128), jnp.float32)
        return (x, cond_512)
    x, cond_512 = _rec_inputs()

    def _L0_cond_setup():
        import jax, jax.numpy as jnp
        from jax import lax
        import numpy as np
        CIN, COUT, K, STYLE_DIM = (64, 64, 3, 128)
        N_LAYERS = 4
        TYPES = ('same', 'upsample', 'same', 'downsample')
        SCALE = 1.0 / float(np.sqrt(CIN * K ** 2))
        EPS = 1e-08
        _BK = np.array([1.0, 3.0, 3.0, 1.0], dtype=np.float32)
        BLUR_K = _BK / _BK.sum()

        def _blur(x, kern, pad):
            B, C, _ = x.shape
            xp = jnp.pad(x, ((0, 0), (0, 0), (pad[0], pad[1])))
            w = jnp.broadcast_to(kern.astype(x.dtype)[None, None, :], (C, 1, kern.shape[0]))
            return lax.conv_general_dilated(xp, w, (1,), 'VALID', feature_group_count=C, dimension_numbers=('NCH', 'OIH', 'NCH'))

        def _conv_same(x, w):
            p = (K - 1) // 2
            return lax.conv_general_dilated(x[None], w, (1,), [(p, p)], dimension_numbers=('NCH', 'OIH', 'NCH'))[0]

        def _conv_down(x, w):
            return lax.conv_general_dilated(x[None], w, (2,), 'VALID', dimension_numbers=('NCH', 'OIH', 'NCH'))[0]

        def _conv_up(x, w_t):
            return lax.conv_transpose(x[None], w_t, (2,), 'VALID', dimension_numbers=('NCH', 'IOH', 'NCH'), transpose_kernel=True)[0]

        def _layer(x, style, w, b, mw, mb, typ):
            s = style @ mw.T + mb
            weight = SCALE * w * s[:, None, :, None]
            demod = lax.rsqrt(jnp.sum(weight * weight, axis=(2, 3)) + EPS)
            weight = weight * demod[:, :, None, None]
            blur_k = jnp.asarray(BLUR_K)
            if typ == 'same':
                out = jax.vmap(_conv_same)(x, weight) + b[None, :, None]
            elif typ == 'upsample':
                out = jax.vmap(_conv_up)(x, weight.transpose(0, 2, 1, 3)) + b[None, :, None]
                out = _blur(out, 2.0 * blur_k, (1, 1))
            elif typ == 'downsample':
                xb = _blur(x, blur_k, (2, 2))
                out = jax.vmap(_conv_down)(xb, weight) + b[None, :, None]
            else:
                raise NotImplementedError(typ)
            return out
        key = jax.random.key(seed)
        ks = jax.random.split(key, 6)
        B, L = (16, 1024)
        return {'x': jax.random.normal(ks[0], (B, CIN, L), dtype=jnp.float32), 'style': jax.random.normal(ks[1], (B, STYLE_DIM), dtype=jnp.float32), 'weights': jax.random.normal(ks[2], (N_LAYERS, COUT, CIN, K), dtype=jnp.float32), 'biases': jax.random.normal(ks[3], (N_LAYERS, COUT), dtype=jnp.float32) * 0.1, 'mod_w': jax.random.normal(ks[4], (N_LAYERS, CIN, STYLE_DIM), dtype=jnp.float32) / np.sqrt(STYLE_DIM), 'mod_b': 1.0 + 0.1 * jax.random.normal(ks[5], (N_LAYERS, CIN), dtype=jnp.float32)}
    _L0_cond_all = _L0_cond_setup()
    _L0_cond_in = {k: v for k, v in _L0_cond_all.items() if k in ('weights', 'biases', 'mod_w', 'mod_b')}
    del _L0_cond_all

    def _L0_ffn_setup():
        import jax, jax.numpy as jnp
        import numpy as np
        BATCH, SEQ, D = (2, 512, 1024)
        K, TOPK, RANK = (64, 16, 16)
        ALPHA = 32.0
        SCALING = ALPHA / RANK
        key = jax.random.key(seed)
        k1, k2, k3, k4 = jax.random.split(key, 4)
        x = jax.random.normal(k1, (BATCH, SEQ, D), dtype=jnp.float32)
        A = jax.random.normal(k2, (K, RANK, D), dtype=jnp.float32) * 0.02
        B = jax.random.normal(k3, (K, D, RANK), dtype=jnp.float32) * 0.02
        Wr = jax.random.normal(k4, (K, D), dtype=jnp.float32) * 0.02
        return {'x': x, 'A': A, 'B': B, 'Wr': Wr}
    _L0_ffn_all = _L0_ffn_setup()
    _L0_ffn_in = {k: v for k, v in _L0_ffn_all.items() if k in ('A', 'B', 'Wr')}
    del _L0_ffn_all

    def _L1_cond_setup():
        import jax, jax.numpy as jnp
        from jax import lax
        import numpy as np
        CIN, COUT, K, STYLE_DIM = (64, 64, 3, 128)
        N_LAYERS = 4
        TYPES = ('same', 'upsample', 'same', 'downsample')
        SCALE = 1.0 / float(np.sqrt(CIN * K ** 2))
        EPS = 1e-08
        _BK = np.array([1.0, 3.0, 3.0, 1.0], dtype=np.float32)
        BLUR_K = _BK / _BK.sum()

        def _blur(x, kern, pad):
            B, C, _ = x.shape
            xp = jnp.pad(x, ((0, 0), (0, 0), (pad[0], pad[1])))
            w = jnp.broadcast_to(kern.astype(x.dtype)[None, None, :], (C, 1, kern.shape[0]))
            return lax.conv_general_dilated(xp, w, (1,), 'VALID', feature_group_count=C, dimension_numbers=('NCH', 'OIH', 'NCH'))

        def _conv_same(x, w):
            p = (K - 1) // 2
            return lax.conv_general_dilated(x[None], w, (1,), [(p, p)], dimension_numbers=('NCH', 'OIH', 'NCH'))[0]

        def _conv_down(x, w):
            return lax.conv_general_dilated(x[None], w, (2,), 'VALID', dimension_numbers=('NCH', 'OIH', 'NCH'))[0]

        def _conv_up(x, w_t):
            return lax.conv_transpose(x[None], w_t, (2,), 'VALID', dimension_numbers=('NCH', 'IOH', 'NCH'), transpose_kernel=True)[0]

        def _layer(x, style, w, b, mw, mb, typ):
            s = style @ mw.T + mb
            weight = SCALE * w * s[:, None, :, None]
            demod = lax.rsqrt(jnp.sum(weight * weight, axis=(2, 3)) + EPS)
            weight = weight * demod[:, :, None, None]
            blur_k = jnp.asarray(BLUR_K)
            if typ == 'same':
                out = jax.vmap(_conv_same)(x, weight) + b[None, :, None]
            elif typ == 'upsample':
                out = jax.vmap(_conv_up)(x, weight.transpose(0, 2, 1, 3)) + b[None, :, None]
                out = _blur(out, 2.0 * blur_k, (1, 1))
            elif typ == 'downsample':
                xb = _blur(x, blur_k, (2, 2))
                out = jax.vmap(_conv_down)(xb, weight) + b[None, :, None]
            else:
                raise NotImplementedError(typ)
            return out
        key = jax.random.key(seed)
        ks = jax.random.split(key, 6)
        B, L = (16, 1024)
        return {'x': jax.random.normal(ks[0], (B, CIN, L), dtype=jnp.float32), 'style': jax.random.normal(ks[1], (B, STYLE_DIM), dtype=jnp.float32), 'weights': jax.random.normal(ks[2], (N_LAYERS, COUT, CIN, K), dtype=jnp.float32), 'biases': jax.random.normal(ks[3], (N_LAYERS, COUT), dtype=jnp.float32) * 0.1, 'mod_w': jax.random.normal(ks[4], (N_LAYERS, CIN, STYLE_DIM), dtype=jnp.float32) / np.sqrt(STYLE_DIM), 'mod_b': 1.0 + 0.1 * jax.random.normal(ks[5], (N_LAYERS, CIN), dtype=jnp.float32)}
    _L1_cond_all = _L1_cond_setup()
    _L1_cond_in = {k: v for k, v in _L1_cond_all.items() if k in ('weights', 'biases', 'mod_w', 'mod_b')}
    del _L1_cond_all

    def _L1_ffn_setup():
        import jax, jax.numpy as jnp
        import numpy as np
        B, S, IN, OUT = (4, 512, 1024, 1024)
        PACK = 8

        def _dequant(qweight, scales, zeros):
            qw = jax.lax.bitcast_convert_type(qweight, jnp.uint32)
            shifts = jnp.arange(PACK, dtype=jnp.uint32) * jnp.uint32(4)
            nib = qw[:, None, :] >> shifts[None, :, None] & jnp.uint32(15)
            q = nib.reshape(-1, qw.shape[1]).astype(jnp.float32)
            return scales[:, 0][None, :] * q - zeros[:, 0][None, :]
        key = jax.random.key(seed)
        k1, k2, k3, k4, k5 = jax.random.split(key, 5)
        x = jax.random.normal(k1, (B, S, IN), dtype=jnp.float32)
        qweight = jax.random.randint(k2, (IN // PACK, OUT), 0, 2147483647, dtype=jnp.int32)
        scales = jax.random.uniform(k3, (OUT, 1), dtype=jnp.float32, minval=0.005, maxval=0.02)
        zeros = jax.random.uniform(k4, (OUT, 1), dtype=jnp.float32, minval=0.0, maxval=0.15)
        bias = jax.random.normal(k5, (OUT,), dtype=jnp.float32) * 0.02
        return {'x': x, 'qweight': qweight, 'scales': scales, 'zeros': zeros, 'bias': bias}
    _L1_ffn_all = _L1_ffn_setup()
    _L1_ffn_in = {k: v for k, v in _L1_ffn_all.items() if k in ('qweight', 'scales', 'zeros', 'bias')}
    del _L1_ffn_all
    return {'x': x, 'cond_512': cond_512, 'L0_cond_weights': _L0_cond_in['weights'], 'L0_cond_biases': _L0_cond_in['biases'], 'L0_cond_mod_w': _L0_cond_in['mod_w'], 'L0_cond_mod_b': _L0_cond_in['mod_b'], 'L0_ffn_A': _L0_ffn_in['A'], 'L0_ffn_B': _L0_ffn_in['B'], 'L0_ffn_Wr': _L0_ffn_in['Wr'], 'L1_cond_weights': _L1_cond_in['weights'], 'L1_cond_biases': _L1_cond_in['biases'], 'L1_cond_mod_w': _L1_cond_in['mod_w'], 'L1_cond_mod_b': _L1_cond_in['mod_b'], 'L1_ffn_qweight': _L1_ffn_in['qweight'], 'L1_ffn_scales': _L1_ffn_in['scales'], 'L1_ffn_zeros': _L1_ffn_in['zeros'], 'L1_ffn_bias': _L1_ffn_in['bias']}

def reference(x, cond_512, L0_cond_weights, L0_cond_biases, L0_cond_mod_w, L0_cond_mod_b, L0_ffn_A, L0_ffn_B, L0_ffn_Wr, L1_cond_weights, L1_cond_biases, L1_cond_mod_w, L1_cond_mod_b, L1_ffn_qweight, L1_ffn_scales, L1_ffn_zeros, L1_ffn_bias):
    import jax
    import jax.numpy as jnp

    def _L0_cond_ref(x, style, weights, biases, mod_w, mod_b):
        import jax, jax.numpy as jnp
        from jax import lax
        import numpy as np
        CIN, COUT, K, STYLE_DIM = (64, 64, 3, 128)
        N_LAYERS = 4
        TYPES = ('same', 'upsample', 'same', 'downsample')
        SCALE = 1.0 / float(np.sqrt(CIN * K ** 2))
        EPS = 1e-08
        _BK = np.array([1.0, 3.0, 3.0, 1.0], dtype=np.float32)
        BLUR_K = _BK / _BK.sum()

        def _blur(x, kern, pad):
            B, C, _ = x.shape
            xp = jnp.pad(x, ((0, 0), (0, 0), (pad[0], pad[1])))
            w = jnp.broadcast_to(kern.astype(x.dtype)[None, None, :], (C, 1, kern.shape[0]))
            return lax.conv_general_dilated(xp, w, (1,), 'VALID', feature_group_count=C, dimension_numbers=('NCH', 'OIH', 'NCH'))

        def _conv_same(x, w):
            p = (K - 1) // 2
            return lax.conv_general_dilated(x[None], w, (1,), [(p, p)], dimension_numbers=('NCH', 'OIH', 'NCH'))[0]

        def _conv_down(x, w):
            return lax.conv_general_dilated(x[None], w, (2,), 'VALID', dimension_numbers=('NCH', 'OIH', 'NCH'))[0]

        def _conv_up(x, w_t):
            return lax.conv_transpose(x[None], w_t, (2,), 'VALID', dimension_numbers=('NCH', 'IOH', 'NCH'), transpose_kernel=True)[0]

        def _layer(x, style, w, b, mw, mb, typ):
            s = style @ mw.T + mb
            weight = SCALE * w * s[:, None, :, None]
            demod = lax.rsqrt(jnp.sum(weight * weight, axis=(2, 3)) + EPS)
            weight = weight * demod[:, :, None, None]
            blur_k = jnp.asarray(BLUR_K)
            if typ == 'same':
                out = jax.vmap(_conv_same)(x, weight) + b[None, :, None]
            elif typ == 'upsample':
                out = jax.vmap(_conv_up)(x, weight.transpose(0, 2, 1, 3)) + b[None, :, None]
                out = _blur(out, 2.0 * blur_k, (1, 1))
            elif typ == 'downsample':
                xb = _blur(x, blur_k, (2, 2))
                out = jax.vmap(_conv_down)(xb, weight) + b[None, :, None]
            else:
                raise NotImplementedError(typ)
            return out
        out = x
        for i, typ in enumerate(TYPES):
            out = _layer(out, style, weights[i], biases[i], mod_w[i], mod_b[i], typ)
        return out

    def _L0_ffn_ref(x, A, B, Wr):
        import jax, jax.numpy as jnp
        import numpy as np
        BATCH, SEQ, D = (2, 512, 1024)
        K, TOPK, RANK = (64, 16, 16)
        ALPHA = 32.0
        SCALING = ALPHA / RANK
        prefix = x.shape[:-1]
        xf = x.reshape(-1, x.shape[-1])
        N = xf.shape[0]
        scores = xf @ Wr.T
        top_vals, top_idx = jax.lax.top_k(scores, TOPK)
        gates = jax.nn.softmax(top_vals, axis=-1)
        G = jnp.zeros((N, K), xf.dtype).at[jnp.arange(N)[:, None], top_idx].set(gates)
        h = jnp.einsum('nd,krd->nkr', xf, A)
        out = jnp.einsum('nkr,kdr->nd', h * G[:, :, None], B)
        return (out * SCALING).reshape(*prefix, -1)

    def _L1_cond_ref(x, style, weights, biases, mod_w, mod_b):
        import jax, jax.numpy as jnp
        from jax import lax
        import numpy as np
        CIN, COUT, K, STYLE_DIM = (64, 64, 3, 128)
        N_LAYERS = 4
        TYPES = ('same', 'upsample', 'same', 'downsample')
        SCALE = 1.0 / float(np.sqrt(CIN * K ** 2))
        EPS = 1e-08
        _BK = np.array([1.0, 3.0, 3.0, 1.0], dtype=np.float32)
        BLUR_K = _BK / _BK.sum()

        def _blur(x, kern, pad):
            B, C, _ = x.shape
            xp = jnp.pad(x, ((0, 0), (0, 0), (pad[0], pad[1])))
            w = jnp.broadcast_to(kern.astype(x.dtype)[None, None, :], (C, 1, kern.shape[0]))
            return lax.conv_general_dilated(xp, w, (1,), 'VALID', feature_group_count=C, dimension_numbers=('NCH', 'OIH', 'NCH'))

        def _conv_same(x, w):
            p = (K - 1) // 2
            return lax.conv_general_dilated(x[None], w, (1,), [(p, p)], dimension_numbers=('NCH', 'OIH', 'NCH'))[0]

        def _conv_down(x, w):
            return lax.conv_general_dilated(x[None], w, (2,), 'VALID', dimension_numbers=('NCH', 'OIH', 'NCH'))[0]

        def _conv_up(x, w_t):
            return lax.conv_transpose(x[None], w_t, (2,), 'VALID', dimension_numbers=('NCH', 'IOH', 'NCH'), transpose_kernel=True)[0]

        def _layer(x, style, w, b, mw, mb, typ):
            s = style @ mw.T + mb
            weight = SCALE * w * s[:, None, :, None]
            demod = lax.rsqrt(jnp.sum(weight * weight, axis=(2, 3)) + EPS)
            weight = weight * demod[:, :, None, None]
            blur_k = jnp.asarray(BLUR_K)
            if typ == 'same':
                out = jax.vmap(_conv_same)(x, weight) + b[None, :, None]
            elif typ == 'upsample':
                out = jax.vmap(_conv_up)(x, weight.transpose(0, 2, 1, 3)) + b[None, :, None]
                out = _blur(out, 2.0 * blur_k, (1, 1))
            elif typ == 'downsample':
                xb = _blur(x, blur_k, (2, 2))
                out = jax.vmap(_conv_down)(xb, weight) + b[None, :, None]
            else:
                raise NotImplementedError(typ)
            return out
        out = x
        for i, typ in enumerate(TYPES):
            out = _layer(out, style, weights[i], biases[i], mod_w[i], mod_b[i], typ)
        return out

    def _L1_ffn_ref(x, qweight, scales, zeros, bias):
        import jax, jax.numpy as jnp
        import numpy as np
        B, S, IN, OUT = (4, 512, 1024, 1024)
        PACK = 8

        def _dequant(qweight, scales, zeros):
            qw = jax.lax.bitcast_convert_type(qweight, jnp.uint32)
            shifts = jnp.arange(PACK, dtype=jnp.uint32) * jnp.uint32(4)
            nib = qw[:, None, :] >> shifts[None, :, None] & jnp.uint32(15)
            q = nib.reshape(-1, qw.shape[1]).astype(jnp.float32)
            return scales[:, 0][None, :] * q - zeros[:, 0][None, :]
        W = _dequant(qweight, scales, zeros)
        out = jnp.einsum('bsi,io->bso', x, W) + bias
        return out
    x = x + _L0_ffn_ref(_L0_cond_ref(x, cond_512, L0_cond_weights, L0_cond_biases, L0_cond_mod_w, L0_cond_mod_b), L0_ffn_A, L0_ffn_B, L0_ffn_Wr)
    x = x + _L1_ffn_ref(_L1_cond_ref(x, cond_512, L1_cond_weights, L1_cond_biases, L1_cond_mod_w, L1_cond_mod_b), L1_ffn_qweight, L1_ffn_scales, L1_ffn_zeros, L1_ffn_bias)
    return x

_drawn_inputs = setup_inputs


def setup_inputs(seed=0):
    import zlib

    import numpy as np

    out = dict(_drawn_inputs(seed))
    spreads = {}
    factors = {'L0_cond_weights': 8.0,
     'L0_cond_biases': 8.0,
     'L0_cond_mod_w': 8.0,
     'L0_cond_mod_b': 8.0,
     'L0_ffn_A': 8.0,
     'L0_ffn_B': 8.0,
     'L0_ffn_Wr': 8.0,
     'L1_ffn_bias': 64.0}
    for name, (base, spread) in spreads.items():
        noise = np.random.default_rng([zlib.crc32(name.encode()), seed]).standard_normal(out[name].shape)
        drawn = base * np.exp(spread * noise) if base else spread * noise
        out[name] = jnp.asarray(drawn.astype(out[name].dtype))
    for name, factor in factors.items():
        out[name] = (out[name] * factor).astype(out[name].dtype)
    return out
```

```python
from contextlib import ExitStack

import numpy as np

import concourse.bass as bass
import concourse.mybir as mybir

F32 = mybir.dt.float32
F32R = mybir.dt.float32r
I32 = mybir.dt.int32
ALU = mybir.AluOpType
ACT = mybir.ActivationFunctionType
AX = mybir.AxisListType

class Buffers:
    pass


B, C, D = 32, 64, 1024
STYLE = 128
P = 128
NPAIR = B // 2
H = D // 2
NE, RANK = 64, 16
KR = NE * RANK
KT = D // P
TAPS = 3
LAYERS = 4
SCALE = 1.0 / float(np.sqrt(C * TAPS ** 2))
EPS = 1e-8
LORA_SCALE = 2.0
LOWEST = -3.0e38
PACK = 8


def program(nc, t):
    with ExitStack() as outer:
        def sem(name):
            return outer.enter_context(nc.semaphore(name))

        def tensor(stack, name, shape, dt):
            return stack.enter_context(nc.sbuf_tensor(name, shape, dt))

        conv_ps = [outer.enter_context(nc.psum_tensor(f"conv_ps{i}", [P, 512], F32)) for i in range(4)]
        prod_ps = [outer.enter_context(nc.psum_tensor(f"prod_ps{i}", [P, 512], F32)) for i in range(2)]
        turn_ps = [outer.enter_context(nc.psum_tensor(f"turn_ps{i}", [P, 512], F32)) for i in range(2)]

        ident = tensor(outer, "ident", [P, P], F32)
        eps_col = tensor(outer, "eps_col", [P, 1], F32)
        w_hi = tensor(outer, "w_hi", [P, 12, P], F32R)
        w_lo = tensor(outer, "w_lo", [P, 12, P], F32R)
        style_tab = tensor(outer, "style_tab", [P, LAYERS, B], F32)
        demod_tab = tensor(outer, "demod_tab", [P, LAYERS, B], F32)
        scale1, bias1, scale2, bias2, edge2, scale3, bias3 = [
            tensor(outer, n, [P, B], F32) for n in ("scale1", "bias1", "scale2", "bias2", "edge2", "scale3", "bias3")]
        bias_tab = tensor(outer, "bias_tab", [P, LAYERS], F32)
        x_in = [tensor(outer, f"x_in{a}", [P, D + 2], F32) for a in range(2)]
        xz_hi = [tensor(outer, f"xz_hi{a}", [P, 2, H + 1], F32R) for a in range(2)]
        xz_lo = [tensor(outer, f"xz_lo{a}", [P, 2, H + 1], F32R) for a in range(2)]

        x_scratch = nc.dram_tensor("x_after_first", [NPAIR, P, D], F32, kind="Internal").ap()

        S = Buffers()
        S.ident_ready = sem("ident_ready")
        S.small_loaded = sem("small_loaded")
        S.table_step = sem("table_step")
        S.act_step = sem("act_step")
        S.pe_step = sem("pe_step")
        S.router_loaded = sem("router_loaded")
        S.a_loaded = sem("a_loaded")
        S.b_loaded = sem("b_loaded")
        S.weights_turned = sem("weights_turned")
        S.weights_hi = sem("weights_hi")
        S.weights_lo = sem("weights_lo")
        S.consts_loaded = sem("consts_loaded")
        S.quant_loaded = sem("quant_loaded")
        S.quant_ready = sem("quant_ready")
        S.xin_loaded0 = sem("xin_loaded0")
        S.xin_loaded1 = sem("xin_loaded1")
        S.xin_split = sem("xin_split")
        S.layer1_done = sem("layer1_done")
        S.layer2_done = sem("layer2_done")
        S.layer3_done = sem("layer3_done")
        S.layer4_done = sem("layer4_done")
        S.in2_hi = sem("in2_hi")
        S.in2_ready = sem("in2_ready")
        S.in3_hi = sem("in3_hi")
        S.in3_ready = sem("in3_ready")
        S.in4_hi = sem("in4_hi")
        S.in4_ready = sem("in4_ready")
        S.in2_scaled = sem("in2_scaled")
        S.in3_outer = sem("in3_outer")
        S.in3_inner = sem("in3_inner")
        S.in4_scaled = sem("in4_scaled")
        S.cond_ready = sem("cond_ready")
        S.turned = sem("turned")
        S.xt_hi = sem("xt_hi")
        S.xt_ready = sem("xt_ready")
        S.scored = sem("scored")
        S.top_max = sem("top_max")
        S.exp_ready = sem("exp_ready")
        S.hidden_done = sem("hidden_done")
        S.gated = sem("gated")
        S.gated_turned = sem("gated_turned")
        S.hgt_hi = sem("hgt_hi")
        S.hgt_ready = sem("hgt_ready")
        S.out_done = sem("out_done")
        S.x1_ready = sem("x1_ready")
        S.res_loaded = sem("res_loaded")
        S.x1_stored = sem("x1_stored")
        S.rowsum_done = sem("rowsum_done")
        S.rowsum_read = sem("rowsum_read")
        S.biased = sem("biased")
        S.y_ready = sem("y_ready")
        S.y_stored = sem("y_stored")
        S.dve_step = sem("dve_step")
        S.pads_ready = sem("pads_ready")
        S.tail = sem("tail")
        S.fix_q = sem("fix_q")

        x_pairs = t["x"].rearrange("(p two) c d -> p (two c) d", two=2)
        out_pairs = t["out"].rearrange("(p two) c d -> p (two c) d", two=2)

        def setup_buffers(stack, L):
            T = lambda n, s, d=F32: tensor(stack, f"L{L}_{n}", s, d)
            s = Buffers()
            s.style, s.style_T = T("style", [B, STYLE]), T("style_T", [STYLE, B])
            s.mod_w, s.mod_wT, s.mod_b = T("mod_w", [C, LAYERS, STYLE]), T("mod_wT", [STYLE, LAYERS, 2, C]), T("mod_b", [P, LAYERS])
            s.w, s.wsq, s.wsum = T("w", [P, LAYERS, C * TAPS]), T("wsq", [C, LAYERS, C * TAPS]), T("wsum", [C, LAYERS, C])
            s.wsum_T, s.style_sq = T("wsum_T", [C, LAYERS, 2, C]), T("style_sq", [P, LAYERS, B])
            s.same, s.down, s.up = [T(f"same{i}", [C, 5, C]) for i in range(2)], T("down", [C, 10, C]), T("up", [P, 8, C])
            s.blur, s.blur_d = [T(f"blur{i}", [P, 5 + i, C]) for i in range(3)], [T(f"blur_d{i}", [C, 5 + i, C]) for i in range(3)]
            s.var, s.root, s.newton = T("var", [P, LAYERS * B]), T("root", [P, LAYERS * B]), T("newton", [P, LAYERS * B])
            return s

        def setup_loads(sp, L, s):
            g = lambda n: t[f"L{L}_cond_{n}"]
            w = g("weights").rearrange("l o i k -> o l (i k)")
            with nc.allow_non_contiguous_dma(reason="a few hundred words"):
                for dst, src in (
                        (s.w[0:C], w), (s.w[C:P, 1], w[:, 1]), (s.style[:, :], t["cond_512"]),
                        (s.mod_w[:, :, :], g("mod_w").rearrange("l i k -> i l k")),
                        (s.mod_b[0:C], g("mod_b").rearrange("l i -> i l")), (s.mod_b[C:P], g("mod_b").rearrange("l i -> i l")),
                        (bias_tab[0:C], g("biases").rearrange("l i -> i l")), (bias_tab[C:P], g("biases").rearrange("l i -> i l"))):
                    sp.dma_start(dst, src).then_inc(S.small_loaded, 16)
        SMALL = 8 * 16

        TABLE_STEPS, ACT_STEPS, PE_STEPS = 29, 4, 5

        def setup_tensor(pe, L, s):
            tb, pb = L * TABLE_STEPS, L * PE_STEPS
            pe.wait_ge(S.ident_ready, 2)
            pe.wait_ge(S.small_loaded, SMALL * (L + 1))
            nc.tensor.transpose(turn_ps[0][:, 0:B], s.style[:, :], ident[0:B, 0:B])
            for l in range(LAYERS):
                last = nc.tensor.transpose(turn_ps[1][:, l * C:(l + 1) * C], s.mod_w[:, l, :], ident[0:C, 0:C])
            last.then_inc(S.pe_step, 1)
            pe.wait_ge(S.table_step, tb + 3)
            for l in range(LAYERS):
                last = nc.tensor.matmul(turn_ps[0][:, 64 + l * B:64 + (l + 1) * B], s.mod_wT[:, l].rearrange("k two i -> k (two i)"),
                                        s.style_T[:, :], start=True, stop=True)
            last.then_inc(S.pe_step, 1)
            pe.wait_ge(S.table_step, tb + 9)
            for l in range(LAYERS):
                last = nc.tensor.transpose(turn_ps[1][0:C, 256 + l * C:256 + (l + 1) * C], s.wsum[:, l, :], ident[0:C, 0:C])
            last.then_inc(S.pe_step, 1)
            pe.wait_ge(S.table_step, tb + 11)
            for l in range(LAYERS):
                last = nc.tensor.matmul(turn_ps[0][:, 256 + l * B:256 + (l + 1) * B], s.wsum_T[:, l].rearrange("i two o -> i (two o)"),
                                        s.style_sq[0:C, l, :], start=True, stop=True)
            last.then_inc(S.pe_step, 1)
            pe.wait_ge(S.table_step, tb + 16)
            for i in range(2):
                for q in range(2):
                    for f in range(2):
                        j = 2 - 2 * q + f
                        nc.tensor.transpose(conv_ps[0][:, (2 * i + q) * P + f * C:(2 * i + q) * P + (f + 1) * C],
                                            s.same[i][:, j:j + 2, :].rearrange("o j i -> o (j i)"), ident[0:C, 0:C])
            for q in range(4):
                for f in range(2):
                    j = 2 + 2 * q - 2 * f
                    last = nc.tensor.transpose(conv_ps[1][:, q * P + f * C:q * P + (f + 1) * C],
                                               s.down[:, j:j + 2, :].rearrange("o j i -> o (j i)"), ident[0:C, 0:C])
            last.then_inc(S.pe_step, 1)

        UP_PARTS = [(8, slice(0, 2), slice(4, 8, 3)), (9, slice(0, 2), slice(0, 4, 3)),
                    (10, slice(0, 1), slice(6, 7)), (10, slice(1, 2), slice(5, 6)),
                    (11, slice(0, 1), slice(2, 3)), (11, slice(1, 2), slice(1, 2))]

        def up_part(w, i):
            tile, halves, _ = UP_PARTS[i]
            return w[:, tile, :].rearrange("p (f o) -> p f o", f=2)[:, halves, :]

        def setup_scalar(act, L, s):
            tb, pb = L * TABLE_STEPS, L * PE_STEPS
            act.wait_ge(S.pe_step, pb + 4)
            act.wait_ge(S.ident_ready, 2)
            nc.scalar.activation(s.root[:, :], turn_ps[0][:, 256:256 + LAYERS * B], ACT.Sqrt, bias=eps_col[:, 0:1],
                                 scale=SCALE * SCALE).then_inc(S.act_step, 1)
            act.wait_ge(S.pe_step, pb + 5)
            for b in range(2):
                nc.scalar.activation(w_hi[:, 4 * b:4 * b + 4, :].rearrange("p q m -> p (q m)"), conv_ps[b][:, :],
                                     ACT.Identity).then_inc(S.act_step, 1)
            act.wait_ge(S.table_step, tb + 16)
            for i in range(len(UP_PARTS)):
                last = nc.scalar.activation(up_part(w_hi, i), s.up[:, UP_PARTS[i][2], :], ACT.Identity)
            last.then_inc(S.act_step, 1)

        def setup_vector(v, L, s):
            tb, pb, ab = L * TABLE_STEPS, L * PE_STEPS, L * ACT_STEPS
            count = [tb]

            def step(ins, wait=True):
                count[0] += 1
                ins.then_inc(S.table_step, 1)
                if wait:
                    v.wait_ge(S.table_step, count[0])

            V = nc.vector
            v.wait_ge(S.pe_step, pb + 1)
            step(V.tensor_copy(s.style_T[:, :], turn_ps[0][:, 0:B]), False)
            for half in range(2):
                step(V.tensor_copy(s.mod_wT[:, :, half, :], turn_ps[1][:, 0:LAYERS * C].rearrange("k (l i) -> k l i", l=LAYERS)), False)
            v.wait_ge(S.small_loaded, SMALL * (L + 1))
            step(V.tensor_tensor(s.wsq[:, :, :], s.w[0:C], s.w[0:C], ALU.mult))
            v.wait_ge(S.pe_step, pb + 2)
            for l in range(LAYERS):
                step(V.tensor_scalar(style_tab[:, l, :], turn_ps[0][:, 64 + l * B:64 + (l + 1) * B], s.mod_b[:, l:l + 1], None, ALU.add), False)
            step(V.tensor_reduce(s.wsum[:, :, :].rearrange("o l i -> o (l i)"),
                                 s.wsq[:, :, :].rearrange("o l (i k) -> o (l i) k", k=TAPS), AX.X, ALU.add))
            v.wait_ge(S.pe_step, pb + 3)
            src = turn_ps[1][0:C, 256:512].rearrange("i (l o) -> i l o", l=LAYERS)
            V.tensor_copy(s.wsum_T[:, :, 0, :], src)
            V.tensor_copy(s.wsum_T[:, :, 1, :], src)
            step(V.tensor_tensor(s.style_sq[:, :, :], style_tab[:, :, :], style_tab[:, :, :], ALU.mult), False)
            step(V.memset(s.same[0][:, :, :], 0.0), False)
            V.memset(s.same[1][:, :, :], 0.0)
            V.memset(s.down[:, :, :], 0.0)
            V.memset(s.up[:, :, :], 0.0)
            for b in s.blur + s.blur_d:
                last = V.memset(b[:, :, :], 0.0)
            step(last)
            taps = lambda l, k, hi=C: s.w[0:hi, l, :].rearrange("o (i k) -> o k i", k=TAPS)[:, k, :]
            for n, l in ((0, 0), (1, 2)):
                for k in range(TAPS):
                    V.tensor_scalar(s.same[n][:, 3 - k, :], taps(l, k), SCALE, None, ALU.mult)
            for k in range(TAPS):
                V.tensor_scalar(s.blur_d[0][:, 1 + k, :], taps(3, k), SCALE / 8, None, ALU.mult)
                last = V.tensor_scalar(s.blur[0][:, 1 + k, :], taps(1, k, P), SCALE / 4, None, ALU.mult)
            step(last)
            for i in range(2):
                V.tensor_tensor(s.blur_d[i + 1][:, 1:5 + i, :], s.blur_d[i][:, 1:5 + i, :], s.blur_d[i][:, 0:4 + i, :], ALU.add)
                step(V.tensor_tensor(s.blur[i + 1][:, 1:5 + i, :], s.blur[i][:, 1:5 + i, :], s.blur[i][:, 0:4 + i, :], ALU.add))
            V.tensor_tensor(s.down[:, 2:8, :], s.blur_d[2][:, 1:7, :], s.blur_d[2][:, 0:6, :], ALU.add)
            V.tensor_tensor(s.up[0:C, 2:8, :], s.blur[2][0:C, 1:7, :], s.blur[2][0:C, 0:6, :], ALU.add)
            step(V.tensor_tensor(s.up[C:P, 0:6, :], s.blur[2][C:P, 1:7, :], s.blur[2][C:P, 0:6, :], ALU.add))
            v.wait_ge(S.act_step, ab + 1)
            v.wait_ge(S.pe_step, pb + 4)
            demod = demod_tab[:, :, :].rearrange("o l b -> o (l b)")
            V.tensor_scalar(s.var[:, :], turn_ps[0][:, 256:256 + LAYERS * B], SCALE * SCALE, EPS, ALU.mult, ALU.add)
            step(V.reciprocal(demod, s.root[:, :]))
            step(V.tensor_tensor(s.newton[:, :], demod, demod, ALU.mult))
            step(V.tensor_tensor(s.newton[:, :], s.newton[:, :], s.var[:, :], ALU.mult))
            step(V.tensor_scalar(s.newton[:, :], s.newton[:, :], -0.5, 1.5, ALU.mult, ALU.add))
            step(V.tensor_tensor(demod, demod, s.newton[:, :], ALU.mult))
            st, de = (lambda l: style_tab[:, l, :]), (lambda l: demod_tab[:, l, :])
            bi = lambda l: bias_tab[:, l:l + 1]
            step(V.tensor_tensor(scale1[:, :], de(0), de(1), ALU.mult), False)
            step(V.tensor_scalar(bias1[:, :], de(1), bi(0), None, ALU.mult), False)
            step(V.tensor_tensor(scale2[:, :], st(1), st(2), ALU.mult), False)
            step(V.tensor_scalar(bias2[:, :], st(2), bi(1), 2.0, ALU.mult, ALU.mult), False)
            step(V.tensor_scalar(edge2[:, :], st(2), bi(1), -0.25, ALU.mult, ALU.mult), False)
            step(V.tensor_tensor(scale3[:, :], de(2), st(3), ALU.mult), False)
            step(V.tensor_scalar(bias3[:, :], st(3), bi(2), None, ALU.mult), False)
            for b in range(2):
                v.wait_ge(S.act_step, ab + 2 + b)
                V.tensor_tensor(w_lo[:, 4 * b:4 * b + 4, :].rearrange("p q m -> p (q m)"), conv_ps[b][:, :],
                                w_hi[:, 4 * b:4 * b + 4, :].rearrange("p q m -> p (q m)").bitcast(F32), ALU.subtract)
            v.wait_ge(S.act_step, ab + 4)
            for i in range(len(UP_PARTS)):
                last = V.tensor_tensor(up_part(w_lo, i), s.up[:, UP_PARTS[i][2], :], up_part(w_hi, i).bitcast(F32), ALU.subtract)
            step(last, False)

        def at(tab, c, a, bufs):
            n = 2 * c + a - bufs.first_sample
            return tab[:, n:n + 1] if isinstance(n, int) else tab[:, bass.ds(n, 1)]

        def products(out, tiles, rhs_hi, rhs_lo):
            n = len(tiles)
            for i, w in enumerate(tiles):
                nc.tensor.matmul(out, w_hi[:, w, :], rhs_hi(i), start=(i == 0), stop=False)
                nc.tensor.matmul(out, w_hi[:, w, :], rhs_lo(i), start=False, stop=False)
                last = nc.tensor.matmul(out, w_lo[:, w, :], rhs_hi(i), start=False, stop=(i == n - 1))
            return last

        def pe_layer1(pe, c, a):
            pe.wait_ge(S.xin_split, 2 * c + a + 1)
            cut = lambda w: (lambda i: w[a][:, 0, i:i + H])
            products(conv_ps[a][:, :], (0, 1), cut(xz_hi), cut(xz_lo)).then_inc(S.layer1_done, 1)

        def pe_layer2(pe, c, a):
            pe.wait_ge(S.in2_ready, 2 * c + a + 1)
            cut = lambda w: (lambda i: w[a][:, 1, i:i + H])
            for m in range(2):
                products(conv_ps[2 - 2 * a + m][:, :], (8 + 2 * m, 9 + 2 * m), cut(xz_hi), cut(xz_lo)).then_inc(S.layer2_done, 1)

        def pe_layer3(pe, c, a, bufs):
            pe.wait_ge(S.in3_ready, 2 * c + a + 1)
            cut = lambda w, m: (lambda i: w[a][:, (m + i) % 2, (m + i) // 2:(m + i) // 2 + H])
            for m in range(2):
                products(conv_ps[2 - 2 * a + m][:, :], (2, 3), cut(bufs.s_hi, m), cut(bufs.s_lo, m)).then_inc(S.layer3_done, 1)

        def pe_layer4(pe, c, a):
            pe.wait_ge(S.in4_ready, 2 * c + a + 1)
            cut = lambda w: (lambda i: w[a][:, (i + 1) % 2, (0, 0, 1, 1)[i]:(0, 0, 1, 1)[i] + H])
            products(conv_ps[2 + a][:, :], (4, 5, 6, 7), cut(xz_hi), cut(xz_lo)).then_inc(S.layer4_done, 1)

        def act_layer1(act, c, a, bufs):
            act.wait_ge(S.layer1_done, 2 * c + a + 1)
            act.nop(nofuse=True)
            ps, hi = conv_ps[a], xz_hi[a]
            sc, bi = at(scale1, c, a, bufs), at(bias1, c, a, bufs)
            nc.scalar.activation(ps[:, :], ps[:, :], ACT.Identity, bias=bi, scale=sc).then_inc(S.in2_scaled, 1)
            act.wait_ge(S.in2_scaled, 2 * c + a + 1)
            nc.scalar.activation(hi[0:C, 1, 0:H], ps[0:C, :], ACT.Identity)
            nc.scalar.activation(hi[C:P, 1, 1:H + 1], ps[C:P, :], ACT.Identity).then_inc(S.in2_hi, 1)

        def act_layer2(act, c, a, bufs):
            sc, bi, ed = at(scale2, c, a, bufs), at(bias2, c, a, bufs), at(edge2, c, a, bufs)
            outer_ps, inner_ps, hi = conv_ps[2 - 2 * a], conv_ps[3 - 2 * a], bufs.s_hi[a]
            act.wait_ge(S.layer2_done, 4 * c + 2 * a + 1)
            act.nop(nofuse=True)
            nc.scalar.activation(outer_ps[:, :], outer_ps[:, :], ACT.Identity, bias=bi, scale=sc).then_inc(S.in3_outer, 1)
            act.wait_ge(S.layer2_done, 4 * c + 2 * a + 2)
            act.nop(nofuse=True)
            nc.scalar.activation(inner_ps[:, :], inner_ps[:, :], ACT.Identity, bias=bi, scale=sc).then_inc(S.in3_inner, 1)
            act.wait_ge(S.in3_outer, 6 * c + 3 * a + 1)
            act.nop(nofuse=True)
            nc.scalar.activation(outer_ps[0:C, 0:1], outer_ps[0:C, 0:1], ACT.Identity, bias=ed[0:C]).then_inc(S.in3_outer, 1)
            nc.scalar.activation(outer_ps[C:P, H - 1:H], outer_ps[C:P, H - 1:H], ACT.Identity, bias=ed[C:P]).then_inc(S.in3_outer, 1)
            act.wait_ge(S.in3_inner, 2 * c + a + 1)
            nc.scalar.activation(hi[:, 1, 0:H], inner_ps[:, :], ACT.Identity).then_inc(S.in3_hi, 1)
            act.wait_ge(S.in3_outer, 6 * c + 3 * a + 3)
            nc.scalar.activation(hi[0:C, 0, 0:H], outer_ps[0:C, :], ACT.Identity)
            nc.scalar.activation(hi[C:P, 0, 1:H + 1], outer_ps[C:P, :], ACT.Identity).then_inc(S.in3_hi, 1)

        def act_layer3(act, c, a, bufs):
            sc, bi = at(scale3, c, a, bufs), at(bias3, c, a, bufs)
            for m in range(2):
                ps = conv_ps[2 - 2 * a + m]
                act.wait_ge(S.layer3_done, 4 * c + 2 * a + m + 1)
                act.nop(nofuse=True)
                nc.scalar.activation(ps[:, :], ps[:, :], ACT.Identity, bias=bi, scale=sc).then_inc(S.in4_scaled, 1)
                act.wait_ge(S.in4_scaled, 4 * c + 2 * a + m + 1)
                nc.scalar.activation(xz_hi[a][:, m, m:m + H], ps[:, :], ACT.Identity).then_inc(S.in4_hi, 1)

        def act_layer4(act, c, a, bufs):
            act.wait_ge(S.layer4_done, 2 * c + a + 1)
            act.nop(nofuse=True)
            dm = demod_tab[:, LAYERS - 1, :]
            nc.scalar.activation(bufs.cond[:, a, :], conv_ps[2 + a][:, :], ACT.Identity, bias=bias_tab[:, LAYERS - 1:LAYERS],
                                 scale=at(dm, c, a, bufs)).then_inc(S.cond_ready, 1)

        def low(out, whole, hi):
            return nc.vector.tensor_tensor(out, whole, hi.bitcast(F32), ALU.subtract)

        def dve_split(v, c, a, bufs, first):
            v.wait_ge((S.xin_loaded0, S.xin_loaded1)[a], 32 * (c + 1))
            if not first:
                v.wait_ge(S.layer4_done, 2 * c + a - 1)
            src = x_in[a][:, 0:D + 2].rearrange("p (j two) -> p two j", two=2)[:, 0, :]
            sc = at(style_tab[:, 0, :], c, a, bufs)
            nc.vector.tensor_scalar(xz_hi[a][:, 0, :], src, sc, None, ALU.mult).then_inc(S.dve_step, 1)
            v.wait_ge(S.dve_step, 2 * c + a + 1)
            nc.vector.scalar_tensor_tensor(out=xz_lo[a][:, 0, :], in0=src, scalar=sc, in1=xz_hi[a][:, 0, :].bitcast(F32),
                                           op0=ALU.mult, op1=ALU.subtract).then_inc(S.xin_split, 1)

        def dve_layer1(v, c, a):
            v.wait_ge(S.in2_hi, 2 * c + a + 1)
            low(xz_lo[a][0:C, 1, 0:H], conv_ps[a][0:C, :], xz_hi[a][0:C, 1, 0:H])
            low(xz_lo[a][C:P, 1, 1:H + 1], conv_ps[a][C:P, :], xz_hi[a][C:P, 1, 1:H + 1]).then_inc(S.in2_ready, 1)

        def dve_layer2(v, c, a, bufs):
            hi, lo = bufs.s_hi[a], bufs.s_lo[a]
            v.wait_ge(S.in3_hi, 4 * c + 2 * a + 1)
            low(lo[:, 1, 0:H], conv_ps[3 - 2 * a][:, :], hi[:, 1, 0:H])
            ps = conv_ps[2 - 2 * a]
            v.wait_ge(S.in3_hi, 4 * c + 2 * a + 2)
            low(lo[0:C, 0, 0:H], ps[0:C, :], hi[0:C, 0, 0:H])
            low(lo[C:P, 0, 1:H + 1], ps[C:P, :], hi[C:P, 0, 1:H + 1]).then_inc(S.in3_ready, 1)

        def dve_layer3(v, c, a):
            for m in range(2):
                v.wait_ge(S.in4_hi, 4 * c + 2 * a + m + 1)
                last = low(xz_lo[a][:, m, m:m + H], conv_ps[2 - 2 * a + m][:, :], xz_hi[a][:, m, m:m + H])
            last.then_inc(S.in4_ready, 1)

        def dve_pads(v, bufs):
            for a in range(2):
                for w in (bufs.s_hi[a], bufs.s_lo[a]):
                    nc.vector.memset(w[C:P, 0, 0:1].bitcast(F32), 0.0)
                    last = nc.vector.memset(w[0:C, 0, H:H + 1].bitcast(F32), 0.0)
            return last

        def pe_turn(pe, f, bufs, packed):
            for a in range(2):
                pe.wait_ge(S.cond_ready, 2 * f + a + 1)
                for j in range(4):
                    cols = slice(j, H, 4) if packed else slice(j * P, (j + 1) * P)
                    last = nc.tensor.transpose(turn_ps[a][:, j * P:(j + 1) * P], bufs.cond[:, a, cols], ident[:, :])
                last.then_inc(S.turned, 1)

        def act_turn(act, f, bufs):
            for a in range(2):
                act.wait_ge(S.turned, 2 * f + a + 1)
                nc.scalar.activation(bufs.xt_hi[:, :, a * C:(a + 1) * C], turn_ps[a][:, :].rearrange("p (k o) -> p k o", k=KT),
                                     ACT.Identity).then_inc(S.xt_hi, 1)

        def dve_turn(v, f, bufs):
            for a in range(2):
                v.wait_ge(S.xt_hi, 2 * f + a + 1)
                low(bufs.xt_lo[:, :, a * C:(a + 1) * C], turn_ps[a][:, :].rearrange("p (k o) -> p k o", k=KT),
                    bufs.xt_hi[:, :, a * C:(a + 1) * C]).then_inc(S.xt_ready, 1)

        def pe_scores_hidden(pe, f, bufs):
            pe.wait_ge(S.xt_ready, 2 * f + 2)
            for part, (xt, wr) in enumerate(((bufs.xt_hi, bufs.wr_hi), (bufs.xt_hi, bufs.wr_lo), (bufs.xt_lo, bufs.wr_hi))):
                for k in range(KT):
                    last = nc.tensor.matmul(turn_ps[0][:, 0:NE], xt[:, k, :], wr[:, k, :],
                                            start=(part == 0 and k == 0), stop=(part == 2 and k == KT - 1))
            last.then_inc(S.scored, 1)
            pe.wait_ge(S.x1_ready, 2 * f + 1)
            for n in range(2):
                cols = slice(n * 512, (n + 1) * 512)
                for k in range(KT):
                    nc.tensor.matmul(prod_ps[n][:, :], bufs.xt_hi[:, k, :], bufs.a_hi[:, k, cols], start=(k == 0), stop=False)
                    nc.tensor.matmul(prod_ps[n][:, :], bufs.xt_hi[:, k, :], bufs.a_lo[:, k, cols], start=False, stop=False)
                    last = nc.tensor.matmul(prod_ps[n][:, :], bufs.xt_lo[:, k, :], bufs.a_hi[:, k, cols], start=False, stop=(k == KT - 1))
                last.then_inc(S.hidden_done, 1)

        def pe_gated_turn(pe, f, bufs):
            for n in range(2):
                pe.wait_ge(S.gated, 2 * f + n + 1)
                for j in range(4):
                    last = nc.tensor.transpose(turn_ps[n][:, j * P:(j + 1) * P], bufs.gated[:, n * 512 + j * P:n * 512 + (j + 1) * P], ident[:, :])
                last.then_inc(S.gated_turned, 1)

        def pe_adapter_out(pe, f, bufs):
            pe.wait_ge(S.hgt_ready, 2 * f + 2)
            for n in range(2):
                cols = slice(n * 512, (n + 1) * 512)
                for k in range(KT):
                    nc.tensor.matmul(prod_ps[n][:, :], bufs.xt_hi[:, k, :], bufs.b_hi[:, k, cols], start=(k == 0), stop=False)
                    nc.tensor.matmul(prod_ps[n][:, :], bufs.xt_hi[:, k, :], bufs.b_lo[:, k, cols], start=False, stop=False)
                    last = nc.tensor.matmul(prod_ps[n][:, :], bufs.xt_lo[:, k, :], bufs.b_hi[:, k, cols], start=False, stop=(k == KT - 1))
                last.then_inc(S.out_done, 1)

        def act_exp(act, f, bufs):
            act.wait_ge(S.top_max, f + 1)
            nc.scalar.activation(bufs.gate_exp[:, :], bufs.scores[:, :], ACT.Exp, bias=bufs.neg_max[:, 0:1]).then_inc(S.exp_ready, 1)

        def act_gated_turn(act, f, bufs):
            for n in range(2):
                act.wait_ge(S.gated_turned, 2 * f + n + 1)
                nc.scalar.activation(bufs.xt_hi[:, 4 * n:4 * n + 4, :].rearrange("p k o -> p (k o)"), turn_ps[n][:, :],
                                     ACT.Identity).then_inc(S.hgt_hi, 1)

        TOP_STEPS = 9

        def dve_route(v, f, bufs):
            V = nc.vector
            n = [0]

            def step(ins):
                n[0] += 1
                ins.then_inc(S.tail, 1)
                v.wait_ge(S.tail, TOP_STEPS * f + n[0])
                v.nop(nofuse=True)

            v.wait_ge(S.scored, f + 1)
            step(V.tensor_copy(bufs.scores[:, :], turn_ps[0][:, 0:NE]))
            step(V.max(bufs.top[:, 0:8], bufs.scores[:, :]))
            V.tensor_scalar(bufs.neg_max[:, :], bufs.top[:, 0:1], -1.0, None, ALU.mult).then_inc(S.top_max, 1)
            step(V.match_replace(bufs.rest[:, :], bufs.top[:, 0:8], bufs.scores[:, :], LOWEST))
            step(V.max(bufs.top[:, 8:16], bufs.rest[:, :]))
            step(V.match_replace(bufs.rest2[:, :], bufs.top[:, 8:16], bufs.rest[:, :], LOWEST))
            step(V.tensor_tensor(bufs.chosen[:, :], bufs.rest2[:, :], bufs.scores[:, :], ALU.is_lt))
            v.wait_ge(S.exp_ready, f + 1)
            step(V.tensor_tensor(bufs.gate[:, :], bufs.gate_exp[:, :], bufs.chosen[:, :], ALU.mult))
            step(V.tensor_reduce(bufs.norm[:, 0:1], bufs.gate[:, :], AX.X, ALU.add))
            step(V.reciprocal(bufs.norm[:, 1:2], bufs.norm[:, 0:1]))
            V.tensor_scalar(bufs.norm[:, 2:3], bufs.norm[:, 1:2], LORA_SCALE, None, ALU.mult)

        def dve_gate(v, f, bufs):
            for n in range(2):
                v.wait_ge(S.hidden_done, 2 * f + n + 1)
                shape = lambda ap: ap.rearrange("p (k r) -> p k r", r=RANK)
                nc.vector.tensor_tensor(shape(bufs.gated[:, n * 512:(n + 1) * 512]), shape(prod_ps[n][:, :]),
                                        bufs.gate[:, n * 32:(n + 1) * 32].unsqueeze(2).broadcast_to([P, 32, RANK]), ALU.mult).then_inc(S.gated, 1)

        def dve_gated_turn(v, f, bufs):
            for n in range(2):
                v.wait_ge(S.hgt_hi, 2 * f + n + 1)
                low(bufs.xt_lo[:, 4 * n:4 * n + 4, :].rearrange("p k o -> p (k o)"), turn_ps[n][:, :],
                    bufs.xt_hi[:, 4 * n:4 * n + 4, :].rearrange("p k o -> p (k o)")).then_inc(S.hgt_ready, 1)

        def dve_first_residual(v, f, bufs):
            v.wait_ge(S.res_loaded, 16 * (f + 1))
            for n in range(2):
                cols = slice(n * 512, (n + 1) * 512)
                v.wait_ge(S.out_done, 2 * f + n + 1)
                nc.vector.scalar_tensor_tensor(out=bufs.res[:, cols], in0=prod_ps[n][:, :], scalar=bufs.norm[:, 2:3], in1=bufs.res[:, cols],
                                               op0=ALU.mult, op1=ALU.add).then_inc(S.x1_ready, 1)

        def pe_rowsum(pe, f, bufs):
            pe.wait_ge(S.xt_ready, 2 * f + 2)
            for i, xt in enumerate((bufs.xt_hi, bufs.xt_lo)):
                for k in range(KT):
                    last = nc.tensor.matmul(turn_ps[0][:, 0:2], xt[:, k, :], bufs.ones[:, :], start=(i + k == 0), stop=(i == 1 and k == KT - 1))
            last.then_inc(S.rowsum_done, 1)

        def pe_quant(pe, f, n, bufs):
            if n == 0:
                pe.wait_ge(S.x1_ready, 2 * f + 1)
            cols = slice(n * 512, (n + 1) * 512)
            for k in range(KT):
                nc.tensor.matmul(prod_ps[n][:, :], bufs.xt_hi[:, k, :], bufs.quant[:, k, cols], start=(k == 0), stop=False)
                last = nc.tensor.matmul(prod_ps[n][:, :], bufs.xt_lo[:, k, :], bufs.quant[:, k, cols], start=False, stop=(k == KT - 1))
            last.then_inc(S.out_done, 1)

        def dve_rowsum(v, f, bufs):
            v.wait_ge(S.rowsum_done, f - NPAIR + 1)
            nc.vector.tensor_scalar(bufs.neg_sum[:, :], turn_ps[0][:, 0:1], -1.0, None, ALU.mult).then_inc(S.rowsum_read, 1)

        def dve_second_residual(v, f, bufs):
            g = f - NPAIR
            v.wait_ge(S.biased, g + 1)
            v.wait_ge(S.rowsum_read, g + 2)
            for n in range(2):
                cols = slice(n * 512, (n + 1) * 512)
                nc.vector.scalar_tensor_tensor(out=bufs.res[:, cols], in0=bufs.zeros[:, cols], scalar=bufs.neg_sum[:, 0:1], in1=bufs.res[:, cols],
                                               op0=ALU.mult, op1=ALU.add)
            for n in range(2):
                cols = slice(n * 512, (n + 1) * 512)
                v.wait_ge(S.out_done, 2 * f + n + 1)
                nc.vector.tensor_tensor(bufs.scaled[:, cols], prod_ps[n][:, :], bufs.scales[:, cols], ALU.mult).then_inc(S.x1_ready, 1)
            v.wait_ge(S.x1_ready, 2 * f + 3)
            nc.vector.tensor_tensor(bufs.res[:, :], bufs.res[:, :], bufs.scaled[:, :], ALU.add).then_inc(S.y_ready, 1)

        def work_buffers(stack, L):
            T = lambda n, s, d=F32: tensor(stack, f"L{L}_{n}", s, d)
            w = Buffers()
            w.s_hi = [T(f"s_hi{a}", [P, 2, H + 1], F32R) for a in range(2)]
            w.s_lo = [T(f"s_lo{a}", [P, 2, H + 1], F32R) for a in range(2)]
            w.xt_hi, w.xt_lo = T("xt_hi", [P, KT, P], F32R), T("xt_lo", [P, KT, P], F32R)
            w.cond, w.res = T("cond", [P, 2, H]), T("res", [P, D])
            w.first_sample = B * L
            w.gated = w.cond[:, :, :].rearrange("p a h -> p (a h)")
            return w

        level0 = ExitStack()
        a_hi = tensor(level0, "a_hi", [P, KT, KR], F32R)
        a_lo = tensor(level0, "a_lo", [P, KT, KR], F32R)
        wr_hi = tensor(level0, "wr_hi", [P, KT, NE], F32R)
        wr_lo = tensor(level0, "wr_lo", [P, KT, NE], F32R)
        with ExitStack() as stage:
            a_nat = tensor(stage, "a_nat", [P, KT, D], F32)
            set0 = setup_buffers(stage, 0)
            wr_nat = tensor(stage, "wr_nat", [NE, D], F32)
            b_nat = tensor(stage, "b_nat", [P, KT, KR], F32)
        b_hi = tensor(level0, "b_hi", [P, KT, D], F32R)
        b_lo = tensor(level0, "b_lo", [P, KT, D], F32R)
        buf0 = work_buffers(level0, 0)
        buf0.a_hi, buf0.a_lo, buf0.b_hi, buf0.b_lo, buf0.wr_hi, buf0.wr_lo = a_hi, a_lo, b_hi, b_lo, wr_hi, wr_lo
        T0 = lambda n, s: tensor(level0, n, s, F32)
        buf0.scores, buf0.rest, buf0.rest2, buf0.chosen = T0("scores", [P, NE]), T0("rest", [P, NE]), T0("rest2", [P, NE]), T0("chosen", [P, NE])
        buf0.gate_exp, buf0.gate, buf0.top = T0("gate_exp", [P, NE]), T0("gate", [P, NE]), T0("top", [P, 2 * 8])
        buf0.neg_max, buf0.norm = T0("neg_max", [P, 1]), T0("norm", [P, 3])
        level0.close()

        level1 = ExitStack()
        buf1 = work_buffers(level1, 1)
        T1 = lambda n, s, d=F32: tensor(level1, n, s, d)
        buf1.quant, buf1.ones = T1("quant", [P, KT, D], F32R), T1("ones", [P, 2], F32R)
        buf1.scales, buf1.zeros, buf1.bias = T1("scales", [P, D]), T1("zeros", [P, D]), T1("bias", [P, D])
        buf1.scaled, buf1.neg_sum = T1("scaled", [P, D]), T1("neg_sum", [P, 1])
        set1 = setup_buffers(level1, 1)
        packed, nibble = T1("packed", [P, D], I32), [T1(f"nibble{i}", [P, D], I32) for i in range(2)]
        level1.close()

        a_src, b_src, r_src = t["L0_ffn_A"].rearrange("(g k) r d -> (k r) g d", g=KT), t["L0_ffn_B"].rearrange("k (g d) r -> g d k r", g=KT), t["L0_ffn_Wr"]
        group_ps = [conv_ps[2], conv_ps[3], prod_ps[0], prod_ps[1]]
        GROUPS = [("r", 0, 0)] + [("a", k, h) for k in range(KT) for h in range(2)] + [("b", k, h) for k in range(KT) for h in range(2)]
        position = lambda k: slice(2 * P * (k // 2) + k % 2, 2 * P * (k // 2 + 1), 2)

        def group_out(parts, g):
            kind, k, h = GROUPS[g]
            w = parts[{"r": 0, "a": 1, "b": 2}[kind]]
            return w[:, :, :].rearrange("p k e -> p (k e)") if kind == "r" else w[:, k, h * 512:(h + 1) * 512]

        def pe_turn_weights(pe):
            pe.wait_ge(S.router_loaded, 16)
            for g, (kind, k, h) in enumerate(GROUPS):
                if g >= 4:
                    pe.wait_ge(S.weights_lo, g - 3)
                if (kind, k, h) == ("a", 0, 0):
                    pe.wait_ge(S.a_loaded, 16)
                if (kind, k, h) == ("b", 0, 0):
                    pe.wait_ge(S.b_loaded, 16 * KT)
                ps = group_ps[g % 4]
                if kind == "r":
                    for kk in range(KT):
                        last = nc.tensor.transpose(ps[:, kk * NE:(kk + 1) * NE], wr_nat[:, position(kk)], ident[0:NE, 0:NE])
                else:
                    for j in range(4):
                        src = a_nat[:, 4 * h + j, position(k)] if kind == "a" else b_nat[:, 4 * h + j, k * P:(k + 1) * P]
                        last = nc.tensor.transpose(ps[:, j * P:(j + 1) * P], src, ident[:, :])
                last.then_inc(S.weights_turned, 1)

        def sp_load(sp, c, first):
            src = x_pairs if first else x_scratch
            for a in range(2):
                rows = src[c if first else c - NPAIR, a * C:(a + 1) * C, :]
                done = (S.xin_loaded0, S.xin_loaded1)[a]
                sp.dma_start(x_in[a][0:C, 0:D], rows).then_inc(done, 16)
                sp.dma_start(x_in[a][C:P, 1:D + 1], rows).then_inc(done, 16)

        block = outer.enter_context(nc.Block())

        @block.sync
        def _(sp):
            setup_loads(sp, 0, set0)
            sp.dma_start(wr_nat[:, :], r_src).then_inc(S.router_loaded, 16)
            sp.dma_start(a_nat[:, :, :], a_src).then_inc(S.a_loaded, 16)
            for g in range(KT):
                sp.dma_start(b_nat[:, g, :].rearrange("d (k r) -> d k r", r=RANK), b_src[g]).then_inc(S.b_loaded, 16)
            sp_load(sp, 0, True)
            with sp.Fori(0, NPAIR - 1) as i:
                sp.wait_ge(S.xin_split, 2 * i + 2)
                sp_load(sp, i + 1, True)
            sp.wait_ge(S.x1_stored, 16 * NPAIR)
            setup_loads(sp, 1, set1)
            sp.dma_start(packed[:, :], t["L1_ffn_qweight"]).then_inc(S.quant_loaded, 16)
            for dst, src in ((buf1.scales, t["L1_ffn_scales"].rearrange("o u -> u o")), (buf1.zeros, t["L1_ffn_zeros"].rearrange("o u -> u o")),
                             (buf1.bias, t["L1_ffn_bias"].rearrange("(u o) -> u o", u=1))):
                sp.dma_start(dst[:, :], src.broadcast_to([P, D])).then_inc(S.consts_loaded, 16)
            sp_load(sp, NPAIR, False)
            with sp.Fori(NPAIR, 2 * NPAIR - 1) as i:
                sp.wait_ge(S.xin_split, 2 * i + 2)
                sp_load(sp, i + 1, False)

        @block.gpsimd
        def _(pool):
            nc.gpsimd.memset(ident[:, :], 0.0).then_inc(S.pads_ready, 1)
            nc.gpsimd.memset(eps_col[:, :], EPS).then_inc(S.ident_ready, 1)
            pool.wait_ge(S.pads_ready, 1)
            nc.gpsimd.affine_select(out=ident[:, :], in_=ident[:, :], compare_op=ALU.not_equal, fill=1.0, base=0,
                                    pattern=[[-1, P]], channel_multiplier=1).then_inc(S.ident_ready, 1)
            pool.wait_ge(S.weights_turned, len(GROUPS))
            pool.dma_start(buf0.res[:, :], x_pairs[0]).then_inc(S.res_loaded, 16)
            with pool.Fori(0, NPAIR - 1) as i:
                pool.wait_ge(S.x1_ready, 2 * i + 3)
                pool.dma_start(x_scratch[i], buf0.res[:, :]).then_inc(S.x1_stored, 16)
                pool.wait_ge(S.x1_stored, 16 * i + 16)
                pool.dma_start(buf0.res[:, :], x_pairs[i + 1]).then_inc(S.res_loaded, 16)
            pool.wait_ge(S.x1_ready, 2 * NPAIR + 1)
            pool.dma_start(x_scratch[NPAIR - 1], buf0.res[:, :]).then_inc(S.x1_stored, 16)
            pool.wait_ge(S.x1_stored, 16 * NPAIR)
            pool.wait_ge(S.consts_loaded, 16 * 3)
            pool.dma_start(buf1.res[:, :], x_scratch[0]).then_inc(S.res_loaded, 16)

            def add_bias(f):
                pool.wait_ge(S.res_loaded, 16 * (f + 1))
                nc.gpsimd.tensor_tensor(buf1.res[:, :], buf1.res[:, :], buf1.bias[:, :], ALU.add).then_inc(S.biased, 1)

            with pool.Fori(0, NPAIR - 1) as i:
                add_bias(i + NPAIR)
                pool.wait_ge(S.y_ready, i + 1)
                pool.dma_start(out_pairs[i], buf1.res[:, :]).then_inc(S.y_stored, 16)
                pool.wait_ge(S.y_stored, 16 * i + 16)
                pool.dma_start(buf1.res[:, :], x_scratch[i + 1]).then_inc(S.res_loaded, 16)
            add_bias(2 * NPAIR - 1)
            pool.wait_ge(S.y_ready, NPAIR)
            pool.dma_start(out_pairs[NPAIR - 1], buf1.res[:, :]).then_inc(S.y_stored, 16)
            pool.wait_ge(S.y_stored, 16 * NPAIR)

        @block.tensor
        def _(pe):
            setup_tensor(pe, 0, set0)
            pe_turn_weights(pe)
            pe.wait_ge(S.table_step, TABLE_STEPS)
            pe.wait_ge(S.weights_lo, len(GROUPS))
            for a in range(2):
                pe_layer1(pe, 0, a)
            for a in range(2):
                pe_layer2(pe, 0, a)
            for a in range(2):
                pe_layer3(pe, 0, a, buf0)
            for a in range(2):
                pe_layer4(pe, 0, a)
            with pe.Fori(0, NPAIR - 1) as i:
                c = i + 1
                pe_layer1(pe, c, 0)
                pe_turn(pe, i, buf0, False)
                pe_layer1(pe, c, 1)
                pe_scores_hidden(pe, i, buf0)
                pe_layer2(pe, c, 0)
                pe_layer2(pe, c, 1)
                pe_gated_turn(pe, i, buf0)
                pe_layer3(pe, c, 0, buf0)
                pe_layer3(pe, c, 1, buf0)
                pe_adapter_out(pe, i, buf0)
                pe_layer4(pe, c, 0)
                pe_layer4(pe, c, 1)
            f = NPAIR - 1
            pe_turn(pe, f, buf0, False)
            pe_scores_hidden(pe, f, buf0)
            pe_gated_turn(pe, f, buf0)
            pe_adapter_out(pe, f, buf0)

            setup_tensor(pe, 1, set1)
            pe.wait_ge(S.table_step, 2 * TABLE_STEPS)
            pe.wait_ge(S.quant_ready, 1)
            c = NPAIR
            for a in range(2):
                pe_layer1(pe, c, a)
            for a in range(2):
                pe_layer2(pe, c, a)
            for a in range(2):
                pe_layer3(pe, c, a, buf1)
            for a in range(2):
                pe_layer4(pe, c, a)
            with pe.Fori(NPAIR, 2 * NPAIR - 1) as i:
                c = i + 1
                pe_layer1(pe, c, 0)
                pe.wait_ge(S.rowsum_read, i - NPAIR + 1)
                pe_turn(pe, i, buf1, True)
                pe_layer1(pe, c, 1)
                pe_rowsum(pe, i, buf1)
                pe_quant(pe, i, 0, buf1)
                pe_layer2(pe, c, 0)
                pe_layer2(pe, c, 1)
                pe_quant(pe, i, 1, buf1)
                pe_layer3(pe, c, 0, buf1)
                pe_layer3(pe, c, 1, buf1)
                pe_layer4(pe, c, 0)
                pe_layer4(pe, c, 1)
            f = 2 * NPAIR - 1
            pe.wait_ge(S.rowsum_read, NPAIR)
            pe_turn(pe, f, buf1, True)
            pe_rowsum(pe, f, buf1)
            pe_quant(pe, f, 0, buf1)
            pe_quant(pe, f, 1, buf1)

        @block.scalar
        def _(act):
            setup_scalar(act, 0, set0)
            for g in range(len(GROUPS)):
                act.wait_ge(S.weights_turned, g + 1)
                if GROUPS[g] == ("b", 0, 0):
                    act.wait_ge(S.table_step, TABLE_STEPS)
                nc.scalar.activation(group_out((wr_hi, a_hi, b_hi), g), group_ps[g % 4][:, :], ACT.Identity).then_inc(S.weights_hi, 1)
            act.wait_ge(S.table_step, TABLE_STEPS)
            for a in range(2):
                act_layer1(act, 0, a, buf0)
            for a in range(2):
                act_layer2(act, 0, a, buf0)
            for a in range(2):
                act_layer3(act, 0, a, buf0)
            for a in range(2):
                act_layer4(act, 0, a, buf0)
            nc.scalar.preload_act_table(ACT.Exp)
            with act.Fori(0, NPAIR - 1) as i:
                c = i + 1
                act_turn(act, i, buf0)
                act_layer1(act, c, 0, buf0)
                act_layer1(act, c, 1, buf0)
                act_exp(act, i, buf0)
                act_layer2(act, c, 0, buf0)
                act_layer2(act, c, 1, buf0)
                act_gated_turn(act, i, buf0)
                act_layer3(act, c, 0, buf0)
                act_layer3(act, c, 1, buf0)
                act_layer4(act, c, 0, buf0)
                act_layer4(act, c, 1, buf0)
            f = NPAIR - 1
            act_turn(act, f, buf0)
            act_exp(act, f, buf0)
            act_gated_turn(act, f, buf0)

            setup_scalar(act, 1, set1)
            act.wait_ge(S.table_step, 2 * TABLE_STEPS)
            c = NPAIR
            for a in range(2):
                act_layer1(act, c, a, buf1)
            for a in range(2):
                act_layer2(act, c, a, buf1)
            for a in range(2):
                act_layer3(act, c, a, buf1)
            for a in range(2):
                act_layer4(act, c, a, buf1)
            nc.scalar.preload_act_table(ACT.Exp)
            with act.Fori(NPAIR, 2 * NPAIR - 1) as i:
                c = i + 1
                act_turn(act, i, buf1)
                act_layer1(act, c, 0, buf1)
                act_layer1(act, c, 1, buf1)
                act_layer2(act, c, 0, buf1)
                act_layer2(act, c, 1, buf1)
                act_layer3(act, c, 0, buf1)
                act_layer3(act, c, 1, buf1)
                act_layer4(act, c, 0, buf1)
                act_layer4(act, c, 1, buf1)
            act_turn(act, 2 * NPAIR - 1, buf1)

        @block.vector
        def _(v):
            v.sem_inc(S.x1_ready, 1)
            v.sem_inc(S.rowsum_read, 1)
            for a in range(2):
                nc.vector.memset(x_in[a][0:C, D:D + 1], 0.0)
                nc.vector.memset(x_in[a][C:P, 0:1], 0.0)
            setup_vector(v, 0, set0)
            for g in range(len(GROUPS)):
                v.wait_ge(S.weights_hi, g + 1)
                low(group_out((wr_lo, a_lo, b_lo), g), group_ps[g % 4][:, :], group_out((wr_hi, a_hi, b_hi), g)).then_inc(S.weights_lo, 1)

            def zero_ends(bufs):
                return dve_pads(v, bufs)

            zero_ends(buf0).then_inc(S.pads_ready, 1)
            v.wait_ge(S.pads_ready, 2)

            def conv_zeros(a):
                for w in (xz_hi[a], xz_lo[a]):
                    nc.vector.memset(w[C:P, 1, 0:1].bitcast(F32), 0.0)
                    nc.vector.memset(w[0:C, 1, H:H + 1].bitcast(F32), 0.0)

            def layer4_zeros(a):
                for w in (xz_hi[a], xz_lo[a]):
                    nc.vector.memset(w[:, 0, H:H + 1].bitcast(F32), 0.0)
                    nc.vector.memset(w[:, 1, 0:1].bitcast(F32), 0.0)

            def layer1(c, a):
                v.wait_ge(S.in2_hi, 2 * c + a + 1)
                conv_zeros(a)
                dve_layer1(v, c, a)

            def layer3(c, a):
                v.wait_ge(S.layer3_done, 4 * c + 2 * a + 1)
                layer4_zeros(a)
                dve_layer3(v, c, a)

            for a in range(2):
                dve_split(v, 0, a, buf0, True)
            for a in range(2):
                layer1(0, a)
            for a in range(2):
                dve_layer2(v, 0, a, buf0)
            for a in range(2):
                layer3(0, a)
            with v.Fori(0, NPAIR - 1) as i:
                c = i + 1
                dve_split(v, c, 0, buf0, False)
                dve_split(v, c, 1, buf0, False)
                dve_turn(v, i, buf0)
                layer1(c, 0)
                layer1(c, 1)
                dve_route(v, i, buf0)
                dve_gate(v, i, buf0)
                dve_layer2(v, c, 0, buf0)
                dve_layer2(v, c, 1, buf0)
                dve_gated_turn(v, i, buf0)
                layer3(c, 0)
                layer3(c, 1)
                dve_first_residual(v, i, buf0)
            f = NPAIR - 1
            dve_turn(v, f, buf0)
            dve_route(v, f, buf0)
            dve_gate(v, f, buf0)
            dve_gated_turn(v, f, buf0)
            dve_first_residual(v, f, buf0)

            v.wait_ge(S.x1_stored, 16 * NPAIR)
            setup_vector(v, 1, set1)
            nc.vector.memset(buf1.ones[:, :].bitcast(F32), 1.0)
            v.wait_ge(S.quant_loaded, 16)
            for k in range(KT):
                n = nibble[k % 2]
                nc.vector.tensor_scalar(n[:, :], packed[:, :], 4 * k, 15, ALU.logical_shift_right, ALU.bitwise_and).then_inc(S.fix_q, 1)
                v.wait_ge(S.fix_q, k + 1)
                last = nc.vector.tensor_copy(buf1.quant[:, k, :], n[:, :])
            last.then_inc(S.quant_ready, 1)
            zero_ends(buf1).then_inc(S.pads_ready, 1)
            v.wait_ge(S.pads_ready, 3)
            v.wait_ge(S.consts_loaded, 16 * 3)
            c = NPAIR
            for a in range(2):
                dve_split(v, c, a, buf1, False)
            for a in range(2):
                layer1(c, a)
            for a in range(2):
                dve_layer2(v, c, a, buf1)
            for a in range(2):
                layer3(c, a)
            with v.Fori(NPAIR, 2 * NPAIR - 1) as i:
                c = i + 1
                dve_split(v, c, 0, buf1, False)
                dve_split(v, c, 1, buf1, False)
                dve_turn(v, i, buf1)
                dve_rowsum(v, i, buf1)
                layer1(c, 0)
                layer1(c, 1)
                dve_layer2(v, c, 0, buf1)
                dve_layer2(v, c, 1, buf1)
                dve_second_residual(v, i, buf1)
                layer3(c, 0)
                layer3(c, 1)
            f = 2 * NPAIR - 1
            dve_turn(v, f, buf1)
            dve_rowsum(v, f, buf1)
            dve_second_residual(v, f, buf1)


def kernel(**inputs):
    import concourse.bacc as bacc
    from concourse.bass_utils import run_bass_kernel_spmd

    nc = bacc.Bacc("TRN2", target_bir_lowering=False, num_devices=1)
    arrays, tensors = {}, {}
    for name, value in inputs.items():
        a = np.ascontiguousarray(value)
        arrays[f"in_{name}"] = a
        tensors[name] = nc.dram_tensor(f"in_{name}", a.shape, mybir.dt.from_np(a.dtype), kind="ExternalInput").ap()
    tensors["out"] = nc.dram_tensor("out_x", (B, C, D), F32, kind="ExternalOutput").ap()
    program(nc, tensors)
    result = run_bass_kernel_spmd(nc, [arrays], core_ids=[0])
    return result.results[0]["out_x"]
```

```python
from contextlib import ExitStack

import numpy as np

import concourse.bass as bass
import concourse.mybir as mybir

F32 = mybir.dt.float32
F32R = mybir.dt.float32r
I32 = mybir.dt.int32
ALU = mybir.AluOpType
ACT = mybir.ActivationFunctionType
AX = mybir.AxisListType

class Buffers:
    pass


B, C, D = 32, 64, 1024
STYLE = 128
P = 128
NPAIR = B // 2
H = D // 2
DOWN_PAIRS, R_PAIRS, E_PAIRS = 3, 4, 4
NE, RANK = 64, 16
KR = NE * RANK
KT = D // P
TAPS = 3
LAYERS = 4
SCALE = 1.0 / float(np.sqrt(C * TAPS ** 2))
EPS = 1e-8
LORA_SCALE = 2.0
LOWEST = -3.0e38


def program(nc, t):
    with ExitStack() as outer:
        def sem(name):
            return outer.enter_context(nc.semaphore(name))

        def tensor(stack, name, shape, dt):
            return stack.enter_context(nc.sbuf_tensor(name, shape, dt))

        conv_ps = [outer.enter_context(nc.psum_tensor(f"conv_ps{i}", [P, 512], F32)) for i in range(2)]
        fold_ps = [outer.enter_context(nc.psum_tensor(f"fold_ps{i}", [P, 512], F32)) for i in range(2)]
        prod_ps = [outer.enter_context(nc.psum_tensor(f"prod_ps{i}", [P, 512], F32)) for i in range(2)]
        turn_ps = [outer.enter_context(nc.psum_tensor(f"turn_ps{i}", [P, 512], F32)) for i in range(2)]

        ident = tensor(outer, "ident", [P, P], F32)
        spread = tensor(outer, "spread", [P, 3, C], F32)
        eps_col = tensor(outer, "eps_col", [P, 1], F32)
        w1_hi, w1_lo = tensor(outer, "w1_hi", [P, 2, P], F32R), tensor(outer, "w1_lo", [P, 2, P], F32R)
        fold3_hi, fold3_lo = tensor(outer, "fold3_hi", [P, 2, P], F32R), tensor(outer, "fold3_lo", [P, 2, P], F32R)
        fold2_hi, fold2_lo = tensor(outer, "fold2_hi", [P, 5, P], F32R), tensor(outer, "fold2_lo", [P, 5, P], F32R)
        down_T = tensor(outer, "down_T", [P, DOWN_PAIRS, C], F32)
        style_tab = tensor(outer, "style_tab", [P, LAYERS, B], F32)
        demod_tab = tensor(outer, "demod_tab", [P, LAYERS, B], F32)
        bias_tab = tensor(outer, "bias_tab", [P, LAYERS], F32)
        scale1, bias1, scale2, scale3, bias4 = [tensor(outer, n, [P, B], F32) for n in ("scale1", "bias1", "scale2", "scale3", "bias4")]
        cond_edge = tensor(outer, "cond_edge", [P, 2, B], F32)
        x_in = [tensor(outer, f"x_in{a}", [P, D + 2], F32) for a in range(2)]

        x_scratch = nc.dram_tensor("x_after_first", [NPAIR, P, D], F32, kind="Internal").ap()

        S = Buffers()
        S.link = sem("link")
        S.small_loaded = sem("small_loaded")
        S.edges_clear = sem("edges_clear")
        S.edges_loaded = sem("edges_loaded")
        S.ident_ready = sem("ident_ready")
        S.style_turned = sem("style_turned")
        S.sums_ready = sem("sums_ready")
        S.sums_turned = sem("sums_turned")
        S.style_T_ready = sem("style_T_ready")
        S.style_done = sem("style_done")
        S.images_ready = sem("images_ready")
        S.images_turned = sem("images_turned")
        S.style_sq_ready = sem("style_sq_ready")
        S.squares_done = sem("squares_done")
        S.tables_ready = sem("tables_ready")
        S.inner_done = sem("inner_done")
        S.inner_ready = sem("inner_ready")
        S.tiles_hi = sem("tiles_hi")
        S.root_ready = sem("root_ready")
        S.tiles_ready = sem("tiles_ready")
        S.bias4_ready = sem("bias4_ready")
        S.edge_ready = sem("edge_ready")
        S.edge_done = sem("edge_done")
        S.edges_done = sem("edges_done")
        S.fold3_done = sem("fold3_done")
        S.fold_in_hi = sem("fold_in_hi")
        S.fold_in_ready = sem("fold_in_ready")
        S.fold3_ready = sem("fold3_ready")
        S.fold2_done = sem("fold2_done")
        S.fold3_hi = sem("fold3_hi")
        S.fold2_ready = sem("fold2_ready")
        S.fold2_lo = sem("fold2_lo")
        S.partial_scores = sem("partial_scores")
        S.parts_copied = sem("parts_copied")
        S.sums_reduced = sem("sums_reduced")
        S.cond_done = sem("cond_done")
        S.fold2_hi = sem("fold2_hi")
        S.xin_loaded0 = sem("xin_loaded0")
        S.xin_loaded1 = sem("xin_loaded1")
        S.layer1_done = sem("layer1_done")
        S.xin_hi = sem("xin_hi")
        S.xin_split = sem("xin_split")
        S.cond_ready = sem("cond_ready")
        S.layer1_scaled = sem("layer1_scaled")
        S.layer1_hi = sem("layer1_hi")
        S.layer1_ready = sem("layer1_ready")
        S.pads_ready = sem("pads_ready")
        S.turned = sem("turned")
        S.xt_hi = sem("xt_hi")
        S.xt_ready = sem("xt_ready")
        S.scored = sem("scored")
        S.x1_ready = sem("x1_ready")
        S.hidden_done = sem("hidden_done")
        S.gated = sem("gated")
        S.gated_turned = sem("gated_turned")
        S.hgt_ready = sem("hgt_ready")
        S.out_done = sem("out_done")
        S.top_max = sem("top_max")
        S.exp_ready = sem("exp_ready")
        S.hgt_hi = sem("hgt_hi")
        S.tail = sem("tail")
        S.res_loaded = sem("res_loaded")
        S.rowsum_done = sem("rowsum_done")
        S.rowsum_read = sem("rowsum_read")
        S.biased = sem("biased")
        S.y_ready = sem("y_ready")
        S.weights_lo = sem("weights_lo")
        S.router_loaded = sem("router_loaded")
        S.weights_turned = sem("weights_turned")
        S.x1_stored = sem("x1_stored")
        S.quant_loaded = sem("quant_loaded")
        S.consts_loaded = sem("consts_loaded")
        S.ident_clear = sem("ident_clear")
        S.spread_ready = sem("spread_ready")
        S.y_stored = sem("y_stored")
        S.quant_ready = sem("quant_ready")
        S.weights_hi = sem("weights_hi")
        S.nibble_ready = sem("nibble_ready")
        S.a_loaded = [sem(f"a_loaded{i}") for i in range(3)]
        S.b_loaded = [sem(f"b_loaded{i}") for i in range(3)]

        x_pairs = t["x"].rearrange("(p two) c d -> p (two c) d", two=2)
        out_pairs = t["out"].rearrange("(p two) c d -> p (two c) d", two=2)

        def low(out, whole, hi):
            return nc.vector.tensor_tensor(out, whole, hi.bitcast(F32), ALU.subtract)

        link_count = [0]

        def link(v, ins):
            link_count[0] += 1
            ins.then_inc(S.link, 1)
            v.wait_ge(S.link, link_count[0])

        def products(out, stationary, hi, lo, moving_hi, moving_lo):
            n = len(stationary)
            for i, w in enumerate(stationary):
                nc.tensor.matmul(out, hi[:, w, :], moving_hi(i), start=(i == 0), stop=False)
                nc.tensor.matmul(out, hi[:, w, :], moving_lo(i), start=False, stop=False)
                last = nc.tensor.matmul(out, lo[:, w, :], moving_hi(i), start=False, stop=(i == n - 1))
            return last

        def setup_buffers(stack, L):
            T = lambda n, s, d=F32: tensor(stack, f"L{L}_{n}", s, d)
            s = Buffers()
            s.level = L
            s.style, s.style_T = T("style", [B, STYLE]), T("style_T", [STYLE, B])
            s.mod_w, s.mod_wT, s.mod_b = T("mod_w", [C, LAYERS, STYLE]), T("mod_wT", [STYLE, LAYERS, 2, C]), T("mod_b", [P, LAYERS])
            s.w, s.wsq, s.wsum = T("w", [P, LAYERS, C * TAPS]), T("wsq", [C, LAYERS, C * TAPS]), T("wsum", [C, LAYERS + 2, C])
            s.wsum_T, s.style_sq = T("wsum_T", [C, LAYERS + 2, 2, C]), T("style_sq", [P, LAYERS, B])
            s.same, s.down, s.up = [T(f"same{i}", [C, 5, C]) for i in range(2)], T("down", [C, 10, C]), T("up", [P, 10, C])
            s.same3 = T("same3", [P, 4, C])
            s.blur, s.blur_d = [T(f"blur{i}", [P, 7 - i, C]) for i in range(2)], [T(f"blur_d{i}", [C, 7 - i, C]) for i in range(2)]
            s.blur, s.blur_d = s.blur + s.blur[0:1], s.blur_d + s.blur_d[0:1]
            s.var, s.root, s.newton = T("var", [P, LAYERS * B]), T("root", [P, LAYERS * B]), T("newton", [P, LAYERS * B])
            s.bias2, s.edge2, s.bias3, s.inner = T("bias2", [P, B]), T("edge2", [P, B]), T("bias3", [P, B]), T("inner", [P, B])
            s.w_hi, s.w_lo = T("w_hi", [P, 10, P], F32R), T("w_lo", [P, 10, P], F32R)
            s.x_edge = T("x_edge", [P, 2, B, 10])
            s.edge, s.edge_hi, s.edge_lo = [None] * 4, [None] * 4, [None] * 4
            for i in range(2):
                n = 4 - i
                s.edge[i], s.edge_hi[i], s.edge_lo[i] = T(f"side{i}", [P, 2, n, B]), T(f"side_hi{i}", [P, 2, n, B], F32R), T(f"side_lo{i}", [P, 2, n, B], F32R)
                s.edge[i + 2], s.edge_hi[i + 2], s.edge_lo[i + 2] = s.edge[i], s.edge_hi[i], s.edge_lo[i]
            s.scaled = T("side_scaled", [P, 2, 3, B])
            return s

        SMALL = 9 * 16
        EDGES = 4 * 16

        def setup_loads(sp, L, s):
            g = lambda n: t[f"L{L}_cond_{n}"]
            w = g("weights").rearrange("l o i k -> o l (i k)")
            with nc.allow_non_contiguous_dma(reason="a few hundred words"):
                for dst, src in (
                        (s.style[:, :], t["cond_512"]), (s.mod_w[:, :, :], g("mod_w").rearrange("l i k -> i l k")),
                        (s.mod_b[0:C], g("mod_b").rearrange("l i -> i l")), (s.mod_b[C:P], g("mod_b").rearrange("l i -> i l")),
                        (s.w[0:C], w), (s.w[C:P, 1:3], w[:, 1:3]),
                        (bias_tab[0:C], g("biases").rearrange("l i -> i l")), (bias_tab[C:P], g("biases").rearrange("l i -> i l"))):
                    sp.dma_start(dst, src).then_inc(S.small_loaded, 16)
                sp.dma_start(s.w[C:P, 0], w[:, 0]).then_inc(S.small_loaded, 16)

        def edge_loads(sp, L, s):
            src = (t["x"].rearrange("b c d -> c b d") if L == 0 else x_scratch.rearrange("p (two c) d -> c (p two) d", two=2))
            sp.wait_ge(S.edges_clear, L + 1)
            with nc.allow_non_contiguous_dma(reason="8 words of each row"):
                sp.dma_start(s.x_edge[0:C, 0, :, 0:8], src[:, :, 0:8]).then_inc(S.edges_loaded, 16)
                sp.dma_start(s.x_edge[C:P, 0, :, 1:9], src[:, :, 0:8]).then_inc(S.edges_loaded, 16)
                sp.dma_start(s.x_edge[0:C, 1, :, 0:6], src[:, :, D - 6:D]).then_inc(S.edges_loaded, 16)
                sp.dma_start(s.x_edge[C:P, 1, :, 0:7], src[:, :, D - 7:D]).then_inc(S.edges_loaded, 16)

        def setup_tensor(pe, L, s):
            n = L + 1
            pe.wait_ge(S.ident_ready, 2)
            pe.wait_ge(S.small_loaded, SMALL * n)
            nc.tensor.transpose(turn_ps[0][:, 0:B], s.style[:, :], ident[0:B, 0:B])
            for l in range(LAYERS):
                last = nc.tensor.transpose(turn_ps[1][:, l * C:(l + 1) * C], s.mod_w[:, l, :], ident[0:C, 0:C])
            last.then_inc(S.style_turned, 1)
            pe.wait_ge(S.sums_ready, n)
            for l in range(LAYERS + 2):
                last = nc.tensor.transpose(prod_ps[0][0:C, l * C:(l + 1) * C], s.wsum[:, l, :], ident[0:C, 0:C])
            last.then_inc(S.sums_turned, 1)
            pe.wait_ge(S.style_T_ready, n)
            for l in range(LAYERS):
                last = nc.tensor.matmul(turn_ps[0][:, 64 + l * B:64 + (l + 1) * B], s.mod_wT[:, l].rearrange("k two i -> k (two i)"),
                                        s.style_T[:, :], start=True, stop=True)
            last.then_inc(S.style_done, 1)
            pe.wait_ge(S.images_ready, n)
            for q in range(2):
                for f in range(2):
                    j = 2 - 2 * q + f
                    for i, ps in enumerate((conv_ps[0][:, 0:2 * P], conv_ps[0][:, 2 * P:4 * P])):
                        nc.tensor.transpose(ps[:, q * P + f * C:q * P + (f + 1) * C],
                                            s.same[i][:, j:j + 2, :].rearrange("o j i -> o (j i)"), ident[0:C, 0:C])
            for q in range(4):
                for f in range(2):
                    j = 2 + 2 * q - 2 * f
                    nc.tensor.transpose(fold_ps[0][:, q * P + f * C:q * P + (f + 1) * C],
                                        s.down[:, j:j + 2, :].rearrange("o j i -> o (j i)"), ident[0:C, 0:C])
            for q in range(5):
                out = conv_ps[1][:, q * P:(q + 1) * P] if q < 4 else fold_ps[1][:, 2 * P:3 * P]
                for f, j in enumerate((max(2 * q - 1, 0), min(2 * q + 1, 8))):
                    nc.tensor.transpose(out[:, f * C:(f + 1) * C], s.up[0:C, j:j + 2, :].rearrange("o j i -> o (j i)"), ident[0:C, 0:C])
            for q in range(DOWN_PAIRS):
                j = 2 + 2 * (DOWN_PAIRS - 1 - q)
                last = nc.tensor.transpose(fold_ps[1][:, q * C:(q + 1) * C], s.down[:, j:j + 2, :].rearrange("o j i -> o (j i)"), ident[0:C, 0:C])
            last.then_inc(S.images_turned, 1)
            pe.wait_ge(S.style_sq_ready, n)
            for l in range(LAYERS):
                last = nc.tensor.matmul(turn_ps[0][:, 256 + l * B:256 + (l + 1) * B], s.wsum_T[:, l].rearrange("i two o -> i (two o)"),
                                        s.style_sq[0:C, l, :], start=True, stop=True)
            last.then_inc(S.squares_done, 1)

        def inner_tensor(pe, L, s):
            n = L + 1
            pe.wait_ge(S.tables_ready, n)
            nc.tensor.matmul(turn_ps[1][:, 0:B], s.wsum_T[:, LAYERS].rearrange("i two o -> i (two o)"), s.bias2[0:C, :],
                             start=True, stop=True).then_inc(S.inner_done, 1)
            pe.wait_ge(S.inner_ready, n)
            nc.tensor.matmul(turn_ps[1][:, B:2 * B], s.wsum_T[:, LAYERS + 1].rearrange("i two o -> i (two o)"), s.inner[0:C, :],
                             start=True, stop=True).then_inc(S.inner_done, 1)

        UP_PARTS = [(6, slice(0, 2), slice(4, 8, 3)), (7, slice(0, 2), slice(0, 4, 3)),
                    (8, slice(0, 1), slice(6, 7)), (8, slice(1, 2), slice(5, 6)),
                    (9, slice(0, 1), slice(2, 3)), (9, slice(1, 2), slice(1, 2))]

        def up_part(w, i):
            tile, halves, _ = UP_PARTS[i]
            return w[:, tile, :].rearrange("p (f o) -> p f o", f=2)[:, halves, :]

        def turned_parts(s, hi):
            flat = lambda w: w.rearrange("p q m -> p (q m)")
            w1, f2, f3, w = (w1_hi, fold2_hi, fold3_hi, s.w_hi) if hi else (w1_lo, fold2_lo, fold3_lo, s.w_lo)
            pairs = [(flat(w1[:, :, :]), conv_ps[0][:, 0:2 * P]), (flat(f2[:, 0:4, :]), conv_ps[1][:, :]), (f2[:, 4, :], fold_ps[1][:, 2 * P:3 * P]),
                     (flat(f3[:, :, :]), s.same3[:, :, :].rearrange("p j i -> p (j i)")),
                     (flat(w[:, 0:2, :]), conv_ps[0][:, 2 * P:4 * P]), (flat(w[:, 2:6, :]), fold_ps[0][:, :])]
            return pairs + [(up_part(w, i), s.up[:, UP_PARTS[i][2], :]) for i in range(len(UP_PARTS))]

        def setup_scalar(act, L, s):
            n = L + 1
            act.wait_ge(S.images_ready, n)
            act.wait_ge(S.images_turned, n)
            for out, whole in turned_parts(s, True):
                last = nc.scalar.activation(out, whole, ACT.Identity)
            last.then_inc(S.tiles_hi, 1)
            act.wait_ge(S.squares_done, n)
            act.wait_ge(S.ident_ready, 2)
            nc.scalar.activation(s.root[:, :], turn_ps[0][:, 256:256 + LAYERS * B], ACT.Sqrt, bias=eps_col[:, 0:1],
                                 scale=SCALE * SCALE).then_inc(S.root_ready, 1)

        def setup_vector(v, L, s):
            n = L + 1
            V = nc.vector
            for b in [s.same[0], s.same[1], s.down, s.up, s.same3] + s.blur[0:2] + s.blur_d[0:2] + s.edge[0:2]:
                V.memset(b[:, :, :], 0.0) if len(b.shape) == 3 else V.memset(b[:, :, :, :], 0.0)
            V.memset(s.x_edge[:, :, :, :], 0.0).then_inc(S.edges_clear, 1)
            v.wait_ge(S.edges_clear, n)
            v.wait_ge(S.small_loaded, SMALL * n)
            link(v, V.tensor_tensor(s.wsq[:, :, :], s.w[0:C], s.w[0:C], ALU.mult))
            taps_inside = lambda ap: ap.rearrange("o l (i k) -> o (l i) k", k=TAPS)
            V.tensor_reduce(s.wsum[:, 0:LAYERS, :].rearrange("o l i -> o (l i)"), taps_inside(s.wsq[:, :, :]), AX.X, ALU.add)
            V.tensor_reduce(s.wsum[:, LAYERS:, :].rearrange("o l i -> o (l i)"), taps_inside(s.w[0:C, 2:4]), AX.X, ALU.add).then_inc(S.sums_ready, 1)
            v.wait_ge(S.style_turned, n)
            V.tensor_copy(s.style_T[:, :], turn_ps[0][:, 0:B])
            for half in range(2):
                last = V.tensor_copy(s.mod_wT[:, :, half, :], turn_ps[1][:, 0:LAYERS * C].rearrange("k (l i) -> k l i", l=LAYERS))
            last.then_inc(S.style_T_ready, 1)
            taps = lambda l, k, rows=slice(0, C): s.w[rows, l, :].rearrange("o (i k) -> o k i", k=TAPS)[:, k, :]
            for i, l in ((0, 0), (1, 2)):
                for k in range(TAPS):
                    V.tensor_scalar(s.same[i][:, 3 - k, :], taps(l, k), SCALE, None, ALU.mult)
            for k in range(TAPS):
                V.tensor_scalar(s.same3[0:C, k, :], taps(2, k), SCALE, None, ALU.mult)
                V.tensor_scalar(s.same3[C:P, k + 1, :], taps(2, k, slice(C, P)), SCALE, None, ALU.mult)
                V.tensor_scalar(s.blur_d[0][:, 1 + k, :], taps(3, k), SCALE / 8, None, ALU.mult)
                last = V.tensor_scalar(s.blur[0][:, 1 + k, :], taps(1, k, slice(0, P)), SCALE / 4, None, ALU.mult)
            link(v, last)
            for i in range(2):
                V.tensor_tensor(s.blur_d[i + 1][:, 1:5 + i, :], s.blur_d[i][:, 1:5 + i, :], s.blur_d[i][:, 0:4 + i, :], ALU.add)
                link(v, V.tensor_tensor(s.blur[i + 1][:, 1:5 + i, :], s.blur[i][:, 1:5 + i, :], s.blur[i][:, 0:4 + i, :], ALU.add))
            V.tensor_tensor(s.down[:, 2:8, :], s.blur_d[2][:, 1:7, :], s.blur_d[2][:, 0:6, :], ALU.add)
            V.tensor_tensor(s.up[0:C, 2:8, :], s.blur[2][0:C, 1:7, :], s.blur[2][0:C, 0:6, :], ALU.add)
            V.tensor_tensor(s.up[C:P, 0:6, :], s.blur[2][C:P, 1:7, :], s.blur[2][C:P, 0:6, :], ALU.add).then_inc(S.images_ready, 1)
            v.wait_ge(S.sums_turned, n)
            src = prod_ps[0][0:C, 0:(LAYERS + 2) * C].rearrange("i (l o) -> i l o", l=LAYERS + 2)
            V.tensor_copy(s.wsum_T[:, :, 0, :], src)
            V.tensor_copy(s.wsum_T[:, :, 1, :], src)
            v.wait_ge(S.style_done, n)
            for l in range(LAYERS):
                last = V.tensor_scalar(style_tab[:, l, :], turn_ps[0][:, 64 + l * B:64 + (l + 1) * B], s.mod_b[:, l:l + 1], None, ALU.add)
            link(v, last)
            V.tensor_tensor(s.style_sq[:, :, :], style_tab[:, :, :], style_tab[:, :, :], ALU.mult).then_inc(S.style_sq_ready, 1)
            v.wait_ge(S.tiles_hi, n)
            V.tensor_copy(down_T[:, :, :].rearrange("p q i -> p (q i)"), fold_ps[1][:, 0:DOWN_PAIRS * C])
            for (out, whole), (hi, _) in zip(turned_parts(s, False), turned_parts(s, True)):
                last = low(out, whole, hi)
            last.then_inc(S.tiles_ready, 1)
            v.wait_ge(S.root_ready, n)
            demod = demod_tab[:, :, :].rearrange("o l b -> o (l b)")
            V.tensor_scalar(s.var[:, :], turn_ps[0][:, 256:256 + LAYERS * B], SCALE * SCALE, EPS, ALU.mult, ALU.add)
            link(v, V.reciprocal(demod, s.root[:, :]))
            link(v, V.tensor_tensor(s.newton[:, :], demod, demod, ALU.mult))
            link(v, V.tensor_tensor(s.newton[:, :], s.newton[:, :], s.var[:, :], ALU.mult))
            link(v, V.tensor_scalar(s.newton[:, :], s.newton[:, :], -0.5, 1.5, ALU.mult, ALU.add))
            link(v, V.tensor_tensor(demod, demod, s.newton[:, :], ALU.mult))
            st, de = (lambda l: style_tab[:, l, :]), (lambda l: demod_tab[:, l, :])
            bi = lambda l: bias_tab[:, l:l + 1]
            V.tensor_tensor(scale1[:, :], de(0), de(1), ALU.mult)
            V.tensor_scalar(bias1[:, :], de(1), bi(0), None, ALU.mult)
            V.tensor_tensor(scale2[:, :], st(1), st(2), ALU.mult)
            V.tensor_scalar(s.bias2[:, :], st(2), bi(1), 2.0, ALU.mult, ALU.mult)
            V.tensor_scalar(s.edge2[:, :], st(2), bi(1), -0.25, ALU.mult, ALU.mult)
            V.tensor_tensor(scale3[:, :], de(2), st(3), ALU.mult)
            V.tensor_scalar(s.bias3[:, :], st(3), bi(2), None, ALU.mult).then_inc(S.tables_ready, 1)
            v.wait_ge(S.tables_ready, n)

        def inner_vector(v, L, s):
            V = nc.vector
            v.wait_ge(S.inner_done, 2 * L + 1)
            link(v, V.tensor_tensor(s.inner[:, :], turn_ps[1][:, 0:B], scale3[:, :], ALU.mult))
            V.scalar_tensor_tensor(out=s.inner[:, :], in0=s.inner[:, :], scalar=SCALE, in1=s.bias3[:, :], op0=ALU.mult, op1=ALU.add).then_inc(S.inner_ready, 1)
            v.wait_ge(S.inner_done, 2 * L + 2)
            link(v, V.scalar_tensor_tensor(out=bias4[:, :], in0=turn_ps[1][:, B:2 * B], scalar=SCALE, in1=demod_tab[:, 3, :], op0=ALU.mult, op1=ALU.mult))
            V.tensor_scalar(bias4[:, :], bias4[:, :], bias_tab[:, 3:4], None, ALU.add).then_inc(S.bias4_ready, 1)

        def edge_tensor(pe, L, s):
            n = L + 1
            flat = lambda ap: ap.rearrange("p s j b -> p s (j b)")
            part = lambda w, k: (lambda i: flat(w[k][:, :, i:i + 3, :]))
            sides = lambda ps, j: ps[:, 0:2 * j * B].rearrange("p (s j) -> p s j", s=2)
            pe.wait_ge(S.tiles_ready, n)
            pe.wait_ge(S.edge_ready, 4 * L + 1)
            products(sides(prod_ps[0], 3), (0, 1), w1_hi, w1_lo, part(s.edge_hi, 0), part(s.edge_lo, 0)).then_inc(S.edge_done, 1)
            pe.wait_ge(S.edge_ready, 4 * L + 2)
            two = lambda w: (lambda i: flat(w[1][:, :, i:i + 2, :]))
            for m in range(2):
                last = products(sides(prod_ps[m], 2), (6 + 2 * m, 7 + 2 * m), s.w_hi, s.w_lo, two(s.edge_hi), two(s.edge_lo))
            last.then_inc(S.edge_done, 1)
            pe.wait_ge(S.edge_ready, 4 * L + 3)
            products(sides(prod_ps[0], 3), (0, 1), s.w_hi, s.w_lo, part(s.edge_hi, 2), part(s.edge_lo, 2)).then_inc(S.edge_done, 1)
            pe.wait_ge(S.edge_ready, 4 * L + 4)
            for side in range(2):
                one = lambda w: (lambda i: w[3][:, side, i, :])
                last = products(prod_ps[1][:, side * B:(side + 1) * B], (3 - side, 4 - side, 5 - side), s.w_hi, s.w_lo, one(s.edge_hi), one(s.edge_lo))
            last.then_inc(S.edge_done, 1)

        def edge_vector(v, L, s):
            V = nc.vector
            lo_half, hi_half = slice(0, C), slice(C, P)

            def wide(tab, like, rows=slice(0, P)):
                return tab[rows, :].unsqueeze(1).broadcast_to([rows.stop - rows.start, like, B])

            def parts(k):
                everything = lambda w: w[k][:, :, :, :].rearrange("p s j b -> p (s j b)")
                link(v, V.tensor_copy(everything(s.edge_hi), everything(s.edge)))
                low(everything(s.edge_lo), everything(s.edge), everything(s.edge_hi)).then_inc(S.edge_ready, 1)

            v.wait_ge(S.edges_loaded, EDGES * (L + 1))
            for side in range(2):
                last = V.tensor_tensor(s.edge[0][:, side, :, :], s.x_edge[:, side, :, 0:8].rearrange("p b (j two) -> p j two b", two=2)[:, :, 0, :],
                                       wide(style_tab[:, 0, :], 4), ALU.mult)
            link(v, last)
            parts(0)
            v.wait_ge(S.edge_done, 4 * L + 1)
            link(v, V.tensor_tensor(s.scaled[:, :, :, :].rearrange("p s j b -> p (s j) b"), prod_ps[0][:, 0:6 * B].rearrange("p (j b) -> p j b", b=B),
                                    wide(scale1, 6), ALU.mult))
            for side, rows, src, dst in ((0, lo_half, slice(0, 3), slice(0, 3)), (0, hi_half, slice(0, 2), slice(1, 3)),
                                         (1, lo_half, slice(1, 3), slice(0, 2)), (1, hi_half, slice(0, 3), slice(0, 3))):
                last = V.tensor_tensor(s.edge[1][rows, side, dst, :], s.scaled[rows, side, src, :], wide(bias1, src.stop - src.start, rows), ALU.add)
            link(v, last)
            parts(1)
            v.wait_ge(S.edge_done, 4 * L + 2)
            link(v, V.memset(s.edge[2][:, :, :, :], 0.0))
            for m in range(2):
                four = s.scaled[:, :, 0:2, :]
                for side in range(2):
                    last = V.tensor_tensor(four[:, side, :, :], prod_ps[m][:, side * 2 * B:(side + 1) * 2 * B].rearrange("p (j b) -> p j b", b=B), wide(scale2, 2), ALU.mult)
                link(v, last)
                moves = [((0, lo_half, slice(0, 2), slice(0, 3, 2)), (0, hi_half, slice(0, 1), slice(2, 3)),
                          (1, lo_half, slice(1, 2), slice(1, 2)), (1, hi_half, slice(0, 2), slice(1, 4, 2))),
                         ((0, slice(0, P), slice(0, 2), slice(1, 4, 2)), (1, slice(0, P), slice(0, 2), slice(0, 3, 2)))][m]
                for side, rows, src, dst in moves:
                    last = V.tensor_tensor(s.edge[2][rows, side, dst, :], s.scaled[rows, side, src, :], wide(s.bias2, src.stop - src.start, rows), ALU.add)
                link(v, last)
            V.tensor_tensor(s.edge[2][lo_half, 0, 0, :], s.edge[2][lo_half, 0, 0, :], s.edge2[lo_half, :], ALU.add)
            link(v, V.tensor_tensor(s.edge[2][hi_half, 1, 3, :], s.edge[2][hi_half, 1, 3, :], s.edge2[hi_half, :], ALU.add))
            parts(2)
            v.wait_ge(S.edge_done, 4 * L + 3)
            six = lambda ap: ap[:, :, :, :].rearrange("p s j b -> p (s j) b")
            link(v, V.tensor_tensor(six(s.scaled), prod_ps[0][:, 0:6 * B].rearrange("p (j b) -> p j b", b=B), wide(scale3, 6), ALU.mult))
            link(v, V.tensor_tensor(six(s.edge[3]), six(s.scaled), wide(s.bias3, 6), ALU.add))
            parts(3)
            v.wait_ge(S.edge_done, 4 * L + 4)
            link(v, V.tensor_tensor(cond_edge[:, :, :], prod_ps[1][:, 0:2 * B].rearrange("p (s b) -> p s b", s=2), wide(demod_tab[:, 3, :], 2), ALU.mult))
            V.tensor_scalar(cond_edge[:, :, :], cond_edge[:, :, :], bias_tab[:, 3:4], None, ALU.add).then_inc(S.edges_done, 1)

        def at(tab, c, a, bufs):
            n = 2 * c + a - bufs.first_sample
            return tab[:, n:n + 1] if isinstance(n, int) else tab[:, bass.ds(n, 1)]

        def conv_buffers(stack, L):
            T = lambda n, s, d=F32R: tensor(stack, f"L{L}_{n}", s, d)
            b = Buffers()
            b.first_sample = B * L
            b.x_hi, b.x_lo = [T(f"x_hi{a}", [P, H + 1]) for a in range(2)], [T(f"x_lo{a}", [P, H + 1]) for a in range(2)]
            b.h_hi, b.h_lo = [T(f"h_hi{a}", [P, H + 3]) for a in range(2)], [T(f"h_lo{a}", [P, H + 3]) for a in range(2)]
            b.v_hi, b.v_lo = T("v_hi", [P, DOWN_PAIRS, 2, C]), T("v_lo", [P, DOWN_PAIRS, 2, C])
            b.r_hi, b.r_lo = T("r_hi", [P, R_PAIRS, 2, C]), T("r_lo", [P, R_PAIRS, 2, C])
            b.e_hi, b.e_lo = T("e_hi", [P, E_PAIRS, 2, P]), T("e_lo", [P, E_PAIRS, 2, P])
            return b

        def act_fold_start(act, c, bufs, first=False):
            if not first:
                act.wait_ge(S.fold3_done, c)
                act.nop(nofuse=True)
            for a in range(2):
                nc.scalar.activation(bufs.v_hi[:, :, a, :], down_T[:, :, :], ACT.Identity, scale=at(scale3, c, a, bufs)).then_inc(S.fold_in_hi, 1)

        def dve_fold_start(v, c, bufs):
            for a in range(2):
                v.wait_ge(S.fold_in_hi, 2 * c + a + 1)
                nc.vector.scalar_tensor_tensor(out=bufs.v_lo[:, :, a, :], in0=down_T[:, :, :], scalar=at(scale3, c, a, bufs),
                                               in1=bufs.v_hi[:, :, a, :].bitcast(F32), op0=ALU.mult, op1=ALU.subtract).then_inc(S.fold_in_ready, 1)

        def pe_fold3(pe, c, bufs, first=False):
            pe.wait_ge(S.fold_in_ready, 2 * c + 2)
            if not first:
                pe.wait_ge(S.fold3_ready, 2 * c)
            flat = lambda w: w[:, :, :, :].rearrange("p q a i -> p (q a i)")
            hi, lo = flat(bufs.v_hi), flat(bufs.v_lo)
            for n, first_block in enumerate((1, 0)):
                out = fold_ps[0][:, first_block * P:(first_block + DOWN_PAIRS) * P]
                for i, (w, v) in enumerate(((fold3_hi, hi), (fold3_hi, lo), (fold3_lo, hi))):
                    last = nc.tensor.matmul(out, w[:, n, :], v, start=(n == 0 and i == 0), stop=(n == 1 and i == 2), skip_group_check=True)
            last.then_inc(S.fold3_done, 1)

        def fold3_out(a):
            return fold_ps[0][:, :].rearrange("p (m a i) -> p m a i", m=R_PAIRS, a=2)[:, :, a, :]

        def act_fold3(act, c, bufs, first=False):
            act.wait_ge(S.fold3_done, c + 1)
            if not first:
                act.wait_ge(S.fold2_done, c)
            act.nop(nofuse=True)
            for a in range(2):
                nc.scalar.activation(bufs.r_hi[:, :, a, :], fold3_out(a), ACT.Identity, scale=at(scale2, c, a, bufs)).then_inc(S.fold3_hi, 1)

        def dve_fold3(v, c, bufs):
            v.wait_ge(S.fold3_hi, 2 * c + 2)
            for a in range(2):
                nc.vector.scalar_tensor_tensor(out=bufs.r_lo[:, :, a, :], in0=fold3_out(a), scalar=at(scale2, c, a, bufs),
                                               in1=bufs.r_hi[:, :, a, :].bitcast(F32), op0=ALU.mult, op1=ALU.subtract).then_inc(S.fold3_ready, 1)

        FOLD2 = [(0, 0, 0), (2, 0, 1), (4, 0, 2), (1, 1, 1), (3, 1, 2)]

        def pe_fold2(pe, c, bufs, first=False):
            pe.wait_ge(S.fold3_ready, 2 * c + 2)
            if not first:
                pe.wait_ge(S.fold2_hi, 2 * c)
                pe.wait_ge(S.fold2_ready, c)
            for n, (tile, m, block) in enumerate(FOLD2):
                out = fold_ps[1][:, block * P:(block + 2) * P]
                for i, (w, r) in enumerate(((fold2_hi, bufs.r_hi), (fold2_hi, bufs.r_lo), (fold2_lo, bufs.r_hi))):
                    last = nc.tensor.matmul(out, w[:, tile, :], r[:, m:R_PAIRS:2, :, :], start=(n == 0 and i == 0),
                                            stop=(n == len(FOLD2) - 1 and i == 2), skip_group_check=True)
            last.then_inc(S.fold2_done, 1)

        def act_fold2(act, c, bufs, first=False):
            act.wait_ge(S.fold2_done, c + 1)
            if not first:
                act.wait_ge(S.cond_done, 2 * c)
            flat = lambda ap: ap.rearrange("p q a m -> p (q a) m")
            blocks = fold_ps[1][:, :].rearrange("p (q o) -> p q o", o=C)
            hi = bufs.e_hi
            nc.scalar.activation(flat(hi[:, :, :, 0:C]), blocks, ACT.Identity).then_inc(S.fold2_hi, 1)
            act.wait_ge(S.fold2_hi, 2 * c + 1)
            nc.scalar.activation(flat(hi[0:C, :, :, C:P]), flat(hi[C:P, :, :, 0:C]).bitcast(F32), ACT.Identity)
            nc.scalar.activation(flat(hi[C:P, 0:E_PAIRS - 1, :, C:P]), flat(hi[0:C, 1:E_PAIRS, :, 0:C]).bitcast(F32), ACT.Identity).then_inc(S.fold2_hi, 1)

        def dve_fold2(v, c, bufs):
            flat = lambda ap: ap.rearrange("p q a m -> p (q a) m")
            blocks = fold_ps[1][:, :].rearrange("p (q o) -> p q o", o=C)
            v.wait_ge(S.fold2_hi, 2 * c + 1)
            lo = bufs.e_lo
            low(flat(lo[:, :, :, 0:C]), blocks, flat(bufs.e_hi[:, :, :, 0:C])).then_inc(S.fold2_lo, 1)
            v.wait_ge(S.fold2_lo, c + 1)
            nc.vector.tensor_copy(flat(lo[0:C, :, :, C:P]), flat(lo[C:P, :, :, 0:C]).bitcast(F32))
            nc.vector.tensor_copy(flat(lo[C:P, 0:E_PAIRS - 1, :, C:P]), flat(lo[0:C, 1:E_PAIRS, :, 0:C]).bitcast(F32)).then_inc(S.fold2_ready, 1)

        def dve_split(v, c, a, bufs, first=False):
            v.wait_ge((S.xin_loaded0, S.xin_loaded1)[a], 32 * (c + 1))
            if not first:
                v.wait_ge(S.layer1_done, 2 * c + a - 1)
            src = x_in[a][:, 0:D + 2].rearrange("p (j two) -> p two j", two=2)[:, 0, :]
            sc = at(style_tab[:, 0, :], c, a, bufs)
            nc.vector.tensor_scalar(bufs.x_hi[a][:, :], src, sc, None, ALU.mult).then_inc(S.xin_hi, 1)
            v.wait_ge(S.xin_hi, 2 * c + a + 1)
            nc.vector.scalar_tensor_tensor(out=bufs.x_lo[a][:, :], in0=src, scalar=sc, in1=bufs.x_hi[a][:, :].bitcast(F32),
                                           op0=ALU.mult, op1=ALU.subtract).then_inc(S.xin_split, 1)

        def pe_layer1(pe, c, a, bufs, first=False):
            pe.wait_ge(S.xin_split, 2 * c + a + 1)
            if not first:
                pe.wait_ge(S.cond_ready, 2 * c + a - 1)
            cut = lambda w: (lambda i: w[a][:, i:i + H])
            products(conv_ps[a][:, :], (0, 1), w1_hi, w1_lo, cut(bufs.x_hi), cut(bufs.x_lo)).then_inc(S.layer1_done, 1)

        def act_layer1(act, c, a, bufs):
            act.wait_ge(S.layer1_done, 2 * c + a + 1)
            act.nop(nofuse=True)
            ps, hi = conv_ps[a], bufs.h_hi[a]
            nc.scalar.activation(ps[:, :], ps[:, :], ACT.Identity, bias=at(bias1, c, a, bufs), scale=at(scale1, c, a, bufs)).then_inc(S.layer1_scaled, 1)
            act.wait_ge(S.layer1_scaled, 2 * c + a + 1)
            nc.scalar.activation(hi[0:C, 1:H + 1], ps[0:C, :], ACT.Identity)
            nc.scalar.activation(hi[C:P, 2:H + 2], ps[C:P, :], ACT.Identity).then_inc(S.layer1_hi, 1)

        def dve_layer1(v, c, a, bufs):
            v.wait_ge(S.layer1_hi, 2 * c + a + 1)
            low(bufs.h_lo[a][0:C, 1:H + 1], conv_ps[a][0:C, :], bufs.h_hi[a][0:C, 1:H + 1])
            low(bufs.h_lo[a][C:P, 2:H + 2], conv_ps[a][C:P, :], bufs.h_hi[a][C:P, 2:H + 2]).then_inc(S.layer1_ready, 1)

        def pe_cond(pe, c, a, bufs):
            if a == 0:
                pe.wait_ge(S.fold2_hi, 2 * c + 2)
                pe.wait_ge(S.fold2_ready, c + 1)
            pe.wait_ge(S.layer1_ready, 2 * c + a + 1)
            cut = lambda w: (lambda q: w[a][:, q:q + H])
            products(conv_ps[a][:, :], (3, 2, 1, 0), bufs.e_hi[:, :, a, :], bufs.e_lo[:, :, a, :], cut(bufs.h_hi), cut(bufs.h_lo)).then_inc(S.cond_done, 1)

        def act_cond(act, c, a, bufs):
            act.wait_ge(S.cond_done, 2 * c + a + 1)
            act.nop(nofuse=True)
            nc.scalar.activation(bufs.cond[:, a, 1:H - 1], conv_ps[a][:, 1:H - 1], ACT.Identity, bias=at(bias4, c, a, bufs),
                                 scale=at(demod_tab[:, LAYERS - 1, :], c, a, bufs))
            n = 2 * c + a - bufs.first_sample
            ends = cond_edge[:, :, n:n + 1] if isinstance(n, int) else cond_edge[:, :, bass.ds(n, 1)]
            nc.scalar.activation(bufs.cond[:, a, 0:H:H - 1], ends.rearrange("p s u -> p (s u)"), ACT.Identity).then_inc(S.cond_ready, 1)

        def dve_pads(v, bufs):
            for a in range(2):
                for w in (bufs.h_hi[a], bufs.h_lo[a]):
                    nc.vector.memset(w[0:C, 0:1].bitcast(F32), 0.0)
                    nc.vector.memset(w[0:C, H + 1:H + 3].bitcast(F32), 0.0)
                    nc.vector.memset(w[C:P, 0:2].bitcast(F32), 0.0)
                    last = nc.vector.memset(w[C:P, H + 2:H + 3].bitcast(F32), 0.0)
            for w in (bufs.e_hi, bufs.e_lo):
                last = nc.vector.memset(w[C:P, E_PAIRS - 1, :, C:P].bitcast(F32), 0.0)
            last.then_inc(S.pads_ready, 1)

        def pe_turn(pe, f, bufs, packed):
            for a in range(2):
                pe.wait_ge(S.cond_ready, 2 * f + a + 1)
                for j in range(4):
                    cols = slice(j, H, 4) if packed else slice(j * P, (j + 1) * P)
                    last = nc.tensor.transpose(turn_ps[a][:, j * P:(j + 1) * P], bufs.cond[:, a, cols], ident[:, :])
                last.then_inc(S.turned, 1)

        def act_turn(act, f, bufs):
            for a in range(2):
                act.wait_ge(S.turned, 2 * f + a + 1)
                nc.scalar.activation(bufs.xt_hi[:, :, a * C:(a + 1) * C], turn_ps[a][:, :].rearrange("p (k o) -> p k o", k=KT),
                                     ACT.Identity).then_inc(S.xt_hi, 1)

        def dve_turn(v, f, bufs):
            for a in range(2):
                v.wait_ge(S.xt_hi, 2 * f + a + 1)
                low(bufs.xt_lo[:, :, a * C:(a + 1) * C], turn_ps[a][:, :].rearrange("p (k o) -> p k o", k=KT),
                    bufs.xt_hi[:, :, a * C:(a + 1) * C]).then_inc(S.xt_ready, 1)

        def pe_scores(pe, f, bufs):
            pe.wait_ge(S.xt_ready, 2 * f + 2)
            for k in range(KT):
                last = nc.tensor.matmul(turn_ps[0][:, 0:2 * P], bufs.wr[:, k, :], bufs.xt[:, k, :, :], start=(k == 0), stop=(k == KT - 1))
            last.then_inc(S.partial_scores, 1)

        def act_scores(act, f, bufs):
            act.wait_ge(S.partial_scores, f + 1)
            act.wait_ge(S.scored, f + 1)
            nc.scalar.activation(bufs.score_parts[:, :], turn_ps[0][:, 0:2 * P], ACT.Identity).then_inc(S.parts_copied, 1)

        def pe_score_sum(pe, f, bufs):
            pe.wait_ge(S.parts_copied, f + 1)
            nc.tensor.matmul(turn_ps[1][:, 0:NE], bufs.score_parts[:, 0:P], spread[:, 1, :], start=True, stop=False)
            nc.tensor.matmul(turn_ps[1][:, 0:NE], bufs.score_parts[0:NE, P:2 * P], spread[0:NE, 1, :], start=False, stop=True).then_inc(S.scored, 1)

        def pe_hidden(pe, f, n, bufs):
            if n == 0:
                pe.wait_ge(S.x1_ready, 2 * f + 1)
            cols = slice(n * 512, (n + 1) * 512)
            for k in range(KT):
                nc.tensor.matmul(prod_ps[n][:, :], bufs.xt_hi[:, k, :], bufs.a_hi[:, k, cols], start=(k == 0), stop=False)
                nc.tensor.matmul(prod_ps[n][:, :], bufs.xt_hi[:, k, :], bufs.a_lo[:, k, cols], start=False, stop=False)
                last = nc.tensor.matmul(prod_ps[n][:, :], bufs.xt_lo[:, k, :], bufs.a_hi[:, k, cols], start=False, stop=(k == KT - 1))
            last.then_inc(S.hidden_done, 1)

        def pe_gated_turn(pe, f, bufs):
            for n in range(2):
                pe.wait_ge(S.gated, 2 * f + n + 1)
                for j in range(4):
                    last = nc.tensor.transpose(turn_ps[n][:, j * P:(j + 1) * P], bufs.gated[:, n * 512 + j * P:n * 512 + (j + 1) * P], ident[:, :])
                last.then_inc(S.gated_turned, 1)

        def pe_adapter_out(pe, f, bufs):
            pe.wait_ge(S.hgt_ready, 2 * f + 2)
            for n in range(2):
                cols = slice(n * 512, (n + 1) * 512)
                for k in range(KT):
                    nc.tensor.matmul(prod_ps[n][:, :], bufs.xt_hi[:, k, :], bufs.b_hi[:, k, cols], start=(k == 0), stop=False)
                    nc.tensor.matmul(prod_ps[n][:, :], bufs.xt_hi[:, k, :], bufs.b_lo[:, k, cols], start=False, stop=False)
                    last = nc.tensor.matmul(prod_ps[n][:, :], bufs.xt_lo[:, k, :], bufs.b_hi[:, k, cols], start=False, stop=(k == KT - 1))
                last.then_inc(S.out_done, 1)

        def act_exp(act, f, bufs):
            act.wait_ge(S.top_max, f + 1)
            nc.scalar.activation(bufs.gate_exp[:, :], bufs.scores[:, :], ACT.Exp, bias=bufs.neg_max[:, 0:1]).then_inc(S.exp_ready, 1)

        def act_gated_turn(act, f, bufs):
            for n in range(2):
                act.wait_ge(S.gated_turned, 2 * f + n + 1)
                nc.scalar.activation(bufs.xt_hi[:, 4 * n:4 * n + 4, :], turn_ps[n][:, :].rearrange("p (k o) -> p k o", k=4),
                                     ACT.Identity).then_inc(S.hgt_hi, 1)

        TOP_STEPS = 9

        def dve_route(v, f, bufs):
            V = nc.vector
            n = [0]

            def step(ins):
                n[0] += 1
                ins.then_inc(S.tail, 1)
                v.wait_ge(S.tail, TOP_STEPS * f + n[0])
                v.nop(nofuse=True)

            v.wait_ge(S.scored, f + 2)
            step(V.tensor_copy(bufs.scores[:, :], turn_ps[1][:, 0:NE]))
            step(V.max(bufs.top[:, 0:8], bufs.scores[:, :]))
            V.tensor_scalar(bufs.neg_max[:, :], bufs.top[:, 0:1], -1.0, None, ALU.mult).then_inc(S.top_max, 1)
            step(V.match_replace(bufs.rest[:, :], bufs.top[:, 0:8], bufs.scores[:, :], LOWEST))
            step(V.max(bufs.top[:, 8:16], bufs.rest[:, :]))
            step(V.match_replace(bufs.rest2[:, :], bufs.top[:, 8:16], bufs.rest[:, :], LOWEST))
            step(V.tensor_tensor(bufs.chosen[:, :], bufs.rest2[:, :], bufs.scores[:, :], ALU.is_lt))
            v.wait_ge(S.exp_ready, f + 1)
            step(V.tensor_tensor(bufs.gate[:, :], bufs.gate_exp[:, :], bufs.chosen[:, :], ALU.mult))
            step(V.tensor_reduce(bufs.norm[:, 0:1], bufs.gate[:, :], AX.X, ALU.add))
            step(V.reciprocal(bufs.norm[:, 1:2], bufs.norm[:, 0:1]))
            V.tensor_scalar(bufs.norm[:, 2:3], bufs.norm[:, 1:2], LORA_SCALE, None, ALU.mult)

        def dve_gate(v, f, n, bufs):
            v.wait_ge(S.hidden_done, 2 * f + n + 1)
            shape = lambda ap: ap.rearrange("p (k r) -> p k r", r=RANK)
            experts = slice(n * NE // 2, (n + 1) * NE // 2)
            nc.vector.tensor_tensor(shape(bufs.gated[:, n * 512:(n + 1) * 512]), shape(prod_ps[n][:, :]),
                                    bufs.gate[:, experts].unsqueeze(2).broadcast_to([P, NE // 2, RANK]), ALU.mult).then_inc(S.gated, 1)

        def dve_gated_turn(v, f, bufs):
            for n in range(2):
                v.wait_ge(S.hgt_hi, 2 * f + n + 1)
                low(bufs.xt_lo[:, 4 * n:4 * n + 4, :], turn_ps[n][:, :].rearrange("p (k o) -> p k o", k=4),
                    bufs.xt_hi[:, 4 * n:4 * n + 4, :]).then_inc(S.hgt_ready, 1)

        def dve_first_residual(v, f, bufs):
            v.wait_ge(S.res_loaded, 16 * (f + 1))
            for n in range(2):
                cols = slice(n * 512, (n + 1) * 512)
                v.wait_ge(S.out_done, 2 * f + n + 1)
                nc.vector.scalar_tensor_tensor(out=bufs.res[:, cols], in0=prod_ps[n][:, :], scalar=bufs.norm[:, 2:3], in1=bufs.res[:, cols],
                                               op0=ALU.mult, op1=ALU.add).then_inc(S.x1_ready, 1)

        def pe_rowsum(pe, f, bufs):
            pe.wait_ge(S.sums_reduced, f - NPAIR + 1)
            for a in range(2):
                to_rows = spread[:, 1 - a:3 - a, :].rearrange("p t o -> p (t o)")
                last = nc.tensor.matmul(turn_ps[0][:, 0:1], to_rows, bufs.sums[:, a:a + 1], start=(a == 0), stop=(a == 1))
            last.then_inc(S.rowsum_done, 1)

        def dve_reduce(v, f, bufs):
            v.wait_ge(S.cond_ready, 2 * f + 2)
            nc.vector.tensor_reduce(bufs.sums[:, :], bufs.cond[:, :, :], AX.X, ALU.add).then_inc(S.sums_reduced, 1)

        def pe_quant(pe, f, n, bufs):
            if n == 0:
                pe.wait_ge(S.xt_ready, 2 * f + 2)
                pe.wait_ge(S.x1_ready, 2 * f + 1)
            cols = slice(n * 512, (n + 1) * 512)
            for k in range(KT):
                nc.tensor.matmul(prod_ps[n][:, :], bufs.xt_hi[:, k, :], bufs.quant[:, k, cols], start=(k == 0), stop=False)
                last = nc.tensor.matmul(prod_ps[n][:, :], bufs.xt_lo[:, k, :], bufs.quant[:, k, cols], start=False, stop=(k == KT - 1))
            last.then_inc(S.out_done, 1)

        def dve_rowsum(v, f, bufs):
            v.wait_ge(S.rowsum_done, f - NPAIR + 1)
            nc.vector.tensor_scalar(bufs.neg_sum[:, :], turn_ps[0][:, 0:1], -1.0, None, ALU.mult).then_inc(S.rowsum_read, 1)

        def dve_second_residual(v, f, bufs):
            g = f - NPAIR
            v.wait_ge(S.biased, g + 1)
            v.wait_ge(S.rowsum_read, g + 2)
            for n in range(2):
                cols = slice(n * 512, (n + 1) * 512)
                nc.vector.scalar_tensor_tensor(out=bufs.res[:, cols], in0=bufs.zeros[:, cols], scalar=bufs.neg_sum[:, 0:1], in1=bufs.res[:, cols],
                                               op0=ALU.mult, op1=ALU.add)
            for n in range(2):
                cols = slice(n * 512, (n + 1) * 512)
                v.wait_ge(S.out_done, 2 * f + n + 1)
                nc.vector.tensor_tensor(bufs.scaled[:, cols], prod_ps[n][:, :], bufs.scales[:, cols], ALU.mult).then_inc(S.x1_ready, 1)
            v.wait_ge(S.x1_ready, 2 * f + 3)
            nc.vector.tensor_tensor(bufs.res[:, :], bufs.res[:, :], bufs.scaled[:, :], ALU.add).then_inc(S.y_ready, 1)


        level0 = ExitStack()
        buf0 = conv_buffers(level0, 0)
        T0 = lambda n, s, d=F32: tensor(level0, n, s, d)
        buf0.wr = T0("wr", [P, KT, 2 * NE], F32R)
        buf0.a_hi, buf0.a_lo = T0("a_hi", [P, KT, KR], F32R), T0("a_lo", [P, KT, KR], F32R)
        buf0.scores, buf0.rest, buf0.rest2, buf0.chosen = T0("scores", [P, NE]), T0("rest", [P, NE]), T0("rest2", [P, NE]), T0("chosen", [P, NE])
        buf0.gate_exp, buf0.gate, buf0.top = T0("gate_exp", [P, NE]), T0("gate", [P, NE]), T0("top", [P, 2 * 8])
        buf0.neg_max, buf0.norm = T0("neg_max", [P, 1]), T0("norm", [P, 3])
        buf0.cond = T0("cond0", [P, 2, H])
        A_RING, B_RING = 3, 3
        SETUP_WORDS = 13300
        with ExitStack() as stage:
            a_nat = tensor(stage, "a_nat", [P, A_RING, D], F32)
            set0 = setup_buffers(stage, 0)
            used = 4 * (A_RING * D + SETUP_WORDS)
            tensor(stage, "gap", [P, 8 * KT * D - used], mybir.dt.uint8)
            b_nat = tensor(stage, "b_nat", [P, B_RING, KT, P], F32)
            wr_nat = tensor(stage, "wr_nat", [NE, D], F32)
        buf0.b_hi, buf0.b_lo = T0("b_hi", [P, KT, D], F32R), T0("b_lo", [P, KT, D], F32R)
        buf0.xt, buf0.res = T0("xt0", [P, KT, 2, P], F32R), T0("res0", [P, D])
        buf0.xt_hi, buf0.xt_lo = buf0.xt[:, :, 0, :], buf0.xt[:, :, 1, :]
        buf0.score_parts = T0("score_parts", [P, 2 * P])
        buf0.gated = buf0.cond[:, :, :].rearrange("p a h -> p (a h)")
        level0.close()

        level1 = ExitStack()
        T1 = lambda n, s, d=F32: tensor(level1, n, s, d)
        buf1 = conv_buffers(level1, 1)
        set1 = setup_buffers(level1, 1)
        packed, nibble = T1("packed", [P, D], I32), [T1(f"nibble{i}", [P, D], I32) for i in range(2)]
        buf1.sums, buf1.neg_sum = T1("sums", [P, 2]), T1("neg_sum", [P, 1])
        buf1.quant = T1("quant", [P, KT, D], F32R)
        buf1.scales, buf1.zeros, buf1.bias = T1("scales", [P, D]), T1("zeros", [P, D]), T1("bias", [P, D])
        buf1.scaled, buf1.cond, buf1.res = T1("scaled", [P, D]), T1("cond1", [P, 2, H]), T1("res1", [P, D])
        buf1.xt_hi, buf1.xt_lo = T1("xt_hi1", [P, KT, P], F32R), T1("xt_lo1", [P, KT, P], F32R)
        level1.close()

        a_src, b_src = t["L0_ffn_A"].rearrange("(g k) r d -> g (k r) d", g=KT), t["L0_ffn_B"].rearrange("(g k) (j d) r -> g j d k r", g=KT, d=P)
        group_ps = [fold_ps[0], fold_ps[1], prod_ps[0], prod_ps[1]]
        GROUPS = [("r", 0, 0)] + [(kind, g, h) for kind in "ab" for g in range(KT) for h in range(2)]
        FIRST_B = 1 + 2 * KT
        position = lambda k: slice(2 * P * (k // 2) + k % 2, 2 * P * (k // 2 + 1), 2)

        def group_out(n, hi):
            kind, g, h = GROUPS[n]
            if kind == "r":
                return buf0.wr[:, :, 0:NE] if hi else buf0.wr[:, :, NE:2 * NE]
            if kind == "a":
                return (buf0.a_hi if hi else buf0.a_lo)[:, 4 * h:4 * h + 4, g * P:(g + 1) * P]
            return (buf0.b_hi if hi else buf0.b_lo)[:, g, h * 512:(h + 1) * 512]

        def group_in(n):
            kind = GROUPS[n][0]
            return group_ps[n % 4][:, :] if kind == "b" else group_ps[n % 4][:, :].rearrange("p (k e) -> p k e", k=KT if kind == "r" else 4)

        def pe_turn_weights(pe):
            for n, (kind, g, h) in enumerate(GROUPS):
                if n >= 4:
                    pe.wait_ge(S.weights_lo, n - 3)
                if kind == "r":
                    pe.wait_ge(S.router_loaded, 16)
                elif h == 0:
                    pe.wait_ge((S.a_loaded if kind == "a" else S.b_loaded)[g % A_RING], 16 * (g // A_RING + 1) * (1 if kind == "a" else KT))
                ps = group_ps[n % 4]
                if kind == "r":
                    for k in range(KT):
                        last = nc.tensor.transpose(ps[:, k * NE:(k + 1) * NE], wr_nat[:, position(k)], ident[0:NE, 0:NE])
                else:
                    for j in range(4):
                        src = a_nat[:, g % A_RING, position(4 * h + j)] if kind == "a" else b_nat[:, g % B_RING, 4 * h + j, :]
                        last = nc.tensor.transpose(ps[:, j * P:(j + 1) * P], src, ident[:, :])
                last.then_inc(S.weights_turned, 1)

        def sp_load(sp, c, first):
            src = x_pairs if first else x_scratch
            for a in range(2):
                rows = src[c if first else c - NPAIR, a * C:(a + 1) * C, :]
                done = (S.xin_loaded0, S.xin_loaded1)[a]
                sp.dma_start(x_in[a][0:C, 0:D], rows).then_inc(done, 16)
                sp.dma_start(x_in[a][C:P, 1:D + 1], rows).then_inc(done, 16)

        block = outer.enter_context(nc.Block())

        @block.sync
        def _(sp):
            setup_loads(sp, 0, set0)
            sp_load(sp, 0, True)
            edge_loads(sp, 0, set0)
            sp.dma_start(wr_nat[:, :], t["L0_ffn_Wr"]).then_inc(S.router_loaded, 16)
            for g in range(KT):
                if g >= A_RING:
                    sp.wait_ge(S.weights_turned, 1 + 2 * (g - A_RING + 1))
                sp.dma_start(a_nat[:, g % A_RING, :], a_src[g]).then_inc(S.a_loaded[g % A_RING], 16)
            for g in range(KT):
                if g >= B_RING:
                    sp.wait_ge(S.weights_turned, FIRST_B + 2 * (g - B_RING + 1))
                for j in range(KT):
                    sp.dma_start(b_nat[:, g % B_RING, j, :].rearrange("d (k r) -> d k r", r=RANK), b_src[g, j]).then_inc(S.b_loaded[g % B_RING], 16)
            with sp.Fori(0, NPAIR - 1) as i:
                sp.wait_ge(S.xin_split, 2 * i + 2)
                sp_load(sp, i + 1, True)
            sp.wait_ge(S.x1_stored, 16 * NPAIR)
            setup_loads(sp, 1, set1)
            sp_load(sp, NPAIR, False)
            edge_loads(sp, 1, set1)
            sp.dma_start(packed[:, :], t["L1_ffn_qweight"]).then_inc(S.quant_loaded, 16)
            for dst, src in ((buf1.scales, t["L1_ffn_scales"].rearrange("o u -> u o")), (buf1.zeros, t["L1_ffn_zeros"].rearrange("o u -> u o")),
                             (buf1.bias, t["L1_ffn_bias"].rearrange("(u o) -> u o", u=1))):
                sp.dma_start(dst[:, :], src.broadcast_to([P, D])).then_inc(S.consts_loaded, 16)
            with sp.Fori(NPAIR, 2 * NPAIR - 1) as i:
                sp.wait_ge(S.xin_split, 2 * i + 2)
                sp_load(sp, i + 1, False)

        @block.gpsimd
        def _(pool):
            nc.gpsimd.memset(ident[:, :], 0.0).then_inc(S.ident_clear, 1)
            nc.gpsimd.memset(eps_col[:, :], EPS).then_inc(S.ident_ready, 1)
            pool.wait_ge(S.ident_clear, 1)
            nc.gpsimd.affine_select(out=ident[:, :], in_=ident[:, :], compare_op=ALU.not_equal, fill=1.0, base=0,
                                    pattern=[[-1, P]], channel_multiplier=1).then_inc(S.ident_ready, 1)
            nc.gpsimd.memset(spread[:, :, :], 0.0).then_inc(S.ident_clear, 1)
            pool.wait_ge(S.ident_clear, 2)
            pool.wait_ge(S.ident_ready, 2)
            for rows in (slice(0, C), slice(C, P)):
                nc.gpsimd.tensor_copy(spread[rows, 1, :], ident[rows, rows]).then_inc(S.spread_ready, 1)
            pool.wait_ge(S.weights_turned, len(GROUPS))
            pool.dma_start(buf0.res[:, :], x_pairs[0]).then_inc(S.res_loaded, 16)
            with pool.Fori(0, NPAIR - 1) as i:
                pool.wait_ge(S.x1_ready, 2 * i + 3)
                pool.dma_start(x_scratch[i], buf0.res[:, :]).then_inc(S.x1_stored, 16)
                pool.wait_ge(S.x1_stored, 16 * i + 16)
                pool.dma_start(buf0.res[:, :], x_pairs[i + 1]).then_inc(S.res_loaded, 16)
            pool.wait_ge(S.x1_ready, 2 * NPAIR + 1)
            pool.dma_start(x_scratch[NPAIR - 1], buf0.res[:, :]).then_inc(S.x1_stored, 16)
            pool.wait_ge(S.x1_stored, 16 * NPAIR)
            pool.wait_ge(S.consts_loaded, 16 * 3)
            pool.dma_start(buf1.res[:, :], x_scratch[0]).then_inc(S.res_loaded, 16)

            def add_bias(f):
                pool.wait_ge(S.res_loaded, 16 * (f + 1))
                nc.gpsimd.tensor_tensor(buf1.res[:, :], buf1.res[:, :], buf1.bias[:, :], ALU.add).then_inc(S.biased, 1)

            with pool.Fori(0, NPAIR - 1) as i:
                add_bias(i + NPAIR)
                pool.wait_ge(S.y_ready, i + 1)
                pool.dma_start(out_pairs[i], buf1.res[:, :]).then_inc(S.y_stored, 16)
                pool.wait_ge(S.y_stored, 16 * i + 16)
                pool.dma_start(buf1.res[:, :], x_scratch[i + 1]).then_inc(S.res_loaded, 16)
            add_bias(2 * NPAIR - 1)
            pool.wait_ge(S.y_ready, NPAIR)
            pool.dma_start(out_pairs[NPAIR - 1], buf1.res[:, :]).then_inc(S.y_stored, 16)
            pool.wait_ge(S.y_stored, 16 * NPAIR)

        @block.tensor
        def _(pe):
            def first_pair(L, s, bufs):
                c = L * NPAIR
                setup_tensor(pe, L, s)
                inner_tensor(pe, L, s)
                edge_tensor(pe, L, s)
                pe.wait_ge(S.tiles_ready, L + 1)
                pe_fold3(pe, c, bufs, c == 0)
                for a in range(2):
                    pe_layer1(pe, c, a, bufs, c == 0)
                pe_fold2(pe, c, bufs, c == 0)
                for a in range(2):
                    pe_cond(pe, c, a, bufs)

            first_pair(0, set0, buf0)
            pe_turn_weights(pe)
            pe.wait_ge(S.weights_lo, len(GROUPS))
            pe.wait_ge(S.spread_ready, 2)
            with pe.Fori(0, NPAIR - 1) as i:
                c = i + 1
                pe_layer1(pe, c, 0, buf0)
                pe_turn(pe, i, buf0, False)
                pe_layer1(pe, c, 1, buf0)
                pe_fold3(pe, c, buf0)
                pe_scores(pe, i, buf0)
                pe_hidden(pe, i, 0, buf0)
                pe_score_sum(pe, i, buf0)
                pe_fold2(pe, c, buf0)
                pe_hidden(pe, i, 1, buf0)
                pe_cond(pe, c, 0, buf0)
                pe_gated_turn(pe, i, buf0)
                pe_cond(pe, c, 1, buf0)
                pe_adapter_out(pe, i, buf0)
            f = NPAIR - 1
            pe_turn(pe, f, buf0, False)
            pe_scores(pe, f, buf0)
            pe_hidden(pe, f, 0, buf0)
            pe_score_sum(pe, f, buf0)
            pe_hidden(pe, f, 1, buf0)
            pe_gated_turn(pe, f, buf0)
            pe_adapter_out(pe, f, buf0)

            pe.wait_ge(S.x1_ready, 2 * NPAIR + 1)
            first_pair(1, set1, buf1)
            pe.wait_ge(S.quant_ready, 1)
            with pe.Fori(NPAIR, 2 * NPAIR - 1) as i:
                c = i + 1
                pe_layer1(pe, c, 0, buf1)
                pe.wait_ge(S.rowsum_read, i - NPAIR + 1)
                pe_turn(pe, i, buf1, True)
                pe_layer1(pe, c, 1, buf1)
                pe_fold3(pe, c, buf1)
                pe_quant(pe, i, 0, buf1)
                pe_rowsum(pe, i, buf1)
                pe_fold2(pe, c, buf1)
                pe_quant(pe, i, 1, buf1)
                pe_cond(pe, c, 0, buf1)
                pe_cond(pe, c, 1, buf1)
            f = 2 * NPAIR - 1
            pe.wait_ge(S.rowsum_read, NPAIR)
            pe_turn(pe, f, buf1, True)
            pe_quant(pe, f, 0, buf1)
            pe_rowsum(pe, f, buf1)
            pe_quant(pe, f, 1, buf1)

        @block.scalar
        def _(act):
            def first_pair(L, s, bufs):
                c = L * NPAIR
                setup_scalar(act, L, s)
                act.wait_ge(S.tables_ready, L + 1)
                act.wait_ge(S.tiles_ready, L + 1)
                act_fold_start(act, c, bufs, c == 0)
                act_fold3(act, c, bufs, c == 0)
                for a in range(2):
                    act_layer1(act, c, a, bufs)
                act_fold2(act, c, bufs, c == 0)
                act.wait_ge(S.bias4_ready, L + 1)
                act.wait_ge(S.edges_done, L + 1)
                for a in range(2):
                    act_cond(act, c, a, bufs)

            first_pair(0, set0, buf0)
            for n in range(len(GROUPS)):
                act.wait_ge(S.weights_turned, n + 1)
                nc.scalar.activation(group_out(n, True), group_in(n), ACT.Identity).then_inc(S.weights_hi, 1)
            nc.scalar.preload_act_table(ACT.Exp)
            with act.Fori(0, NPAIR - 1) as i:
                c = i + 1
                act_fold_start(act, c, buf0)
                act_turn(act, i, buf0)
                act_layer1(act, c, 0, buf0)
                act_layer1(act, c, 1, buf0)
                act_fold3(act, c, buf0)
                act_scores(act, i, buf0)
                act_exp(act, i, buf0)
                act_fold2(act, c, buf0)
                act_gated_turn(act, i, buf0)
                act_cond(act, c, 0, buf0)
                act_cond(act, c, 1, buf0)
            f = NPAIR - 1
            act_turn(act, f, buf0)
            act_scores(act, f, buf0)
            act_exp(act, f, buf0)
            act_gated_turn(act, f, buf0)

            first_pair(1, set1, buf1)
            nc.scalar.preload_act_table(ACT.Identity)
            with act.Fori(NPAIR, 2 * NPAIR - 1) as i:
                c = i + 1
                act_fold_start(act, c, buf1)
                act_turn(act, i, buf1)
                act_layer1(act, c, 0, buf1)
                act_layer1(act, c, 1, buf1)
                act_fold3(act, c, buf1)
                act_fold2(act, c, buf1)
                act_cond(act, c, 0, buf1)
                act_cond(act, c, 1, buf1)
            act_turn(act, 2 * NPAIR - 1, buf1)

        @block.vector
        def _(v):
            v.sem_inc(S.x1_ready, 1)
            v.sem_inc(S.rowsum_read, 1)
            v.sem_inc(S.scored, 1)
            for a in range(2):
                nc.vector.memset(x_in[a][0:C, D:D + 1], 0.0)
                nc.vector.memset(x_in[a][C:P, 0:1], 0.0)

            def split(c, bufs, first=False):
                for a in range(2):
                    dve_split(v, c, a, bufs, first)

            def first_pair(L, s, bufs):
                c = L * NPAIR
                dve_pads(v, bufs)
                setup_vector(v, L, s)
                inner_vector(v, L, s)
                edge_vector(v, L, s)
                split(c, bufs, c == 0)
                dve_fold_start(v, c, bufs)
                dve_fold3(v, c, bufs)
                for a in range(2):
                    dve_layer1(v, c, a, bufs)
                dve_fold2(v, c, bufs)

            first_pair(0, set0, buf0)
            for n in range(len(GROUPS)):
                v.wait_ge(S.weights_hi, n + 1)
                low(group_out(n, False), group_in(n), group_out(n, True)).then_inc(S.weights_lo, 1)

            def first_step(i, last):
                c = i + 1
                dve_fold_start(v, c, buf0)
                dve_turn(v, i, buf0)
                dve_layer1(v, c, 0, buf0)
                dve_layer1(v, c, 1, buf0)
                dve_fold3(v, c, buf0)
                dve_route(v, i, buf0)
                dve_gate(v, i, 0, buf0)
                dve_fold2(v, c, buf0)
                dve_gate(v, i, 1, buf0)
                dve_gated_turn(v, i, buf0)
                if not last:
                    split(c + 1, buf0)
                dve_first_residual(v, i, buf0)

            split(1, buf0)
            with v.Fori(0, NPAIR - 2) as i:
                first_step(i, False)
            first_step(NPAIR - 2, True)
            f = NPAIR - 1
            dve_turn(v, f, buf0)
            dve_route(v, f, buf0)
            dve_gate(v, f, 0, buf0)
            dve_gate(v, f, 1, buf0)
            dve_gated_turn(v, f, buf0)
            dve_first_residual(v, f, buf0)

            v.wait_ge(S.x1_stored, 16 * NPAIR)
            first_pair(1, set1, buf1)
            v.wait_ge(S.quant_loaded, 16)
            for k in range(KT):
                n = nibble[k % 2]
                nc.vector.tensor_scalar(n[:, :], packed[:, :], 4 * k, 15, ALU.logical_shift_right, ALU.bitwise_and).then_inc(S.nibble_ready, 1)
                v.wait_ge(S.nibble_ready, k + 1)
                last = nc.vector.tensor_copy(buf1.quant[:, k, :], n[:, :])
            last.then_inc(S.quant_ready, 1)
            v.wait_ge(S.consts_loaded, 16 * 3)

            def second_step(i, last):
                c = i + 1
                dve_fold_start(v, c, buf1)
                dve_turn(v, i, buf1)
                dve_reduce(v, i, buf1)
                dve_layer1(v, c, 0, buf1)
                dve_layer1(v, c, 1, buf1)
                dve_fold3(v, c, buf1)
                if not last:
                    split(c + 1, buf1)
                dve_rowsum(v, i, buf1)
                dve_fold2(v, c, buf1)
                dve_second_residual(v, i, buf1)

            split(NPAIR + 1, buf1)
            with v.Fori(NPAIR, 2 * NPAIR - 2) as i:
                second_step(i, False)
            second_step(2 * NPAIR - 2, True)
            f = 2 * NPAIR - 1
            dve_turn(v, f, buf1)
            dve_reduce(v, f, buf1)
            dve_rowsum(v, f, buf1)
            dve_second_residual(v, f, buf1)


def kernel(**inputs):
    import concourse.bacc as bacc
    from concourse.bass_utils import run_bass_kernel_spmd

    nc = bacc.Bacc("TRN2", target_bir_lowering=False, num_devices=1)
    arrays, tensors = {}, {}
    for name, value in inputs.items():
        a = np.ascontiguousarray(value)
        arrays[f"in_{name}"] = a
        tensors[name] = nc.dram_tensor(f"in_{name}", a.shape, mybir.dt.from_np(a.dtype), kind="ExternalInput").ap()
    tensors["out"] = nc.dram_tensor("out_x", (B, C, D), F32, kind="ExternalOutput").ap()
    program(nc, tensors)
    result = run_bass_kernel_spmd(nc, [arrays], core_ids=[0])
    return result.results[0]["out_x"]
```

```python
from contextlib import ExitStack

import numpy as np

import concourse.bass as bass
import concourse.mybir as mybir

F32 = mybir.dt.float32
F32R = mybir.dt.float32r
I32 = mybir.dt.int32
ALU = mybir.AluOpType
ACT = mybir.ActivationFunctionType
AX = mybir.AxisListType

class Buffers:
    pass


B, C, D = 32, 64, 1024
STYLE = 128
P = 128
NPAIR = B // 2
H = D // 2
DOWN_PAIRS, R_PAIRS, E_PAIRS = 3, 4, 4
NE, RANK = 64, 16
KR = NE * RANK
KT = D // P
TAPS = 3
LAYERS = 4
SCALE = 1.0 / float(np.sqrt(C * TAPS ** 2))
EPS = 1e-8
LORA_SCALE = 2.0
LOWEST = -3.0e38


def program(nc, t):
    with ExitStack() as outer:
        def sem(name):
            return outer.enter_context(nc.semaphore(name))

        def tensor(stack, name, shape, dt):
            return stack.enter_context(nc.sbuf_tensor(name, shape, dt))

        conv_ps = [outer.enter_context(nc.psum_tensor(f"conv_ps{i}", [P, 512], F32)) for i in range(2)]
        fold_ps = [outer.enter_context(nc.psum_tensor(f"fold_ps{i}", [P, 512], F32)) for i in range(2)]
        prod_ps = [outer.enter_context(nc.psum_tensor(f"prod_ps{i}", [P, 512], F32)) for i in range(2)]
        turn_ps = [outer.enter_context(nc.psum_tensor(f"turn_ps{i}", [P, 512], F32)) for i in range(2)]

        ident = tensor(outer, "ident", [P, P], F32)
        spread = tensor(outer, "spread", [P, 3, C], F32)
        eps_col = tensor(outer, "eps_col", [P, 1], F32)
        w1_hi, w1_lo = tensor(outer, "w1_hi", [P, 2, P], F32R), tensor(outer, "w1_lo", [P, 2, P], F32R)
        fold3_hi, fold3_lo = tensor(outer, "fold3_hi", [P, 2, P], F32R), tensor(outer, "fold3_lo", [P, 2, P], F32R)
        fold2_hi, fold2_lo = tensor(outer, "fold2_hi", [P, 5, P], F32R), tensor(outer, "fold2_lo", [P, 5, P], F32R)
        down_T = tensor(outer, "down_T", [P, DOWN_PAIRS, C], F32)
        style_tab = tensor(outer, "style_tab", [P, LAYERS, B], F32)
        demod_tab = tensor(outer, "demod_tab", [P, LAYERS, B], F32)
        bias_tab = tensor(outer, "bias_tab", [P, LAYERS], F32)
        scale1, bias1, scale2, scale3, bias4 = [tensor(outer, n, [P, B], F32) for n in ("scale1", "bias1", "scale2", "scale3", "bias4")]
        cond_edge = tensor(outer, "cond_edge", [P, 2, B], F32)
        x_in = [tensor(outer, f"x_in{a}", [P, D + 2], F32) for a in range(2)]

        x_scratch = nc.dram_tensor("x_after_first", [NPAIR, P, D], F32, kind="Internal").ap()

        S = Buffers()
        S.link = sem("link")
        S.small_loaded = sem("small_loaded")
        S.edges_clear = sem("edges_clear")
        S.edges_loaded = sem("edges_loaded")
        S.ident_ready = sem("ident_ready")
        S.style_turned = sem("style_turned")
        S.sums_ready = sem("sums_ready")
        S.sums_turned = sem("sums_turned")
        S.style_T_ready = sem("style_T_ready")
        S.style_done = sem("style_done")
        S.images_ready = sem("images_ready")
        S.images_turned = sem("images_turned")
        S.style_sq_ready = sem("style_sq_ready")
        S.squares_done = sem("squares_done")
        S.tables_ready = sem("tables_ready")
        S.inner_done = sem("inner_done")
        S.inner_ready = sem("inner_ready")
        S.tiles_hi = sem("tiles_hi")
        S.root_ready = sem("root_ready")
        S.tiles_ready = sem("tiles_ready")
        S.bias4_ready = sem("bias4_ready")
        S.edge_ready = sem("edge_ready")
        S.edge_done = sem("edge_done")
        S.edges_done = sem("edges_done")
        S.fold3_done = sem("fold3_done")
        S.fold_in_hi = sem("fold_in_hi")
        S.fold_in_ready = sem("fold_in_ready")
        S.fold3_ready = sem("fold3_ready")
        S.fold2_done = sem("fold2_done")
        S.fold3_hi = sem("fold3_hi")
        S.fold2_ready = sem("fold2_ready")
        S.fold2_lo = sem("fold2_lo")
        S.partial_scores = sem("partial_scores")
        S.parts_copied = sem("parts_copied")
        S.sums_reduced = sem("sums_reduced")
        S.cond_done = sem("cond_done")
        S.fold2_hi = sem("fold2_hi")
        S.xin_loaded0 = sem("xin_loaded0")
        S.xin_loaded1 = sem("xin_loaded1")
        S.layer1_done = sem("layer1_done")
        S.xin_hi = sem("xin_hi")
        S.xin_split = sem("xin_split")
        S.cond_ready = sem("cond_ready")
        S.layer1_scaled = sem("layer1_scaled")
        S.layer1_hi = sem("layer1_hi")
        S.layer1_ready = sem("layer1_ready")
        S.turned = sem("turned")
        S.xt_hi = sem("xt_hi")
        S.xt_ready = sem("xt_ready")
        S.scored = sem("scored")
        S.x1_ready = sem("x1_ready")
        S.hidden_done = sem("hidden_done")
        S.gated = sem("gated")
        S.gated_turned = sem("gated_turned")
        S.hgt_ready = sem("hgt_ready")
        S.out_done = sem("out_done")
        S.top_max = sem("top_max")
        S.exp_ready = sem("exp_ready")
        S.hgt_hi = sem("hgt_hi")
        S.tail = sem("tail")
        S.res_loaded = sem("res_loaded")
        S.rowsum_done = sem("rowsum_done")
        S.rowsum_read = sem("rowsum_read")
        S.biased = sem("biased")
        S.y_ready = sem("y_ready")
        S.weights_lo = sem("weights_lo")
        S.router_loaded = sem("router_loaded")
        S.weights_turned = sem("weights_turned")
        S.x1_stored = sem("x1_stored")
        S.quant_loaded = sem("quant_loaded")
        S.consts_loaded = sem("consts_loaded")
        S.ident_clear = sem("ident_clear")
        S.spread_ready = sem("spread_ready")
        S.y_stored = sem("y_stored")
        S.last_stored = sem("last_stored")
        S.quant_ready = sem("quant_ready")
        S.weights_hi = sem("weights_hi")
        S.nibble_ready = sem("nibble_ready")
        S.b_hi_ready = sem("b_hi_ready")
        S.b_lo_ready = sem("b_lo_ready")
        S.a_loaded = [sem(f"a_loaded{i}") for i in range(4)]
        S.b_loaded = [sem(f"b_loaded{i}") for i in range(3)]

        x_pairs = t["x"].rearrange("(p two) c d -> p (two c) d", two=2)
        out_pairs = t["out"].rearrange("(p two) c d -> p (two c) d", two=2)

        def low(out, whole, hi):
            return nc.vector.tensor_tensor(out, whole, hi.bitcast(F32), ALU.subtract)

        link_count = [0]

        def link(v, ins):
            link_count[0] += 1
            ins.then_inc(S.link, 1)
            v.wait_ge(S.link, link_count[0])

        def products(out, stationary, hi, lo, moving_hi, moving_lo):
            n = len(stationary)
            for i, w in enumerate(stationary):
                nc.tensor.matmul(out, hi[:, w, :], moving_hi(i), start=(i == 0), stop=False)
                nc.tensor.matmul(out, hi[:, w, :], moving_lo(i), start=False, stop=False)
                last = nc.tensor.matmul(out, lo[:, w, :], moving_hi(i), start=False, stop=(i == n - 1))
            return last

        def setup_inputs(stack, L):
            T = lambda n, s: tensor(stack, f"L{L}_{n}", s, F32)
            s = Buffers()
            s.style, s.mod_w, s.mod_b = T("style", [B, STYLE]), T("mod_w", [C, LAYERS, STYLE]), T("mod_b", [P, LAYERS])
            s.w = T("w", [P, LAYERS, C * TAPS])
            return s

        def setup_buffers(stack, L, s):
            T = lambda n, s, d=F32: tensor(stack, f"L{L}_{n}", s, d)
            s.level = L
            s.style_T, s.mod_wT = T("style_T", [STYLE, B]), T("mod_wT", [STYLE, LAYERS, 2, C])
            s.wsq, s.wsum = T("wsq", [C, LAYERS, C * TAPS]), T("wsum", [C, LAYERS + 2, C])
            s.wsum_T, s.style_sq = T("wsum_T", [C, LAYERS + 2, 2, C]), T("style_sq", [P, LAYERS, B])
            s.same, s.down, s.up = [T(f"same{i}", [C, 5, C]) for i in range(2)], T("down", [C, 10, C]), T("up", [P, 10, C])
            s.same3 = T("same3", [P, 4, C])
            s.blur, s.blur_d = [T(f"blur{i}", [P, 7 - i, C]) for i in range(2)], [T(f"blur_d{i}", [C, 7 - i, C]) for i in range(2)]
            s.blur, s.blur_d = s.blur + s.blur[0:1], s.blur_d + s.blur_d[0:1]
            s.var, s.root, s.newton = T("var", [P, LAYERS * B]), T("root", [P, LAYERS * B]), T("newton", [P, LAYERS * B])
            s.bias2, s.edge2, s.bias3, s.inner = T("bias2", [P, B]), T("edge2", [P, B]), T("bias3", [P, B]), T("inner", [P, B])
            s.w_hi, s.w_lo = T("w_hi", [P, 10, P], F32R), T("w_lo", [P, 10, P], F32R)
            s.x_edge = T("x_edge", [P, 2, B, 10])
            s.edge, s.edge_hi, s.edge_lo = [None] * 4, [None] * 4, [None] * 4
            for i in range(2):
                n = 4 - i
                s.edge[i], s.edge_hi[i], s.edge_lo[i] = T(f"side{i}", [P, 2, n, B]), T(f"side_hi{i}", [P, 2, n, B], F32R), T(f"side_lo{i}", [P, 2, n, B], F32R)
                s.edge[i + 2], s.edge_hi[i + 2], s.edge_lo[i + 2] = s.edge[i], s.edge_hi[i], s.edge_lo[i]
            s.scaled = T("side_scaled", [P, 2, 3, B])
            return s

        SMALL = 9 * 16
        EDGES = 4 * 16

        def setup_loads(sp, L, s):
            g = lambda n: t[f"L{L}_cond_{n}"]
            w = g("weights").rearrange("l o i k -> o l (i k)")
            with nc.allow_non_contiguous_dma(reason="a few hundred words"):
                for dst, src in (
                        (s.style[:, :], t["cond_512"]), (s.mod_w[:, :, :], g("mod_w").rearrange("l i k -> i l k")),
                        (s.mod_b[0:C], g("mod_b").rearrange("l i -> i l")), (s.mod_b[C:P], g("mod_b").rearrange("l i -> i l")),
                        (s.w[0:C], w), (s.w[C:P, 1:3], w[:, 1:3]),
                        (bias_tab[0:C], g("biases").rearrange("l i -> i l")), (bias_tab[C:P], g("biases").rearrange("l i -> i l"))):
                    sp.dma_start(dst, src).then_inc(S.small_loaded, 16)
                sp.dma_start(s.w[C:P, 0], w[:, 0]).then_inc(S.small_loaded, 16)

        def edge_loads(sp, L, s, samples):
            src = (t["x"].rearrange("b c d -> c b d") if L == 0 else x_scratch.rearrange("p (two c) d -> c (p two) d", two=2))[:, samples, :]
            sp.wait_ge(S.edges_clear, L + 1)
            with nc.allow_non_contiguous_dma(reason="8 words of each row"):
                sp.dma_start(s.x_edge[0:C, 0, samples, 0:8], src[:, :, 0:8]).then_inc(S.edges_loaded, 16)
                sp.dma_start(s.x_edge[C:P, 0, samples, 1:9], src[:, :, 0:8]).then_inc(S.edges_loaded, 16)
                sp.dma_start(s.x_edge[0:C, 1, samples, 0:6], src[:, :, D - 6:D]).then_inc(S.edges_loaded, 16)
                sp.dma_start(s.x_edge[C:P, 1, samples, 0:7], src[:, :, D - 7:D]).then_inc(S.edges_loaded, 16)

        def sums_turned(first, end):
            return (turn_ps[1][0:C, 4 * C + first * C:4 * C + end * C] if first < LAYERS
                    else turn_ps[0][0:C, 6 * C + (first - LAYERS) * C:6 * C + (end - LAYERS) * C])

        def setup_tensor(pe, L, s):
            n = L + 1
            pe.wait_ge(S.ident_ready, 2)
            pe.wait_ge(S.small_loaded, SMALL * n)
            nc.tensor.transpose(turn_ps[0][:, 0:B], s.style[:, :], ident[0:B, 0:B])
            for l in range(LAYERS):
                last = nc.tensor.transpose(turn_ps[1][:, l * C:(l + 1) * C], s.mod_w[:, l, :], ident[0:C, 0:C])
            last.then_inc(S.style_turned, 1)
            pe.wait_ge(S.images_ready, n)
            for q in range(2):
                for f in range(2):
                    j = 2 - 2 * q + f
                    for i, ps in enumerate((conv_ps[0][:, 0:2 * P], conv_ps[0][:, 2 * P:4 * P])):
                        nc.tensor.transpose(ps[:, q * P + f * C:q * P + (f + 1) * C],
                                            s.same[i][:, j:j + 2, :].rearrange("o j i -> o (j i)"), ident[0:C, 0:C])
            for q in range(4):
                for f in range(2):
                    j = 2 + 2 * q - 2 * f
                    nc.tensor.transpose(fold_ps[0][:, q * P + f * C:q * P + (f + 1) * C],
                                        s.down[:, j:j + 2, :].rearrange("o j i -> o (j i)"), ident[0:C, 0:C])
            for q in range(5):
                out = conv_ps[1][:, q * P:(q + 1) * P] if q < 4 else fold_ps[1][:, 2 * P:3 * P]
                for f, j in enumerate((max(2 * q - 1, 0), min(2 * q + 1, 8))):
                    nc.tensor.transpose(out[:, f * C:(f + 1) * C], s.up[0:C, j:j + 2, :].rearrange("o j i -> o (j i)"), ident[0:C, 0:C])
            for q in range(DOWN_PAIRS):
                j = 2 + 2 * (DOWN_PAIRS - 1 - q)
                last = nc.tensor.transpose(fold_ps[1][:, q * C:(q + 1) * C], s.down[:, j:j + 2, :].rearrange("o j i -> o (j i)"), ident[0:C, 0:C])
            last.then_inc(S.images_turned, 1)
            pe.wait_ge(S.sums_ready, n)
            pe.wait_ge(S.style_T_ready, n)
            for l in range(LAYERS + 2):
                last = nc.tensor.transpose(sums_turned(l, l + 1), s.wsum[:, l, :], ident[0:C, 0:C])
            last.then_inc(S.sums_turned, 1)
            for l in range(LAYERS):
                last = nc.tensor.matmul(turn_ps[0][:, 64 + l * B:64 + (l + 1) * B], s.mod_wT[:, l].rearrange("k two i -> k (two i)"),
                                        s.style_T[:, :], start=True, stop=True)
            last.then_inc(S.style_done, 1)

        def squares_tensor(pe, L, s):
            pe.wait_ge(S.style_sq_ready, L + 1)
            for l in range(LAYERS):
                last = nc.tensor.matmul(turn_ps[0][:, 256 + l * B:256 + (l + 1) * B], s.wsum_T[:, l].rearrange("i two o -> i (two o)"),
                                        s.style_sq[0:C, l, :], start=True, stop=True)
            last.then_inc(S.squares_done, 1)

        def inner_tensor(pe, L, s, step):
            pe.wait_ge(S.inner_ready, 2 * L + step + 1)
            nc.tensor.matmul(turn_ps[1][:, step * B:(step + 1) * B], s.wsum_T[:, LAYERS + step].rearrange("i two o -> i (two o)"),
                             (s.bias2, s.inner)[step][0:C, :], start=True, stop=True).then_inc(S.inner_done, 1)

        UP_PARTS = [(6, slice(0, 2), slice(4, 8, 3)), (7, slice(0, 2), slice(0, 4, 3)),
                    (8, slice(0, 1), slice(6, 7)), (8, slice(1, 2), slice(5, 6)),
                    (9, slice(0, 1), slice(2, 3)), (9, slice(1, 2), slice(1, 2))]

        def up_part(w, i):
            tile, halves, _ = UP_PARTS[i]
            return w[:, tile, :].rearrange("p (f o) -> p f o", f=2)[:, halves, :]

        def turned_parts(s, hi):
            flat = lambda w: w.rearrange("p q m -> p (q m)")
            w1, f2, f3, w = (w1_hi, fold2_hi, fold3_hi, s.w_hi) if hi else (w1_lo, fold2_lo, fold3_lo, s.w_lo)
            pairs = [(flat(w1[:, :, :]), conv_ps[0][:, 0:2 * P]), (flat(f2[:, 0:4, :]), conv_ps[1][:, :]), (f2[:, 4, :], fold_ps[1][:, 2 * P:3 * P]),
                     (flat(f3[:, :, :]), s.same3[:, :, :].rearrange("p j i -> p (j i)")),
                     (flat(w[:, 0:2, :]), conv_ps[0][:, 2 * P:4 * P]), (flat(w[:, 2:6, :]), fold_ps[0][:, :])]
            return pairs + [(up_part(w, i), s.up[:, UP_PARTS[i][2], :]) for i in range(len(UP_PARTS))]

        def setup_scalar(act, L, s):
            n = L + 1
            act.wait_ge(S.images_ready, n)
            act.wait_ge(S.images_turned, n)
            for out, whole in turned_parts(s, True):
                last = nc.scalar.activation(out, whole, ACT.Identity)
            last.then_inc(S.tiles_hi, 1)
            act.wait_ge(S.squares_done, n)
            act.wait_ge(S.ident_ready, 2)
            nc.scalar.activation(s.root[:, :], turn_ps[0][:, 256:256 + LAYERS * B], ACT.Sqrt, bias=eps_col[:, 0:1],
                                 scale=SCALE * SCALE).then_inc(S.root_ready, 1)

        def setup_clear(V, s):
            for b in [s.same[0], s.same[1], s.down, s.up, s.same3] + s.blur[0:2] + s.blur_d[0:2] + s.edge[0:2]:
                V.memset(b[:, :, :], 0.0) if len(b.shape) == 3 else V.memset(b[:, :, :, :], 0.0)
            V.memset(s.x_edge[:, :, :, :], 0.0).then_inc(S.edges_clear, 1)

        def images_vector(v, L, s):
            n = L + 1
            V = nc.vector
            v.wait_ge(S.edges_clear, n)
            v.wait_ge(S.small_loaded, SMALL * n)
            taps = lambda l, k, rows=slice(0, C): s.w[rows, l, :].rearrange("o (i k) -> o k i", k=TAPS)[:, k, :]
            for i, l in ((0, 0), (1, 2)):
                for k in range(TAPS):
                    V.tensor_scalar(s.same[i][:, 3 - k, :], taps(l, k), SCALE, None, ALU.mult)
            for k in range(TAPS):
                V.tensor_scalar(s.same3[0:C, k, :], taps(2, k), SCALE, None, ALU.mult)
                V.tensor_scalar(s.same3[C:P, k + 1, :], taps(2, k, slice(C, P)), SCALE, None, ALU.mult)
                V.tensor_scalar(s.blur_d[0][:, 1 + k, :], taps(3, k), SCALE / 8, None, ALU.mult)
                last = V.tensor_scalar(s.blur[0][:, 1 + k, :], taps(1, k, slice(0, P)), SCALE / 4, None, ALU.mult)
            link(v, last)
            for i in range(2):
                V.tensor_tensor(s.blur_d[i + 1][:, 1:5 + i, :], s.blur_d[i][:, 1:5 + i, :], s.blur_d[i][:, 0:4 + i, :], ALU.add)
                link(v, V.tensor_tensor(s.blur[i + 1][:, 1:5 + i, :], s.blur[i][:, 1:5 + i, :], s.blur[i][:, 0:4 + i, :], ALU.add))
            V.tensor_tensor(s.down[:, 2:8, :], s.blur_d[2][:, 1:7, :], s.blur_d[2][:, 0:6, :], ALU.add)
            V.tensor_tensor(s.up[0:C, 2:8, :], s.blur[2][0:C, 1:7, :], s.blur[2][0:C, 0:6, :], ALU.add)
            V.tensor_tensor(s.up[C:P, 0:6, :], s.blur[2][C:P, 1:7, :], s.blur[2][C:P, 0:6, :], ALU.add).then_inc(S.images_ready, 1)
            link(v, V.tensor_tensor(s.wsq[:, :, :], s.w[0:C], s.w[0:C], ALU.mult))
            taps_inside = lambda ap: ap.rearrange("o l (i k) -> o (l i) k", k=TAPS)
            V.tensor_reduce(s.wsum[:, 0:LAYERS, :].rearrange("o l i -> o (l i)"), taps_inside(s.wsq[:, :, :]), AX.X, ALU.add)
            V.tensor_reduce(s.wsum[:, LAYERS:, :].rearrange("o l i -> o (l i)"), taps_inside(s.w[0:C, 2:4]), AX.X, ALU.add).then_inc(S.sums_ready, 1)
            v.wait_ge(S.style_turned, n)
            V.tensor_copy(s.style_T[:, :], turn_ps[0][:, 0:B])
            for half in range(2):
                last = V.tensor_copy(s.mod_wT[:, :, half, :], turn_ps[1][:, 0:LAYERS * C].rearrange("k (l i) -> k l i", l=LAYERS))
            last.then_inc(S.style_T_ready, 1)

        def setup_vector(v, L, s):
            n = L + 1
            V = nc.vector
            v.wait_ge(S.sums_turned, n)
            v.wait_ge(S.style_done, n)
            for first, end in ((0, LAYERS), (LAYERS, LAYERS + 2)):
                for half in range(2):
                    V.tensor_copy(s.wsum_T[:, first:end, half, :], sums_turned(first, end).rearrange("i (l o) -> i l o", o=C))
            for l in range(LAYERS):
                last = V.tensor_scalar(style_tab[:, l, :], turn_ps[0][:, 64 + l * B:64 + (l + 1) * B], s.mod_b[:, l:l + 1], None, ALU.add)
            link(v, last)
            V.tensor_tensor(s.style_sq[:, :, :], style_tab[:, :, :], style_tab[:, :, :], ALU.mult).then_inc(S.style_sq_ready, 1)
            v.wait_ge(S.tiles_hi, n)
            V.tensor_copy(down_T[:, :, :].rearrange("p q i -> p (q i)"), fold_ps[1][:, 0:DOWN_PAIRS * C])
            for (out, whole), (hi, _) in zip(turned_parts(s, False), turned_parts(s, True)):
                last = low(out, whole, hi)
            last.then_inc(S.tiles_ready, 1)

        def tables_vector(v, L, s):
            n = L + 1
            V = nc.vector
            v.wait_ge(S.root_ready, n)
            demod = demod_tab[:, :, :].rearrange("o l b -> o (l b)")
            V.tensor_scalar(s.var[:, :], turn_ps[0][:, 256:256 + LAYERS * B], SCALE * SCALE, EPS, ALU.mult, ALU.add)
            link(v, V.reciprocal(demod, s.root[:, :]))
            link(v, V.tensor_tensor(s.newton[:, :], demod, demod, ALU.mult))
            link(v, V.tensor_tensor(s.newton[:, :], s.newton[:, :], s.var[:, :], ALU.mult))
            link(v, V.tensor_scalar(s.newton[:, :], s.newton[:, :], -0.5, 1.5, ALU.mult, ALU.add))
            link(v, V.tensor_tensor(demod, demod, s.newton[:, :], ALU.mult))
            st, de = (lambda l: style_tab[:, l, :]), (lambda l: demod_tab[:, l, :])
            bi = lambda l: bias_tab[:, l:l + 1]
            V.tensor_tensor(scale1[:, :], de(0), de(1), ALU.mult)
            V.tensor_scalar(bias1[:, :], de(1), bi(0), None, ALU.mult)
            V.tensor_tensor(scale2[:, :], st(1), st(2), ALU.mult)
            V.tensor_scalar(s.bias2[:, :], st(2), bi(1), 2.0, ALU.mult, ALU.mult)
            V.tensor_scalar(s.edge2[:, :], st(2), bi(1), -0.25, ALU.mult, ALU.mult)
            V.tensor_tensor(scale3[:, :], de(2), st(3), ALU.mult)
            V.tensor_scalar(s.bias3[:, :], st(3), bi(2), None, ALU.mult).then_inc(S.tables_ready, 1)
            v.wait_ge(S.tables_ready, n)
            v.sem_inc(S.inner_ready, 1)

        def inner_vector(v, L, s, step):
            V = nc.vector
            v.wait_ge(S.inner_done, 2 * L + step + 1)
            if step == 0:
                link(v, V.tensor_tensor(s.inner[:, :], turn_ps[1][:, 0:B], scale3[:, :], ALU.mult))
                V.scalar_tensor_tensor(out=s.inner[:, :], in0=s.inner[:, :], scalar=SCALE, in1=s.bias3[:, :], op0=ALU.mult, op1=ALU.add).then_inc(S.inner_ready, 1)
            else:
                link(v, V.scalar_tensor_tensor(out=bias4[:, :], in0=turn_ps[1][:, B:2 * B], scalar=SCALE, in1=demod_tab[:, 3, :], op0=ALU.mult, op1=ALU.mult))
                V.tensor_scalar(bias4[:, :], bias4[:, :], bias_tab[:, 3:4], None, ALU.add).then_inc(S.bias4_ready, 1)

        def edge_tensor(pe, L, s, layer):
            flat = lambda ap: ap.rearrange("p s j b -> p s (j b)")
            part = lambda w, k, j: (lambda i: flat(w[k][:, :, i:i + j, :]))
            sides = lambda ps, j: ps[:, 0:2 * j * B].rearrange("p (s j) -> p s j", s=2)
            pe.wait_ge(S.edge_ready, 4 * L + layer + 1)
            if layer == 0:
                last = products(sides(prod_ps[0], 3), (0, 1), w1_hi, w1_lo, part(s.edge_hi, 0, 3), part(s.edge_lo, 0, 3))
            elif layer == 1:
                for m in range(2):
                    last = products(sides(prod_ps[m], 2), (6 + 2 * m, 7 + 2 * m), s.w_hi, s.w_lo, part(s.edge_hi, 1, 2), part(s.edge_lo, 1, 2))
            elif layer == 2:
                last = products(sides(prod_ps[0], 3), (0, 1), s.w_hi, s.w_lo, part(s.edge_hi, 2, 3), part(s.edge_lo, 2, 3))
            else:
                for side in range(2):
                    one = lambda w: (lambda i: w[3][:, side, i, :])
                    last = products(prod_ps[1][:, side * B:(side + 1) * B], (3 - side, 4 - side, 5 - side), s.w_hi, s.w_lo, one(s.edge_hi), one(s.edge_lo))
            last.then_inc(S.edge_done, 1)

        def edge_vector(v, L, s, step):
            V = nc.vector
            lo_half, hi_half = slice(0, C), slice(C, P)

            def wide(tab, like, rows=slice(0, P)):
                return tab[rows, :].unsqueeze(1).broadcast_to([rows.stop - rows.start, like, B])

            def parts(k):
                everything = lambda w: w[k][:, :, :, :].rearrange("p s j b -> p (s j b)")
                link(v, V.tensor_copy(everything(s.edge_hi), everything(s.edge)))
                low(everything(s.edge_lo), everything(s.edge), everything(s.edge_hi)).then_inc(S.edge_ready, 1)

            if step == 0:
                v.wait_ge(S.edges_loaded, EDGES * (1 + 2 * L))
                for side in range(2):
                    last = V.tensor_tensor(s.edge[0][:, side, :, :], s.x_edge[:, side, :, 0:8].rearrange("p b (j two) -> p j two b", two=2)[:, :, 0, :],
                                           wide(style_tab[:, 0, :], 4), ALU.mult)
                link(v, last)
                parts(0)
            if step == 1:
                v.wait_ge(S.edge_done, 4 * L + 1)
                link(v, V.tensor_tensor(s.scaled[:, :, :, :].rearrange("p s j b -> p (s j) b"), prod_ps[0][:, 0:6 * B].rearrange("p (j b) -> p j b", b=B),
                                        wide(scale1, 6), ALU.mult))
                for side, rows, src, dst in ((0, lo_half, slice(0, 3), slice(0, 3)), (0, hi_half, slice(0, 2), slice(1, 3)),
                                             (1, lo_half, slice(1, 3), slice(0, 2)), (1, hi_half, slice(0, 3), slice(0, 3))):
                    last = V.tensor_tensor(s.edge[1][rows, side, dst, :], s.scaled[rows, side, src, :], wide(bias1, src.stop - src.start, rows), ALU.add)
                link(v, last)
                parts(1)
            if step == 2:
                v.wait_ge(S.edge_done, 4 * L + 2)
                link(v, V.memset(s.edge[2][:, :, :, :], 0.0))
                for m in range(2):
                    four = s.scaled[:, :, 0:2, :]
                    for side in range(2):
                        last = V.tensor_tensor(four[:, side, :, :], prod_ps[m][:, side * 2 * B:(side + 1) * 2 * B].rearrange("p (j b) -> p j b", b=B), wide(scale2, 2), ALU.mult)
                    link(v, last)
                    moves = [((0, lo_half, slice(0, 2), slice(0, 3, 2)), (0, hi_half, slice(0, 1), slice(2, 3)),
                              (1, lo_half, slice(1, 2), slice(1, 2)), (1, hi_half, slice(0, 2), slice(1, 4, 2))),
                             ((0, slice(0, P), slice(0, 2), slice(1, 4, 2)), (1, slice(0, P), slice(0, 2), slice(0, 3, 2)))][m]
                    for side, rows, src, dst in moves:
                        last = V.tensor_tensor(s.edge[2][rows, side, dst, :], s.scaled[rows, side, src, :], wide(s.bias2, src.stop - src.start, rows), ALU.add)
                    link(v, last)
                V.tensor_tensor(s.edge[2][lo_half, 0, 0, :], s.edge[2][lo_half, 0, 0, :], s.edge2[lo_half, :], ALU.add)
                link(v, V.tensor_tensor(s.edge[2][hi_half, 1, 3, :], s.edge[2][hi_half, 1, 3, :], s.edge2[hi_half, :], ALU.add))
                parts(2)
            if step == 3:
                v.wait_ge(S.edge_done, 4 * L + 3)
                six = lambda ap: ap[:, :, :, :].rearrange("p s j b -> p (s j) b")
                link(v, V.tensor_tensor(six(s.scaled), prod_ps[0][:, 0:6 * B].rearrange("p (j b) -> p j b", b=B), wide(scale3, 6), ALU.mult))
                link(v, V.tensor_tensor(six(s.edge[3]), six(s.scaled), wide(s.bias3, 6), ALU.add))
                parts(3)
            if step == 4:
                v.wait_ge(S.edge_done, 4 * L + 4)
                link(v, V.tensor_tensor(cond_edge[:, :, :], prod_ps[1][:, 0:2 * B].rearrange("p (s b) -> p s b", s=2), wide(demod_tab[:, 3, :], 2), ALU.mult))
                V.tensor_scalar(cond_edge[:, :, :], cond_edge[:, :, :], bias_tab[:, 3:4], None, ALU.add).then_inc(S.edges_done, 1)

        def at(tab, c, a, bufs):
            n = 2 * c + a - bufs.first_sample
            return tab[:, n:n + 1] if isinstance(n, int) else tab[:, bass.ds(n, 1)]

        def conv_buffers(stack, L):
            T = lambda n, s, d=F32R: tensor(stack, f"L{L}_{n}", s, d)
            b = Buffers()
            b.first_sample = B * L
            b.x_hi, b.x_lo = [T(f"x_hi{a}", [P, H + 1]) for a in range(2)], [T(f"x_lo{a}", [P, H + 1]) for a in range(2)]
            b.h_hi, b.h_lo = [T(f"h_hi{a}", [P, H + 3]) for a in range(2)], [T(f"h_lo{a}", [P, H + 3]) for a in range(2)]
            b.v_hi, b.v_lo = T("v_hi", [P, DOWN_PAIRS, 2, C]), T("v_lo", [P, DOWN_PAIRS, 2, C])
            b.r_hi, b.r_lo = T("r_hi", [P, R_PAIRS, 2, C]), T("r_lo", [P, R_PAIRS, 2, C])
            b.e_hi, b.e_lo = T("e_hi", [P, E_PAIRS, 2, P]), T("e_lo", [P, E_PAIRS, 2, P])
            return b

        def act_fold_start(act, c, bufs, first=False):
            if not first:
                act.wait_ge(S.fold3_done, c)
                act.nop(nofuse=True)
            for a in range(2):
                nc.scalar.activation(bufs.v_hi[:, :, a, :], down_T[:, :, :], ACT.Identity, scale=at(scale3, c, a, bufs)).then_inc(S.fold_in_hi, 1)

        def dve_fold_start(v, c, bufs):
            for a in range(2):
                v.wait_ge(S.fold_in_hi, 2 * c + a + 1)
                nc.vector.scalar_tensor_tensor(out=bufs.v_lo[:, :, a, :], in0=down_T[:, :, :], scalar=at(scale3, c, a, bufs),
                                               in1=bufs.v_hi[:, :, a, :].bitcast(F32), op0=ALU.mult, op1=ALU.subtract).then_inc(S.fold_in_ready, 1)

        def pe_fold3(pe, c, bufs, first=False):
            pe.wait_ge(S.fold_in_ready, 2 * c + 2)
            if not first:
                pe.wait_ge(S.fold3_ready, 2 * c)
            flat = lambda w: w[:, :, :, :].rearrange("p q a i -> p (q a i)")
            hi, lo = flat(bufs.v_hi), flat(bufs.v_lo)
            for n, first_block in enumerate((1, 0)):
                out = fold_ps[0][:, first_block * P:(first_block + DOWN_PAIRS) * P]
                for i, (w, v) in enumerate(((fold3_hi, hi), (fold3_hi, lo), (fold3_lo, hi))):
                    last = nc.tensor.matmul(out, w[:, n, :], v, start=(n == 0 and i == 0), stop=(n == 1 and i == 2), skip_group_check=True)
            last.then_inc(S.fold3_done, 1)

        def fold3_out(a):
            return fold_ps[0][:, :].rearrange("p (m a i) -> p m a i", m=R_PAIRS, a=2)[:, :, a, :]

        def act_fold3(act, c, bufs, first=False):
            act.wait_ge(S.fold3_done, c + 1)
            if not first:
                act.wait_ge(S.fold2_done, c)
            act.nop(nofuse=True)
            for a in range(2):
                nc.scalar.activation(bufs.r_hi[:, :, a, :], fold3_out(a), ACT.Identity, scale=at(scale2, c, a, bufs)).then_inc(S.fold3_hi, 1)

        def dve_fold3(v, c, bufs):
            v.wait_ge(S.fold3_hi, 2 * c + 2)
            for a in range(2):
                nc.vector.scalar_tensor_tensor(out=bufs.r_lo[:, :, a, :], in0=fold3_out(a), scalar=at(scale2, c, a, bufs),
                                               in1=bufs.r_hi[:, :, a, :].bitcast(F32), op0=ALU.mult, op1=ALU.subtract).then_inc(S.fold3_ready, 1)

        FOLD2 = [(0, 0, 0), (2, 0, 1), (4, 0, 2), (1, 1, 1), (3, 1, 2)]

        def pe_fold2(pe, c, bufs, first=False):
            pe.wait_ge(S.fold3_ready, 2 * c + 2)
            if not first:
                pe.wait_ge(S.fold2_hi, 2 * c)
                pe.wait_ge(S.fold2_ready, c)
            for n, (tile, m, block) in enumerate(FOLD2):
                out = fold_ps[1][:, block * P:(block + 2) * P]
                for i, (w, r) in enumerate(((fold2_hi, bufs.r_hi), (fold2_hi, bufs.r_lo), (fold2_lo, bufs.r_hi))):
                    last = nc.tensor.matmul(out, w[:, tile, :], r[:, m:R_PAIRS:2, :, :], start=(n == 0 and i == 0),
                                            stop=(n == len(FOLD2) - 1 and i == 2), skip_group_check=True)
            last.then_inc(S.fold2_done, 1)

        def act_fold2(act, c, bufs, first=False):
            act.wait_ge(S.fold2_done, c + 1)
            if not first:
                act.wait_ge(S.cond_done, 2 * c)
            flat = lambda ap: ap.rearrange("p q a m -> p (q a) m")
            blocks = fold_ps[1][:, :].rearrange("p (q o) -> p q o", o=C)
            hi = bufs.e_hi
            nc.scalar.activation(flat(hi[:, :, :, 0:C]), blocks, ACT.Identity).then_inc(S.fold2_hi, 1)
            act.wait_ge(S.fold2_hi, 2 * c + 1)
            nc.scalar.activation(flat(hi[0:C, :, :, C:P]), flat(hi[C:P, :, :, 0:C]).bitcast(F32), ACT.Identity)
            nc.scalar.activation(flat(hi[C:P, 0:E_PAIRS - 1, :, C:P]), flat(hi[0:C, 1:E_PAIRS, :, 0:C]).bitcast(F32), ACT.Identity).then_inc(S.fold2_hi, 1)

        def dve_fold2(v, c, bufs):
            flat = lambda ap: ap.rearrange("p q a m -> p (q a) m")
            blocks = fold_ps[1][:, :].rearrange("p (q o) -> p q o", o=C)
            v.wait_ge(S.fold2_hi, 2 * c + 1)
            lo = bufs.e_lo
            low(flat(lo[:, :, :, 0:C]), blocks, flat(bufs.e_hi[:, :, :, 0:C])).then_inc(S.fold2_lo, 1)
            v.wait_ge(S.fold2_lo, c + 1)
            nc.vector.tensor_copy(flat(lo[0:C, :, :, C:P]), flat(lo[C:P, :, :, 0:C]).bitcast(F32))
            nc.vector.tensor_copy(flat(lo[C:P, 0:E_PAIRS - 1, :, C:P]), flat(lo[0:C, 1:E_PAIRS, :, 0:C]).bitcast(F32)).then_inc(S.fold2_ready, 1)

        def dve_split(v, c, a, bufs, first=False):
            v.wait_ge((S.xin_loaded0, S.xin_loaded1)[a], 32 * (c + 1))
            if not first:
                v.wait_ge(S.layer1_done, 2 * c + a - 1)
            src = x_in[a][:, 0:D + 2].rearrange("p (j two) -> p two j", two=2)[:, 0, :]
            sc = at(style_tab[:, 0, :], c, a, bufs)
            nc.vector.tensor_scalar(bufs.x_hi[a][:, :], src, sc, None, ALU.mult).then_inc(S.xin_hi, 1)
            v.wait_ge(S.xin_hi, 2 * c + a + 1)
            nc.vector.scalar_tensor_tensor(out=bufs.x_lo[a][:, :], in0=src, scalar=sc, in1=bufs.x_hi[a][:, :].bitcast(F32),
                                           op0=ALU.mult, op1=ALU.subtract).then_inc(S.xin_split, 1)

        def pe_layer1(pe, c, a, bufs, first=False):
            pe.wait_ge(S.xin_split, 2 * c + a + 1)
            if not first:
                pe.wait_ge(S.cond_ready, 2 * c + a - 1)
            cut = lambda w: (lambda i: w[a][:, i:i + H])
            products(conv_ps[a][:, :], (0, 1), w1_hi, w1_lo, cut(bufs.x_hi), cut(bufs.x_lo)).then_inc(S.layer1_done, 1)

        def act_layer1(act, c, a, bufs):
            act.wait_ge(S.layer1_done, 2 * c + a + 1)
            act.nop(nofuse=True)
            ps, hi = conv_ps[a], bufs.h_hi[a]
            nc.scalar.activation(ps[:, :], ps[:, :], ACT.Identity, bias=at(bias1, c, a, bufs), scale=at(scale1, c, a, bufs)).then_inc(S.layer1_scaled, 1)
            act.wait_ge(S.layer1_scaled, 2 * c + a + 1)
            nc.scalar.activation(hi[0:C, 1:H + 1], ps[0:C, :], ACT.Identity)
            nc.scalar.activation(hi[C:P, 2:H + 2], ps[C:P, :], ACT.Identity).then_inc(S.layer1_hi, 1)

        def dve_layer1(v, c, a, bufs):
            v.wait_ge(S.layer1_hi, 2 * c + a + 1)
            low(bufs.h_lo[a][0:C, 1:H + 1], conv_ps[a][0:C, :], bufs.h_hi[a][0:C, 1:H + 1])
            low(bufs.h_lo[a][C:P, 2:H + 2], conv_ps[a][C:P, :], bufs.h_hi[a][C:P, 2:H + 2]).then_inc(S.layer1_ready, 1)

        def pe_cond(pe, c, a, bufs):
            if a == 0:
                pe.wait_ge(S.fold2_hi, 2 * c + 2)
                pe.wait_ge(S.fold2_ready, c + 1)
            pe.wait_ge(S.layer1_ready, 2 * c + a + 1)
            cut = lambda w: (lambda q: w[a][:, q:q + H])
            products(conv_ps[a][:, :], (3, 2, 1, 0), bufs.e_hi[:, :, a, :], bufs.e_lo[:, :, a, :], cut(bufs.h_hi), cut(bufs.h_lo)).then_inc(S.cond_done, 1)

        def act_cond(act, c, a, bufs):
            act.wait_ge(S.cond_done, 2 * c + a + 1)
            act.nop(nofuse=True)
            nc.scalar.activation(bufs.cond[:, a, 1:H - 1], conv_ps[a][:, 1:H - 1], ACT.Identity, bias=at(bias4, c, a, bufs),
                                 scale=at(demod_tab[:, LAYERS - 1, :], c, a, bufs))
            n = 2 * c + a - bufs.first_sample
            ends = cond_edge[:, :, n:n + 1] if isinstance(n, int) else cond_edge[:, :, bass.ds(n, 1)]
            nc.scalar.activation(bufs.cond[:, a, 0:H:H - 1], ends.rearrange("p s u -> p (s u)"), ACT.Identity).then_inc(S.cond_ready, 1)

        def dve_pads(v, bufs):
            for a in range(2):
                for w in (bufs.h_hi[a], bufs.h_lo[a]):
                    nc.vector.memset(w[0:C, 0:1].bitcast(F32), 0.0)
                    nc.vector.memset(w[0:C, H + 1:H + 3].bitcast(F32), 0.0)
                    nc.vector.memset(w[C:P, 0:2].bitcast(F32), 0.0)
                    nc.vector.memset(w[C:P, H + 2:H + 3].bitcast(F32), 0.0)
            for w in (bufs.e_hi, bufs.e_lo):
                nc.vector.memset(w[C:P, E_PAIRS - 1, :, C:P].bitcast(F32), 0.0)

        def pe_turn(pe, f, bufs, packed):
            for a in range(2):
                pe.wait_ge(S.cond_ready, 2 * f + a + 1)
                for j in range(4):
                    cols = slice(j, H, 4) if packed else slice(j * P, (j + 1) * P)
                    last = nc.tensor.transpose(turn_ps[a][:, j * P:(j + 1) * P], bufs.cond[:, a, cols], ident[:, :])
                last.then_inc(S.turned, 1)

        def act_turn(act, f, bufs):
            for a in range(2):
                act.wait_ge(S.turned, 2 * f + a + 1)
                nc.scalar.activation(bufs.xt_hi[:, :, a * C:(a + 1) * C], turn_ps[a][:, :].rearrange("p (k o) -> p k o", k=KT),
                                     ACT.Identity).then_inc(S.xt_hi, 1)

        def dve_turn(v, f, bufs):
            for a in range(2):
                v.wait_ge(S.xt_hi, 2 * f + a + 1)
                low(bufs.xt_lo[:, :, a * C:(a + 1) * C], turn_ps[a][:, :].rearrange("p (k o) -> p k o", k=KT),
                    bufs.xt_hi[:, :, a * C:(a + 1) * C]).then_inc(S.xt_ready, 1)

        def pe_scores(pe, f, bufs):
            pe.wait_ge(S.xt_ready, 2 * f + 2)
            for k in range(KT):
                last = nc.tensor.matmul(turn_ps[0][:, 0:2 * P], bufs.wr[:, k, :], bufs.xt[:, k, :, :], start=(k == 0), stop=(k == KT - 1))
            last.then_inc(S.partial_scores, 1)

        def act_scores(act, f, bufs):
            act.wait_ge(S.partial_scores, f + 1)
            act.wait_ge(S.scored, f + 1)
            nc.scalar.activation(bufs.score_parts[:, :], turn_ps[0][:, 0:2 * P], ACT.Identity).then_inc(S.parts_copied, 1)

        def pe_score_sum(pe, f, bufs):
            pe.wait_ge(S.parts_copied, f + 1)
            nc.tensor.matmul(turn_ps[1][:, 0:NE], bufs.score_parts[:, 0:P], spread[:, 1, :], start=True, stop=False)
            nc.tensor.matmul(turn_ps[1][:, 0:NE], bufs.score_parts[0:NE, P:2 * P], spread[0:NE, 1, :], start=False, stop=True).then_inc(S.scored, 1)

        def pe_hidden(pe, f, n, bufs):
            if n == 0:
                pe.wait_ge(S.x1_ready, 2 * f + 1)
            cols = slice(n * 512, (n + 1) * 512)
            for k in range(KT):
                nc.tensor.matmul(prod_ps[n][:, :], bufs.xt_hi[:, k, :], bufs.a_hi[:, k, cols], start=(k == 0), stop=False)
                nc.tensor.matmul(prod_ps[n][:, :], bufs.xt_hi[:, k, :], bufs.a_lo[:, k, cols], start=False, stop=False)
                last = nc.tensor.matmul(prod_ps[n][:, :], bufs.xt_lo[:, k, :], bufs.a_hi[:, k, cols], start=False, stop=(k == KT - 1))
            last.then_inc(S.hidden_done, 1)

        def pe_gated_turn(pe, f, bufs):
            for n in range(2):
                pe.wait_ge(S.gated, 2 * f + n + 1)
                for j in range(4):
                    last = nc.tensor.transpose(turn_ps[n][:, j * P:(j + 1) * P], bufs.gated[:, n * 512 + j * P:n * 512 + (j + 1) * P], ident[:, :])
                last.then_inc(S.gated_turned, 1)

        def pe_adapter_out(pe, f, bufs, n):
            pe.wait_ge(S.hgt_ready, 2 * f + 2)
            cols = slice(n * 512, (n + 1) * 512)
            for k in range(KT):
                nc.tensor.matmul(prod_ps[n][:, :], bufs.xt_hi[:, k, :], bufs.b_hi[:, k, cols], start=(k == 0), stop=False)
                nc.tensor.matmul(prod_ps[n][:, :], bufs.xt_hi[:, k, :], bufs.b_lo[:, k, cols], start=False, stop=False)
                last = nc.tensor.matmul(prod_ps[n][:, :], bufs.xt_lo[:, k, :], bufs.b_hi[:, k, cols], start=False, stop=(k == KT - 1))
            last.then_inc(S.out_done, 1)

        def act_exp(act, f, bufs):
            act.wait_ge(S.top_max, f + 1)
            nc.scalar.activation(bufs.gate_exp[:, :], bufs.scores[:, :], ACT.Exp, bias=bufs.neg_max[:, 0:1]).then_inc(S.exp_ready, 1)

        def act_gated_turn(act, f, bufs):
            for n in range(2):
                act.wait_ge(S.gated_turned, 2 * f + n + 1)
                nc.scalar.activation(bufs.xt_hi[:, 4 * n:4 * n + 4, :], turn_ps[n][:, :].rearrange("p (k o) -> p k o", k=4),
                                     ACT.Identity).then_inc(S.hgt_hi, 1)

        TOP_STEPS = 9

        def dve_route(v, f, bufs):
            V = nc.vector
            n = [0]

            def step(ins):
                n[0] += 1
                ins.then_inc(S.tail, 1)
                v.wait_ge(S.tail, TOP_STEPS * f + n[0])
                v.nop(nofuse=True)

            v.wait_ge(S.scored, f + 2)
            step(V.tensor_copy(bufs.scores[:, :], turn_ps[1][:, 0:NE]))
            step(V.max(bufs.top[:, 0:8], bufs.scores[:, :]))
            V.tensor_scalar(bufs.neg_max[:, :], bufs.top[:, 0:1], -1.0, None, ALU.mult).then_inc(S.top_max, 1)
            step(V.match_replace(bufs.rest[:, :], bufs.top[:, 0:8], bufs.scores[:, :], LOWEST))
            step(V.max(bufs.top[:, 8:16], bufs.rest[:, :]))
            step(V.match_replace(bufs.rest2[:, :], bufs.top[:, 8:16], bufs.rest[:, :], LOWEST))
            step(V.tensor_tensor(bufs.chosen[:, :], bufs.rest2[:, :], bufs.scores[:, :], ALU.is_lt))
            v.wait_ge(S.exp_ready, f + 1)
            step(V.tensor_tensor(bufs.gate[:, :], bufs.gate_exp[:, :], bufs.chosen[:, :], ALU.mult))
            step(V.tensor_reduce(bufs.norm[:, 0:1], bufs.gate[:, :], AX.X, ALU.add))
            step(V.reciprocal(bufs.norm[:, 1:2], bufs.norm[:, 0:1]))
            V.tensor_scalar(bufs.norm[:, 2:3], bufs.norm[:, 1:2], LORA_SCALE, None, ALU.mult)

        def dve_gate(v, f, n, bufs):
            v.wait_ge(S.hidden_done, 2 * f + n + 1)
            by_rank = lambda ap: ap.rearrange("p (r k) -> p r k", k=NE)
            nc.vector.tensor_tensor(by_rank(bufs.gated[:, n * 512:(n + 1) * 512]), by_rank(prod_ps[n][:, :]),
                                    bufs.gate[:, :].unsqueeze(1).broadcast_to([P, RANK // 2, NE]), ALU.mult).then_inc(S.gated, 1)

        def dve_gated_turn(v, f, bufs):
            for n in range(2):
                v.wait_ge(S.hgt_hi, 2 * f + n + 1)
                low(bufs.xt_lo[:, 4 * n:4 * n + 4, :], turn_ps[n][:, :].rearrange("p (k o) -> p k o", k=4),
                    bufs.xt_hi[:, 4 * n:4 * n + 4, :]).then_inc(S.hgt_ready, 1)

        def dve_first_residual(v, f, bufs):
            v.wait_ge(S.res_loaded, 16 * (f + 1))
            for n in range(2):
                cols = slice(n * 512, (n + 1) * 512)
                v.wait_ge(S.out_done, 2 * f + n + 1)
                nc.vector.scalar_tensor_tensor(out=bufs.res[:, cols], in0=prod_ps[n][:, :], scalar=bufs.norm[:, 2:3], in1=bufs.res[:, cols],
                                               op0=ALU.mult, op1=ALU.add).then_inc(S.x1_ready, 1)

        def pe_rowsum(pe, f, bufs):
            pe.wait_ge(S.sums_reduced, f - NPAIR + 1)
            for a in range(2):
                to_rows = spread[:, 1 - a:3 - a, :].rearrange("p t o -> p (t o)")
                last = nc.tensor.matmul(turn_ps[0][:, 0:1], to_rows, bufs.sums[:, a:a + 1], start=(a == 0), stop=(a == 1))
            last.then_inc(S.rowsum_done, 1)

        def dve_reduce(v, f, bufs):
            v.wait_ge(S.cond_ready, 2 * f + 2)
            nc.vector.tensor_reduce(bufs.sums[:, :], bufs.cond[:, :, :], AX.X, ALU.add).then_inc(S.sums_reduced, 1)

        def pe_quant(pe, f, n, bufs):
            if n == 0:
                pe.wait_ge(S.xt_ready, 2 * f + 2)
                pe.wait_ge(S.x1_ready, 2 * f + 1)
            cols = slice(n * 512, (n + 1) * 512)
            for k in range(KT):
                nc.tensor.matmul(prod_ps[n][:, :], bufs.xt_hi[:, k, :], bufs.quant[:, k, cols], start=(k == 0), stop=False)
                last = nc.tensor.matmul(prod_ps[n][:, :], bufs.xt_lo[:, k, :], bufs.quant[:, k, cols], start=False, stop=(k == KT - 1))
            last.then_inc(S.out_done, 1)

        def dve_rowsum(v, f, bufs):
            v.wait_ge(S.rowsum_done, f - NPAIR + 1)
            nc.vector.tensor_scalar(bufs.neg_sum[:, :], turn_ps[0][:, 0:1], -1.0, None, ALU.mult).then_inc(S.rowsum_read, 1)

        def dve_second_residual(v, f, bufs, last=False):
            g = f - NPAIR
            halves = [slice(n * 512, (n + 1) * 512) for n in range(2)]
            v.wait_ge(S.biased, g + 1)
            v.wait_ge(S.rowsum_read, g + 2)
            for cols in halves:
                nc.vector.scalar_tensor_tensor(out=bufs.res[:, cols], in0=bufs.zeros[:, cols], scalar=bufs.neg_sum[:, 0:1], in1=bufs.res[:, cols],
                                               op0=ALU.mult, op1=ALU.add)
            for n, cols in enumerate(halves):
                v.wait_ge(S.out_done, 2 * f + n + 1)
                nc.vector.tensor_tensor(bufs.scaled[:, cols], prod_ps[n][:, :], bufs.scales[:, cols], ALU.mult).then_inc(S.x1_ready, 1)
                if last:
                    v.wait_ge(S.x1_ready, 2 * f + n + 2)
                    nc.vector.tensor_tensor(bufs.res[:, cols], bufs.res[:, cols], bufs.scaled[:, cols], ALU.add).then_inc(S.y_ready, 1)
            if not last:
                v.wait_ge(S.x1_ready, 2 * f + 3)
                nc.vector.tensor_tensor(bufs.res[:, :], bufs.res[:, :], bufs.scaled[:, :], ALU.add).then_inc(S.y_ready, 1)

        level0 = ExitStack()
        buf0 = conv_buffers(level0, 0)
        T0 = lambda n, s, d=F32: tensor(level0, n, s, d)
        A_RING, B_RING, B_COLS = 4, 3, D // RANK
        B_CHUNKS = D // B_COLS
        with ExitStack() as stage:
            set0 = setup_buffers(stage, 0, setup_inputs(stage, 0))
            b_nat = tensor(stage, "b_nat", [P, B_RING, B_COLS * RANK + 2], F32)
        buf0.wr = T0("wr", [P, KT, 2 * NE], F32R)
        buf0.a_hi, buf0.a_lo = T0("a_hi", [P, KT, KR], F32R), T0("a_lo", [P, KT, KR], F32R)
        buf0.scores, buf0.rest, buf0.rest2, buf0.chosen = T0("scores", [P, NE]), T0("rest", [P, NE]), T0("rest2", [P, NE]), T0("chosen", [P, NE])
        buf0.gate_exp, buf0.gate, buf0.top = T0("gate_exp", [P, NE]), T0("gate", [P, NE]), T0("top", [P, 2 * 8])
        buf0.neg_max, buf0.norm = T0("neg_max", [P, 1]), T0("norm", [P, 3])
        buf0.cond = T0("cond0", [P, 2, H])
        buf0.b_hi, buf0.b_lo = T0("b_hi", [P, KT, D], F32R), T0("b_lo", [P, KT, D], F32R)
        with ExitStack() as stage:
            a_nat = tensor(stage, "a_nat", [P, A_RING, D], F32)
            wr_nat = a_nat[0:NE, A_RING - 1, :]
        buf0.xt, buf0.res = T0("xt0", [P, KT, 2, P], F32R), T0("res0", [P, D])
        buf0.xt_hi, buf0.xt_lo = buf0.xt[:, :, 0, :], buf0.xt[:, :, 1, :]
        loaded1 = setup_inputs(level0, 1)
        buf0.gated, buf0.score_parts = buf0.cond[:, :, :].rearrange("p a h -> p (a h)"), buf0.cond[:, 0, 0:2 * P]
        level0.close()

        level1 = ExitStack()
        T1 = lambda n, s, d=F32: tensor(level1, n, s, d)
        buf1 = conv_buffers(level1, 1)
        set1 = setup_buffers(level1, 1, loaded1)
        packed, nibble = T1("packed", [P, D], I32), [T1(f"nibble{i}", [P, D], I32) for i in range(2)]
        buf1.sums, buf1.neg_sum = T1("sums", [P, 2]), T1("neg_sum", [P, 1])
        buf1.quant = T1("quant", [P, KT, D], F32R)
        buf1.scales, buf1.zeros, buf1.bias = T1("scales", [P, D]), T1("zeros", [P, D]), T1("bias", [P, D])
        buf1.scaled, buf1.cond, buf1.res = T1("scaled", [P, D]), T1("cond1", [P, 2, H]), T1("res1", [P, D])
        buf1.xt_hi, buf1.xt_lo = T1("xt_hi1", [P, KT, P], F32R), T1("xt_lo1", [P, KT, P], F32R)
        level1.close()

        a_src, b_src = t["L0_ffn_A"].rearrange("k r d -> r k d"), t["L0_ffn_B"].rearrange("k (c d) r -> c k (d r)", d=B_COLS)
        group_ps = [fold_ps[0], fold_ps[1], prod_ps[0], prod_ps[1]]
        TURNS = (0, 5, 1 + 2 * KT)
        GROUPS = [("r", 0, 0)] + [("a", g, h) for g in range(KT) for h in range(2)]
        position = lambda k: slice(2 * P * (k // 2) + k % 2, 2 * P * (k // 2 + 1), 2)

        def group_out(n, hi):
            kind, g, h = GROUPS[n]
            if kind == "r":
                return buf0.wr[:, :, 0:NE] if hi else buf0.wr[:, :, NE:2 * NE]
            return (buf0.a_hi if hi else buf0.a_lo)[:, 4 * h:4 * h + 4, g * P:(g + 1) * P]

        def group_in(n):
            kind = GROUPS[n][0]
            return group_ps[n % 4][:, :].rearrange("p (k e) -> p k e", k=KT if kind == "r" else 4)

        def pe_turn_weights(pe, first, end):
            for n in range(first, end):
                kind, g, h = GROUPS[n]
                if n >= 4:
                    pe.wait_ge(S.weights_lo, n - 3)
                if kind == "r":
                    pe.wait_ge(S.router_loaded, 16)
                elif h == 0:
                    pe.wait_ge(S.a_loaded[g % A_RING], 32 * (g // A_RING + 1))
                ps = group_ps[n % 4]
                if kind == "r":
                    for k in range(KT):
                        last = nc.tensor.transpose(ps[:, k * NE:(k + 1) * NE], wr_nat[:, position(k)], ident[0:NE, 0:NE])
                else:
                    for j in range(4):
                        last = nc.tensor.transpose(ps[:, j * P:(j + 1) * P], a_nat[:, g % A_RING, position(4 * h + j)], ident[:, :])
                last.then_inc(S.weights_turned, 1)

        def b_chunk(g):
            return b_nat[:, g % B_RING, 1:B_COLS * RANK + 1].rearrange("p (d m two) -> p m d two", d=B_COLS, two=2)[:, :, :, 0]

        def sp_b_chunks(sp, first, end):
            for g in range(first, end):
                if g >= B_RING:
                    sp.wait_ge(S.b_lo_ready, g - B_RING + 1)
                sp.dma_start(b_nat[0:NE, g % B_RING, 1:B_COLS * RANK + 1], b_src[g]).then_inc(S.b_loaded[g % B_RING], 16)
                sp.dma_start(b_nat[NE:P, g % B_RING, 0:B_COLS * RANK], b_src[g]).then_inc(S.b_loaded[g % B_RING], 16)

        def act_b_chunks(act, first, end):
            for g in range(first, end):
                act.wait_ge(S.b_loaded[g % B_RING], 32 * (g // B_RING + 1))
                nc.scalar.activation(buf0.b_hi[:, :, g * B_COLS:(g + 1) * B_COLS], b_chunk(g), ACT.Identity).then_inc(S.b_hi_ready, 1)

        def dve_nibbles(v, first, end):
            for k in range(first, end):
                if k >= 2:
                    v.wait_ge(S.quant_ready, k - 1)
                nc.vector.tensor_scalar(nibble[k % 2][:, :], packed[:, :], 4 * k, 15, ALU.logical_shift_right, ALU.bitwise_and).then_inc(S.nibble_ready, 1)

        def act_nibbles(act, first, end):
            for k in range(first, end):
                act.wait_ge(S.nibble_ready, k + 1)
                nc.scalar.activation(buf1.quant[:, k, :], nibble[k % 2][:, :], ACT.Identity).then_inc(S.quant_ready, 1)

        def dve_b_chunks(v, first, end):
            for g in range(first, end):
                v.wait_ge(S.b_hi_ready, g + 1)
                cols = slice(g * B_COLS, (g + 1) * B_COLS)
                low(buf0.b_lo[:, :, cols], b_chunk(g), buf0.b_hi[:, :, cols]).then_inc(S.b_lo_ready, 1)

        def sp_a_rows(sp, first, end):
            for g in range(first, end):
                if g >= A_RING - 1:
                    sp.wait_ge(S.weights_turned, 1 + 2 * (g - A_RING + 1))
                for e in range(2):
                    sp.dma_start(a_nat[e * NE:(e + 1) * NE, g % A_RING, :], a_src[2 * g + e]).then_inc(S.a_loaded[g % A_RING], 16)

        def sp_load(sp, c, first):
            src = x_pairs if first else x_scratch
            for a in range(2):
                rows = src[c if first else c - NPAIR, a * C:(a + 1) * C, :]
                done = (S.xin_loaded0, S.xin_loaded1)[a]
                sp.dma_start(x_in[a][0:C, 0:D], rows).then_inc(done, 16)
                sp.dma_start(x_in[a][C:P, 1:D + 1], rows).then_inc(done, 16)

        block = outer.enter_context(nc.Block())

        @block.sync
        def _(sp):
            setup_loads(sp, 0, set0)
            sp_b_chunks(sp, 0, B_RING)
            edge_loads(sp, 0, set0, slice(0, B))
            sp_load(sp, 0, True)
            sp_b_chunks(sp, B_RING, B_CHUNKS - 3)
            sp.dma_start(wr_nat[:, :], t["L0_ffn_Wr"]).then_inc(S.router_loaded, 16)
            sp_b_chunks(sp, B_CHUNKS - 3, B_CHUNKS - 1)
            sp_a_rows(sp, 0, 2)
            sp_b_chunks(sp, B_CHUNKS - 1, B_CHUNKS)
            sp.wait_ge(S.xin_split, 2)
            sp_load(sp, 1, True)
            sp_a_rows(sp, 2, KT)
            sp.wait_ge(S.weights_turned, len(GROUPS))
            setup_loads(sp, 1, set1)
            with sp.Fori(1, NPAIR - 1) as i:
                sp.wait_ge(S.xin_split, 2 * i + 2)
                sp_load(sp, i + 1, True)
            sp.wait_ge(S.xin_split, 2 * NPAIR)
            sp.wait_ge(S.x1_stored, 16)
            sp_load(sp, NPAIR, False)
            sp.wait_ge(S.hidden_done, 2 * NPAIR)
            sp.dma_start(packed[:, :], t["L1_ffn_qweight"]).then_inc(S.quant_loaded, 16)
            sp.wait_ge(S.x1_stored, 16 * (NPAIR - 1))
            edge_loads(sp, 1, set1, slice(0, B - 2))
            sp.wait_ge(S.x1_stored, 16 * NPAIR)
            edge_loads(sp, 1, set1, slice(B - 2, B))
            for dst, src in ((buf1.scales, t["L1_ffn_scales"].rearrange("o u -> u o")), (buf1.zeros, t["L1_ffn_zeros"].rearrange("o u -> u o")),
                             (buf1.bias, t["L1_ffn_bias"].rearrange("(u o) -> u o", u=1))):
                sp.dma_start(dst[:, :], src.broadcast_to([P, D])).then_inc(S.consts_loaded, 16)
            with sp.Fori(NPAIR, 2 * NPAIR - 1) as i:
                sp.wait_ge(S.xin_split, 2 * i + 2)
                sp_load(sp, i + 1, False)
            for n in range(2):
                sp.wait_ge(S.y_ready, NPAIR + n)
                sp.dma_start(out_pairs[NPAIR - 1][:, n * 512:(n + 1) * 512], buf1.res[:, n * 512:(n + 1) * 512]).then_inc(S.last_stored, 16)
            sp.wait_ge(S.last_stored, 32)

        @block.gpsimd
        def _(pool):
            nc.gpsimd.memset(ident[:, :], 0.0).then_inc(S.ident_clear, 1)
            nc.gpsimd.memset(eps_col[:, :], EPS).then_inc(S.ident_ready, 1)
            pool.wait_ge(S.ident_clear, 1)
            nc.gpsimd.affine_select(out=ident[:, :], in_=ident[:, :], compare_op=ALU.not_equal, fill=1.0, base=0,
                                    pattern=[[-1, P]], channel_multiplier=1).then_inc(S.ident_ready, 1)
            nc.gpsimd.memset(spread[:, :, :], 0.0).then_inc(S.ident_clear, 1)
            pool.wait_ge(S.ident_clear, 2)
            pool.wait_ge(S.ident_ready, 2)
            for rows in (slice(0, C), slice(C, P)):
                nc.gpsimd.tensor_copy(spread[rows, 1, :], ident[rows, rows]).then_inc(S.spread_ready, 1)
            pool.wait_ge(S.weights_turned, len(GROUPS))
            pool.dma_start(buf0.res[:, :], x_pairs[0]).then_inc(S.res_loaded, 16)
            with pool.Fori(0, NPAIR - 1) as i:
                pool.wait_ge(S.x1_ready, 2 * i + 3)
                pool.dma_start(x_scratch[i], buf0.res[:, :]).then_inc(S.x1_stored, 16)
                pool.wait_ge(S.x1_stored, 16 * i + 16)
                pool.dma_start(buf0.res[:, :], x_pairs[i + 1]).then_inc(S.res_loaded, 16)
            pool.wait_ge(S.hidden_done, 2 * NPAIR)
            setup_clear(nc.gpsimd, set1)
            pool.wait_ge(S.x1_ready, 2 * NPAIR + 1)
            pool.dma_start(x_scratch[NPAIR - 1], buf0.res[:, :]).then_inc(S.x1_stored, 16)
            pool.wait_ge(S.x1_stored, 16 * NPAIR)
            pool.wait_ge(S.consts_loaded, 16 * 3)
            pool.dma_start(buf1.res[:, :], x_scratch[0]).then_inc(S.res_loaded, 16)

            def add_bias(f):
                pool.wait_ge(S.res_loaded, 16 * (f + 1))
                nc.gpsimd.tensor_tensor(buf1.res[:, :], buf1.res[:, :], buf1.bias[:, :], ALU.add).then_inc(S.biased, 1)

            with pool.Fori(0, NPAIR - 1) as i:
                add_bias(i + NPAIR)
                pool.wait_ge(S.y_ready, i + 1)
                pool.dma_start(out_pairs[i], buf1.res[:, :]).then_inc(S.y_stored, 16)
                pool.wait_ge(S.y_stored, 16 * i + 16)
                pool.dma_start(buf1.res[:, :], x_scratch[i + 1]).then_inc(S.res_loaded, 16)
            add_bias(2 * NPAIR - 1)
            pool.wait_ge(S.y_stored, 16 * (NPAIR - 1))

        @block.tensor
        def _(pe):
            def first_pair(L, s, bufs):
                c = L * NPAIR
                squares_tensor(pe, L, s)
                pe.wait_ge(S.tiles_ready, L + 1)
                if L:
                    pe.wait_ge(S.x1_ready, 2 * NPAIR + 1)
                if L == 0:
                    edge_tensor(pe, L, s, 0)
                inner_tensor(pe, L, s, 0)
                pe_fold3(pe, c, bufs, c == 0)
                pe_layer1(pe, c, 0, bufs, c == 0)
                if L:
                    edge_tensor(pe, L, s, 0)
                edge_tensor(pe, L, s, 1)
                inner_tensor(pe, L, s, 1)
                pe_layer1(pe, c, 1, bufs, c == 0)
                edge_tensor(pe, L, s, 2)
                pe_fold2(pe, c, bufs, c == 0)
                edge_tensor(pe, L, s, 3)

            setup_tensor(pe, 0, set0)
            first_pair(0, set0, buf0)
            pe.wait_ge(S.edges_done, 1)
            pe.wait_ge(S.fold2_hi, 2)
            pe.wait_ge(S.fold2_ready, 1)
            pe_turn_weights(pe, 0, TURNS[0])
            for a in range(2):
                pe_cond(pe, 0, a, buf0)
                pe_turn_weights(pe, TURNS[a], TURNS[a + 1])
            pe.wait_ge(S.weights_lo, len(GROUPS))
            pe.wait_ge(S.b_lo_ready, B_CHUNKS)
            pe.wait_ge(S.spread_ready, 2)
            with pe.Fori(0, NPAIR - 1) as i:
                c = i + 1
                pe_layer1(pe, c, 0, buf0)
                pe_turn(pe, i, buf0, False)
                pe_layer1(pe, c, 1, buf0)
                pe_fold3(pe, c, buf0)
                pe_scores(pe, i, buf0)
                pe_hidden(pe, i, 0, buf0)
                pe_score_sum(pe, i, buf0)
                pe_fold2(pe, c, buf0)
                pe_hidden(pe, i, 1, buf0)
                pe_cond(pe, c, 0, buf0)
                pe_gated_turn(pe, i, buf0)
                pe_cond(pe, c, 1, buf0)
                for n in range(2):
                    pe_adapter_out(pe, i, buf0, n)
            f = NPAIR - 1
            pe_turn(pe, f, buf0, False)
            pe_scores(pe, f, buf0)
            pe_hidden(pe, f, 0, buf0)
            pe_score_sum(pe, f, buf0)
            pe_hidden(pe, f, 1, buf0)
            pe_gated_turn(pe, f, buf0)
            pe_adapter_out(pe, f, buf0, 0)
            setup_tensor(pe, 1, set1)
            pe_adapter_out(pe, f, buf0, 1)
            first_pair(1, set1, buf1)
            for a in range(2):
                pe_cond(pe, NPAIR, a, buf1)
            pe.wait_ge(S.quant_ready, KT)
            with pe.Fori(NPAIR, 2 * NPAIR - 1) as i:
                c = i + 1
                pe_layer1(pe, c, 0, buf1)
                pe.wait_ge(S.rowsum_read, i - NPAIR + 1)
                pe_turn(pe, i, buf1, True)
                pe_layer1(pe, c, 1, buf1)
                pe_fold3(pe, c, buf1)
                pe_quant(pe, i, 0, buf1)
                pe_fold2(pe, c, buf1)
                pe_quant(pe, i, 1, buf1)
                pe_rowsum(pe, i, buf1)
                pe_cond(pe, c, 0, buf1)
                pe_cond(pe, c, 1, buf1)
            f = 2 * NPAIR - 1
            pe.wait_ge(S.rowsum_read, NPAIR)
            pe_turn(pe, f, buf1, True)
            pe_quant(pe, f, 0, buf1)
            pe_rowsum(pe, f, buf1)
            pe_quant(pe, f, 1, buf1)

        @block.scalar
        def _(act):
            def first_pair(L, s, bufs):
                c = L * NPAIR
                def weights(chunks, nibbles):
                    if L == 0:
                        act_b_chunks(act, *chunks)
                    else:
                        act_nibbles(act, *nibbles)

                setup_scalar(act, L, s)
                weights((3, 6), (0, 0))
                act.wait_ge(S.tables_ready, L + 1)
                act.wait_ge(S.tiles_ready, L + 1)
                act_fold_start(act, c, bufs, c == 0)
                act_fold3(act, c, bufs, c == 0)
                weights((6, 9), (0, 2))
                act_layer1(act, c, 0, bufs)
                weights((9, 12), (2, 4))
                act_layer1(act, c, 1, bufs)
                weights((12, 13), (4, 6))
                act_fold2(act, c, bufs, c == 0)
                weights((13, B_CHUNKS), (6, 8))
                act.wait_ge(S.bias4_ready, L + 1)
                act.wait_ge(S.edges_done, L + 1)

            def high_parts(first, end):
                for n in range(first, end):
                    act.wait_ge(S.weights_turned, n + 1)
                    nc.scalar.activation(group_out(n, True), group_in(n), ACT.Identity).then_inc(S.weights_hi, 1)

            act_b_chunks(act, 0, 3)
            first_pair(0, set0, buf0)
            act.wait_ge(S.b_lo_ready, B_CHUNKS)
            high_parts(0, TURNS[0])
            for a in range(2):
                act_cond(act, 0, a, buf0)
                high_parts(TURNS[a], TURNS[a + 1])
            nc.scalar.preload_act_table(ACT.Exp)
            with act.Fori(0, NPAIR - 1) as i:
                c = i + 1
                act_fold_start(act, c, buf0)
                act_turn(act, i, buf0)
                act_layer1(act, c, 0, buf0)
                act_fold3(act, c, buf0)
                act_layer1(act, c, 1, buf0)
                act_scores(act, i, buf0)
                act_exp(act, i, buf0)
                act_fold2(act, c, buf0)
                act_gated_turn(act, i, buf0)
                act_cond(act, c, 0, buf0)
                act_cond(act, c, 1, buf0)
            f = NPAIR - 1
            act_turn(act, f, buf0)
            act_scores(act, f, buf0)
            act_exp(act, f, buf0)
            act_gated_turn(act, f, buf0)

            first_pair(1, set1, buf1)
            for a in range(2):
                act_cond(act, NPAIR, a, buf1)
            nc.scalar.preload_act_table(ACT.Identity)
            with act.Fori(NPAIR, 2 * NPAIR - 1) as i:
                c = i + 1
                act_fold_start(act, c, buf1)
                act_turn(act, i, buf1)
                act_layer1(act, c, 0, buf1)
                act_fold3(act, c, buf1)
                act_layer1(act, c, 1, buf1)
                act_fold2(act, c, buf1)
                act_cond(act, c, 0, buf1)
                act_cond(act, c, 1, buf1)
            act_turn(act, 2 * NPAIR - 1, buf1)

        @block.vector
        def _(v):
            v.sem_inc(S.x1_ready, 1)
            v.sem_inc(S.rowsum_read, 1)
            v.sem_inc(S.scored, 1)
            for a in range(2):
                nc.vector.memset(x_in[a][0:C, D:D + 1], 0.0)
                nc.vector.memset(x_in[a][C:P, 0:1], 0.0)

            def split(c, bufs, first=False):
                for a in range(2):
                    dve_split(v, c, a, bufs, first)

            def first_pair(L, s, bufs):
                c = L * NPAIR
                def weights(chunks, nibbles):
                    if L == 0:
                        dve_b_chunks(v, *chunks)
                    else:
                        dve_nibbles(v, *nibbles)

                if L == 0:
                    edge_vector(v, L, s, 0)
                tables_vector(v, L, s)
                dve_fold_start(v, c, bufs)
                split(c, bufs, c == 0)
                if L:
                    inner_vector(v, L, s, 0)
                    dve_fold3(v, c, bufs)
                    edge_vector(v, L, s, 0)
                weights((3, 6), (0, 2))
                edge_vector(v, L, s, 1)
                if L == 0:
                    inner_vector(v, L, s, 0)
                    dve_fold3(v, c, bufs)
                weights((6, 9), (2, 4))
                edge_vector(v, L, s, 2)
                inner_vector(v, L, s, 1)
                dve_layer1(v, c, 0, bufs)
                weights((9, 12), (4, 6))
                edge_vector(v, L, s, 3)
                dve_layer1(v, c, 1, bufs)
                dve_fold2(v, c, bufs)
                weights((12, 14), (6, 8))
                edge_vector(v, L, s, 4)
                weights((14, B_CHUNKS), (KT, KT))

            dve_pads(v, buf0)
            setup_clear(nc.vector, set0)
            images_vector(v, 0, set0)
            dve_b_chunks(v, 0, 3)
            setup_vector(v, 0, set0)
            first_pair(0, set0, buf0)
            v.wait_ge(S.b_lo_ready, B_CHUNKS)
            for n in range(len(GROUPS)):
                v.wait_ge(S.weights_hi, n + 1)
                low(group_out(n, False), group_in(n), group_out(n, True)).then_inc(S.weights_lo, 1)
                if n == TURNS[1] - 1:
                    split(1, buf0)

            def first_step(i, last):
                c = i + 1
                dve_fold_start(v, c, buf0)
                dve_turn(v, i, buf0)
                dve_layer1(v, c, 0, buf0)
                dve_fold3(v, c, buf0)
                dve_layer1(v, c, 1, buf0)
                dve_route(v, i, buf0)
                dve_gate(v, i, 0, buf0)
                dve_fold2(v, c, buf0)
                dve_gate(v, i, 1, buf0)
                dve_gated_turn(v, i, buf0)
                if not last:
                    split(c + 1, buf0)
                dve_first_residual(v, i, buf0)

            with v.Fori(0, NPAIR - 2) as i:
                first_step(i, False)
            first_step(NPAIR - 2, True)
            f = NPAIR - 1
            dve_turn(v, f, buf0)
            dve_route(v, f, buf0)
            dve_gate(v, f, 0, buf0)
            dve_gate(v, f, 1, buf0)
            dve_gated_turn(v, f, buf0)
            images_vector(v, 1, set1)
            setup_vector(v, 1, set1)
            dve_first_residual(v, f, buf0)
            dve_pads(v, buf1)
            v.wait_ge(S.quant_loaded, 16)
            first_pair(1, set1, buf1)
            v.wait_ge(S.consts_loaded, 16 * 3)

            def second_step(i, last):
                c = i + 1
                dve_fold_start(v, c, buf1)
                dve_turn(v, i, buf1)
                dve_layer1(v, c, 0, buf1)
                dve_fold3(v, c, buf1)
                dve_layer1(v, c, 1, buf1)
                dve_reduce(v, i, buf1)
                dve_fold2(v, c, buf1)
                if not last:
                    split(c + 1, buf1)
                dve_rowsum(v, i, buf1)
                dve_second_residual(v, i, buf1)

            split(NPAIR + 1, buf1)
            with v.Fori(NPAIR, 2 * NPAIR - 2) as i:
                second_step(i, False)
            second_step(2 * NPAIR - 2, True)
            f = 2 * NPAIR - 1
            dve_turn(v, f, buf1)
            dve_reduce(v, f, buf1)
            dve_rowsum(v, f, buf1)
            dve_second_residual(v, f, buf1, last=True)


def kernel(**inputs):
    import concourse.bacc as bacc
    from concourse.bass_utils import run_bass_kernel_spmd

    nc = bacc.Bacc("TRN2", target_bir_lowering=False, num_devices=1)
    arrays, tensors = {}, {}
    for name, value in inputs.items():
        a = np.ascontiguousarray(value)
        arrays[f"in_{name}"] = a
        tensors[name] = nc.dram_tensor(f"in_{name}", a.shape, mybir.dt.from_np(a.dtype), kind="ExternalInput").ap()
    tensors["out"] = nc.dram_tensor("out_x", (B, C, D), F32, kind="ExternalOutput").ap()
    program(nc, tensors)
    result = run_bass_kernel_spmd(nc, [arrays], core_ids=[0])
    return result.results[0]["out_x"]
```
